# Optimizing a Trainium2 kernel written in Bass

```python
import numpy as np
import jax
import jax.numpy as jnp

def _softmax(x, axis=-1):
    return jax.nn.softmax(x, axis=axis)

def _gelu(x):
    return jax.nn.gelu(x, approximate=True)

def _silu(x):
    return jax.nn.silu(x)

def _sigmoid(x):
    return jax.nn.sigmoid(x)

def _layernorm(x, axis=-1, eps=1e-05):
    m = jnp.mean(x, axis=axis, keepdims=True)
    v = jnp.var(x, axis=axis, keepdims=True)
    return (x - m) / jnp.sqrt(v + eps)

def _scatter_add(tgt, idx, src, axis=0):
    return tgt.at[idx].add(src)

def _segment_sum(src, seg, n):
    return jax.ops.segment_sum(src, seg, n)
kernel_name = 'mk_gnn_preln_d2_gnn_r8_4a5d30'

def setup_inputs(seed: int=0):
    np.random.seed(seed)
    _w = jnp.asarray

    def _rec_inputs():
        import jax
        import jax.numpy as jnp
        _gk = jax.random.key(seed)
        x = -0.000202 + 1 * jax.random.normal(jax.random.fold_in(_gk, 1), (6250, 256), jnp.float32)
        _s = jax.random.randint(jax.random.fold_in(_gk, 2), (50000,), 0, 6250, jnp.int32)
        _d = jax.random.randint(jax.random.fold_in(_gk, 3), (50000,), 0, 6250, jnp.int32)
        _loop = jnp.arange(6250, dtype=jnp.int32)
        src = jnp.concatenate([_s, _d, _loop])
        dst = jnp.concatenate([_d, _s, _loop])
        _o = jnp.argsort(dst, stable=True)
        src = src[_o]
        dst = dst[_o]
        edge_attr_4 = 0.00121237 + 1.00026 * jax.random.normal(jax.random.fold_in(_gk, 12), (106250, 4), jnp.float32)
        edge_attr_8 = jax.random.uniform(jax.random.fold_in(_gk, 13), (106250, 8), jnp.float32, 0.0, 1)
        node_vec1 = jax.random.uniform(jax.random.fold_in(_gk, 14), (6250, 1), jnp.float32, 0.0, 1)
        return (x, src, dst, edge_attr_4, edge_attr_8, node_vec1)
    x, src, dst, edge_attr_4, edge_attr_8, node_vec1 = _rec_inputs()

    def _L0_gnn_setup():
        import jax, jax.numpy as jnp
        import numpy as np
        N = 3125
        E = 50000
        MUL = 64
        NB = 8
        RN = 64
        NUM_NEIGH = 16.0
        INV_SQRT3 = 1.0 / np.sqrt(3.0)

        def _forward(node_input, node_attr, edge_attr, edge_length_embedded, W_sc0, W_sc1, W_lin1_0, W_lin1_1, fc_w0, fc_w1, W_lin2_0, W_lin2_1, edge_src, edge_dst):
            Nn = node_input.shape[0]
            z = node_attr
            x0 = node_input[:, :MUL]
            x1 = node_input[:, MUL:].reshape(Nn, MUL, 3)
            inv_m = 1.0 / np.sqrt(MUL)
            s0 = x0 @ W_sc0 * z * inv_m
            s1 = jnp.einsum('nuc,uv->nvc', x1, W_sc1) * z[:, :, None] * inv_m
            h0 = x0 @ W_lin1_0 * z * inv_m
            h1 = jnp.einsum('nuc,uv->nvc', x1, W_lin1_1) * z[:, :, None] * inv_m
            hid = jax.nn.silu(edge_length_embedded @ fc_w0 / np.sqrt(NB))
            w = hid @ fc_w1 / np.sqrt(RN)
            wA, wB, wC, wD = (w[:, :MUL], w[:, MUL:2 * MUL], w[:, 2 * MUL:3 * MUL], w[:, 3 * MUL:])
            xs0 = h0[edge_src]
            xs1 = h1[edge_src]
            sh0 = edge_attr[:, :1]
            sh1 = edge_attr[:, 1:4]
            midA = wA * xs0 * sh0
            midD = wD * jnp.einsum('euc,ec->eu', xs1, sh1) * INV_SQRT3
            midB = (wB * xs0)[:, :, None] * sh1[:, None, :]
            midC = wC[:, :, None] * xs1 * sh0[:, None, :]
            mid0 = jnp.concatenate([midA, midD], axis=1)
            mid1 = jnp.concatenate([midB, midC], axis=1)
            inv_nb = 1.0 / np.sqrt(NUM_NEIGH)
            y0 = jax.ops.segment_sum(mid0, edge_dst, num_segments=Nn) * inv_nb
            y1 = jax.ops.segment_sum(mid1.reshape(mid1.shape[0], -1), edge_dst, num_segments=Nn).reshape(Nn, 2 * MUL, 3) * inv_nb
            inv_2m = 1.0 / np.sqrt(2 * MUL)
            o0 = y0 @ W_lin2_0 * z * inv_2m
            o1 = jnp.einsum('nuc,uv->nvc', y1, W_lin2_1) * z[:, :, None] * inv_2m
            c_s = np.float32(np.sin(np.pi / 8.0))
            c_x = np.float32(np.cos(np.pi / 8.0))
            out0 = c_s * s0 + c_x * o0
            out1 = c_s * s1 + c_x * o1
            return jnp.concatenate([out0, out1.reshape(Nn, 3 * MUL)], axis=1)
        key = jax.random.key(seed)
        ks = jax.random.split(key, 14)
        f32 = jnp.float32
        return {'node_input': jax.random.normal(ks[0], (N, 4 * MUL), f32), 'node_attr': jnp.ones((N, 1), f32), 'edge_src': jax.random.randint(ks[1], (E,), 0, N, dtype=jnp.int32), 'edge_dst': jax.random.randint(ks[2], (E,), 0, N, dtype=jnp.int32), 'edge_attr': jax.random.normal(ks[3], (E, 4), f32), 'edge_length_embedded': jax.random.uniform(ks[4], (E, NB), f32), 'W_sc0': jax.random.normal(ks[5], (MUL, MUL), f32), 'W_sc1': jax.random.normal(ks[6], (MUL, MUL), f32), 'W_lin1_0': jax.random.normal(ks[7], (MUL, MUL), f32), 'W_lin1_1': jax.random.normal(ks[8], (MUL, MUL), f32), 'fc_w0': jax.random.normal(ks[9], (NB, RN), f32), 'fc_w1': jax.random.normal(ks[10], (RN, 4 * MUL), f32), 'W_lin2_0': jax.random.normal(ks[11], (2 * MUL, MUL), f32), 'W_lin2_1': jax.random.normal(ks[12], (2 * MUL, MUL), f32)}
    _L0_gnn_all = _L0_gnn_setup()
    _L0_gnn_in = {k: v for k, v in _L0_gnn_all.items() if k in ('W_sc0', 'W_sc1', 'W_lin1_0', 'W_lin1_1', 'fc_w0', 'fc_w1', 'W_lin2_0', 'W_lin2_1')}
    del _L0_gnn_all

    def _L1_gnn_setup():
        import jax, jax.numpy as jnp
        import numpy as np
        N_NODES = 1250
        N_EDGES = 40000
        FEA = 256
        HID = 256
        HEADS = 4
        ODIM = HID // HEADS
        NEG_SLOPE = 0.2

        def _gat_layer(x, W, al, ar, b, src, dst):
            n = x.shape[0]
            z = (x @ W).reshape(n, HEADS, ODIM)
            el = jnp.sum(z * al, axis=-1)
            er = jnp.sum(z * ar, axis=-1)
            e = jax.nn.leaky_relu(el[src] + er[dst], negative_slope=NEG_SLOPE)
            e_max = jax.ops.segment_max(e, dst, num_segments=n)
            ex = jnp.exp(e - e_max[dst])
            denom = jax.ops.segment_sum(ex, dst, num_segments=n)
            alpha = ex / denom[dst]
            msg = z[src] * alpha[:, :, None]
            out = jax.ops.segment_sum(msg, dst, num_segments=n)
            out = out + x.reshape(n, HEADS, ODIM)
            out = out + b.reshape(HEADS, ODIM)
            out = jax.nn.elu(out)
            return out.reshape(n, HID)
        key = jax.random.key(seed)
        ks = jax.random.split(key, 12)
        inp = {'features': jax.random.normal(ks[0], (N_NODES, FEA), dtype=jnp.float32), 'src': jax.random.randint(ks[1], (N_EDGES,), 0, N_NODES, dtype=jnp.int32), 'dst': jax.random.randint(ks[2], (N_EDGES,), 0, N_NODES, dtype=jnp.int32), 'W0': jax.random.normal(ks[3], (FEA, HID), dtype=jnp.float32) * (1.0 / np.sqrt(FEA)), 'al0': jax.random.normal(ks[4], (HEADS, ODIM), dtype=jnp.float32) * 0.1, 'ar0': jax.random.normal(ks[5], (HEADS, ODIM), dtype=jnp.float32) * 0.1, 'b0': jnp.zeros((HID,), dtype=jnp.float32), 'W1': jax.random.normal(ks[6], (HID, HID), dtype=jnp.float32) * (1.0 / np.sqrt(HID)), 'al1': jax.random.normal(ks[7], (HEADS, ODIM), dtype=jnp.float32) * 0.1, 'ar1': jax.random.normal(ks[8], (HEADS, ODIM), dtype=jnp.float32) * 0.1, 'b1': jnp.zeros((HID,), dtype=jnp.float32)}
        return inp
    _L1_gnn_all = _L1_gnn_setup()
    _L1_gnn_in = {k: v for k, v in _L1_gnn_all.items() if k in ('W0', 'al0', 'ar0', 'b0', 'W1', 'al1', 'ar1', 'b1')}
    del _L1_gnn_all
    return {'x': x, 'src': src, 'dst': dst, 'edge_attr_4': edge_attr_4, 'edge_attr_8': edge_attr_8, 'node_vec1': node_vec1, 'L0_gnn_W_sc0': _L0_gnn_in['W_sc0'], 'L0_gnn_W_sc1': _L0_gnn_in['W_sc1'], 'L0_gnn_W_lin1_0': _L0_gnn_in['W_lin1_0'], 'L0_gnn_W_lin1_1': _L0_gnn_in['W_lin1_1'], 'L0_gnn_fc_w0': _L0_gnn_in['fc_w0'], 'L0_gnn_fc_w1': _L0_gnn_in['fc_w1'], 'L0_gnn_W_lin2_0': _L0_gnn_in['W_lin2_0'], 'L0_gnn_W_lin2_1': _L0_gnn_in['W_lin2_1'], 'L1_gnn_W0': _L1_gnn_in['W0'], 'L1_gnn_al0': _L1_gnn_in['al0'], 'L1_gnn_ar0': _L1_gnn_in['ar0'], 'L1_gnn_b0': _L1_gnn_in['b0'], 'L1_gnn_W1': _L1_gnn_in['W1'], 'L1_gnn_al1': _L1_gnn_in['al1'], 'L1_gnn_ar1': _L1_gnn_in['ar1'], 'L1_gnn_b1': _L1_gnn_in['b1']}

def reference(x, src, dst, edge_attr_4, edge_attr_8, node_vec1, L0_gnn_W_sc0, L0_gnn_W_sc1, L0_gnn_W_lin1_0, L0_gnn_W_lin1_1, L0_gnn_fc_w0, L0_gnn_fc_w1, L0_gnn_W_lin2_0, L0_gnn_W_lin2_1, L1_gnn_W0, L1_gnn_al0, L1_gnn_ar0, L1_gnn_b0, L1_gnn_W1, L1_gnn_al1, L1_gnn_ar1, L1_gnn_b1):
    import jax
    import jax.numpy as jnp

    def _L0_gnn_ref(node_input, node_attr, edge_src, edge_dst, edge_attr, edge_length_embedded, W_sc0, W_sc1, W_lin1_0, W_lin1_1, fc_w0, fc_w1, W_lin2_0, W_lin2_1):
        import jax, jax.numpy as jnp
        import numpy as np
        N = 3125
        E = 50000
        MUL = 64
        NB = 8
        RN = 64
        NUM_NEIGH = 16.0
        INV_SQRT3 = 1.0 / np.sqrt(3.0)

        def _forward(node_input, node_attr, edge_attr, edge_length_embedded, W_sc0, W_sc1, W_lin1_0, W_lin1_1, fc_w0, fc_w1, W_lin2_0, W_lin2_1, edge_src, edge_dst):
            Nn = node_input.shape[0]
            z = node_attr
            x0 = node_input[:, :MUL]
            x1 = node_input[:, MUL:].reshape(Nn, MUL, 3)
            inv_m = 1.0 / np.sqrt(MUL)
            s0 = x0 @ W_sc0 * z * inv_m
            s1 = jnp.einsum('nuc,uv->nvc', x1, W_sc1) * z[:, :, None] * inv_m
            h0 = x0 @ W_lin1_0 * z * inv_m
            h1 = jnp.einsum('nuc,uv->nvc', x1, W_lin1_1) * z[:, :, None] * inv_m
            hid = jax.nn.silu(edge_length_embedded @ fc_w0 / np.sqrt(NB))
            w = hid @ fc_w1 / np.sqrt(RN)
            wA, wB, wC, wD = (w[:, :MUL], w[:, MUL:2 * MUL], w[:, 2 * MUL:3 * MUL], w[:, 3 * MUL:])
            xs0 = h0[edge_src]
            xs1 = h1[edge_src]
            sh0 = edge_attr[:, :1]
            sh1 = edge_attr[:, 1:4]
            midA = wA * xs0 * sh0
            midD = wD * jnp.einsum('euc,ec->eu', xs1, sh1) * INV_SQRT3
            midB = (wB * xs0)[:, :, None] * sh1[:, None, :]
            midC = wC[:, :, None] * xs1 * sh0[:, None, :]
            mid0 = jnp.concatenate([midA, midD], axis=1)
            mid1 = jnp.concatenate([midB, midC], axis=1)
            inv_nb = 1.0 / np.sqrt(NUM_NEIGH)
            y0 = jax.ops.segment_sum(mid0, edge_dst, num_segments=Nn) * inv_nb
            y1 = jax.ops.segment_sum(mid1.reshape(mid1.shape[0], -1), edge_dst, num_segments=Nn).reshape(Nn, 2 * MUL, 3) * inv_nb
            inv_2m = 1.0 / np.sqrt(2 * MUL)
            o0 = y0 @ W_lin2_0 * z * inv_2m
            o1 = jnp.einsum('nuc,uv->nvc', y1, W_lin2_1) * z[:, :, None] * inv_2m
            c_s = np.float32(np.sin(np.pi / 8.0))
            c_x = np.float32(np.cos(np.pi / 8.0))
            out0 = c_s * s0 + c_x * o0
            out1 = c_s * s1 + c_x * o1
            return jnp.concatenate([out0, out1.reshape(Nn, 3 * MUL)], axis=1)
        return _forward(node_input, node_attr, edge_attr, edge_length_embedded, W_sc0, W_sc1, W_lin1_0, W_lin1_1, fc_w0, fc_w1, W_lin2_0, W_lin2_1, edge_src, edge_dst)

    def _L1_gnn_ref(features, src, dst, W0, al0, ar0, b0, W1, al1, ar1, b1):
        import jax, jax.numpy as jnp
        import numpy as np
        N_NODES = 1250
        N_EDGES = 40000
        FEA = 256
        HID = 256
        HEADS = 4
        ODIM = HID // HEADS
        NEG_SLOPE = 0.2

        def _gat_layer(x, W, al, ar, b, src, dst):
            n = x.shape[0]
            z = (x @ W).reshape(n, HEADS, ODIM)
            el = jnp.sum(z * al, axis=-1)
            er = jnp.sum(z * ar, axis=-1)
            e = jax.nn.leaky_relu(el[src] + er[dst], negative_slope=NEG_SLOPE)
            e_max = jax.ops.segment_max(e, dst, num_segments=n)
            ex = jnp.exp(e - e_max[dst])
            denom = jax.ops.segment_sum(ex, dst, num_segments=n)
            alpha = ex / denom[dst]
            msg = z[src] * alpha[:, :, None]
            out = jax.ops.segment_sum(msg, dst, num_segments=n)
            out = out + x.reshape(n, HEADS, ODIM)
            out = out + b.reshape(HEADS, ODIM)
            out = jax.nn.elu(out)
            return out.reshape(n, HID)
        x = _gat_layer(features, W0, al0, ar0, b0, src, dst)
        x = _gat_layer(x, W1, al1, ar1, b1, src, dst)
        return x
    h = jnp.maximum(_layernorm(x, axis=-1), 0.0)
    x = x + _L0_gnn_ref(h, node_vec1, src, dst, edge_attr_4, edge_attr_8, L0_gnn_W_sc0, L0_gnn_W_sc1, L0_gnn_W_lin1_0, L0_gnn_W_lin1_1, L0_gnn_fc_w0, L0_gnn_fc_w1, L0_gnn_W_lin2_0, L0_gnn_W_lin2_1)
    h = jnp.maximum(_layernorm(x, axis=-1), 0.0)
    x = x + _L1_gnn_ref(h, src, dst, L1_gnn_W0, L1_gnn_al0, L1_gnn_ar0, L1_gnn_b0, L1_gnn_W1, L1_gnn_al1, L1_gnn_ar1, L1_gnn_b1)
    return x

_drawn_inputs = setup_inputs


def setup_inputs(seed=0):
    import zlib

    import numpy as np

    out = dict(_drawn_inputs(seed))
    spreads = {'L1_gnn_b0': (0.0, 0.1), 'L1_gnn_b1': (0.0, 0.1)}
    factors = {}
    for name, (base, spread) in spreads.items():
        noise = np.random.default_rng([zlib.crc32(name.encode()), seed]).standard_normal(out[name].shape)
        drawn = base * np.exp(spread * noise) if base else spread * noise
        out[name] = jnp.asarray(drawn.astype(out[name].dtype))
    for name, factor in factors.items():
        out[name] = (out[name] * factor).astype(out[name].dtype)
    return out
```

```python
from contextlib import ExitStack

import concourse.bass as bass
from concourse import mybir

F32 = mybir.dt.float32
I32 = mybir.dt.int32
ACT = mybir.ActivationFunctionType
ALU = mybir.AluOpType
AX = mybir.AxisListType

P = 128
N = 6250
E = 106250
D = 256
MUL = 64
HEADS = 4
HF = D // HEADS
NBAS = 8
RN = 64
G = 8
GE = G * P
NG = -(-E // GE)
NTILES = NG * G
EP = NG * GE
NW = 128
PB = 2 * P
NPB = 2 * -(-(N + NW) // (2 * PB))
NC = NPB * PB
NT = NC // P
SPARE = NC - NW
HALF_V = -(-(NG + -(-NC // NW) + 4) // 2)
VT = 2 * HALF_V
SCRATCH = 10240 + 256
ZW = D + 2 * HEADS
LOW = -1.0e38
EPS = 1e-5
INV_M = MUL ** -0.5
C_S = 0.3826834261417389
C_X = 0.9238795042037964
OUT_SCALE = C_X * (2 * MUL) ** -0.5 / 4.0 * RN ** -0.5
INV_SQRT3 = 3.0 ** -0.5
NEG_SLOPE = 0.2


class Mem:
    pass


def allocate(nc, ctx, io):
    m = Mem()
    m.io = io
    m.sems = ctx

    def sb(name, shape, dt=F32):
        return ctx.enter_context(nc.sbuf_tensor(name, shape, dt))

    def dram(name, shape, dt=F32):
        return nc.dram_tensor(name, shape, dt, kind="Internal").ap()

    m.h_rows = dram("h_rows", (NC, D))
    m.x_skip = dram("x_skip", (NC, D))
    m.x1_rows = dram("x1_rows", (NC, D))
    m.hT = [dram(f"hT{l}", (NPB, P, 2 * PB)) for l in range(2)]
    m.z_rows = [dram(f"z_rows{l}", (NC, ZW)) for l in range(2)]
    m.same_seg = dram("same_seg", ((NG + 1) * GE,))
    m.steps_i = dram("steps_i", (2, VT), I32)
    m.steps_f = dram("steps_f", (1, VT))

    m.nodes = sb("nodes", [P, 5 * NC])
    m.scratch = sb("scratch", [P, SCRATCH])
    m.src = sb("src_sb", [P, NTILES], I32)
    m.dst = sb("dst_sb", [P, NTILES], I32)
    m.sh = sb("sh_sb", [P, NTILES * 4])
    m.base_col = sb("base_col", [P, VT])
    m.tab = sb("tab", [1, 2 * VT + 1], I32)
    m.nsteps = sb("nsteps", [1, 2], I32)
    m.nvec = sb("nvec", [P, 3 * NT])
    m.ident = sb("ident", [P, P])
    m.cols = sb("cols", [P, NW])
    m.fc0 = sb("fc0_sb", [2 * NBAS, P])
    m.fc1 = sb("fc1_sb", [P, 4 * MUL])
    m.lin1 = sb("lin1_sb", [P, 2, 4 * MUL])
    m.lin2 = sb("lin2_sb", [P, 5, P])
    m.wz = [sb(f"wz{l}", [P, 2, ZW]) for l in range(2)]
    m.bias = [sb(f"bias{l}", [P, 2]) for l in range(2)]
    m.headsel = sb("headsel", [HEADS, 2, P])
    m.eps = sb("eps", [P, 1])
    m.carry = sb("carry", [HEADS, 2])
    return m


def table_group(m, v):
    return m.tab[0:1, bass.ds(v, 1)]


def table_base(m, v):
    return m.tab[0:1, bass.ds(v + (VT + 1), 1)]


def load_group(eng, m, v):
    return eng.value_load(table_group(m, v), min_val=0, max_val=NG - 1)


def load_base(eng, m, v):
    return eng.value_load(table_base(m, v), min_val=0, max_val=SPARE)


def load_steps(eng, m):
    pairs = eng.value_load(m.nsteps[0:1, 0:1], min_val=NG // 2, max_val=VT // 2 - 1)
    return pairs, pairs * 2


def setup_stage(nc, m):
    io = m.io
    with ExitStack() as ctx:
        def sb(name, shape, dt=F32):
            return ctx.enter_context(nc.sbuf_tensor(name, shape, dt))

        def sem(name):
            return m.sems.enter_context(nc.semaphore(name))

        free = [0]

        def part(parts, width, dt=F32):
            a = m.scratch[0:parts, free[0]:free[0] + width]
            free[0] += width
            return a if dt == F32 else a.bitcast(dt)

        ends = part(1, 2 * NG, I32)
        span = part(1, NG, I32)
        span7 = part(1, NG, I32)
        wins = part(1, NG)
        ones_row = part(1, NG)
        incl = part(1, NG)
        rows2 = part(1, 2 * NG)
        odd = part(1, 1, I32)
        total = part(1, 1, I32)
        ones_lhs = part(1, HALF_V)
        vcol = part(HALF_V, 2)
        gcols = part(HALF_V, NG)
        hit = part(HALF_V, 2 * NG)
        step = part(HALF_V, 2 * 6)
        step_i = part(HALF_V, 2 * 2, I32)
        dst_a = part(NG + 1, GE, I32)
        dst_b = part(NG + 1, GE, I32)
        differ = part(NG + 1, GE)
        att = part(P, 4 * D)
        att_w = part(P, 2 * D)
        ps_rows = ctx.enter_context(nc.psum_tensor("ps_rows", [HALF_V, 2 * NG], F32))

        s_ends = sem("su_ends")
        s_edges = sem("su_edges")
        s_dstrows = sem("su_dstrows")
        s_w = sem("su_weights")
        s_zero = sem("su_zeroed")
        s_pool = sem("su_pool")
        s_dve = sem("su_dve")
        s_bc = sem("su_rows_broadcast")
        s_tab = sem("su_table_stored")
        s_tabback = sem("su_table_loaded")
        s_flags = sem("su_flags_stored")

        loads = [0]
        block = ctx.enter_context(nc.Block())

        @block.sync
        def _(sp):
            sp.dma_start(ends, io["dst_ends"]).then_inc(s_ends, 16)
            sp.dma_start(dst_a, io["dst_line"][0:(NG + 1) * GE].rearrange("(p j) -> p j", j=GE)).then_inc(s_dstrows, 16)
            sp.dma_start(dst_b, io["dst_line"][1:(NG + 1) * GE + 1].rearrange("(p j) -> p j", j=GE)).then_inc(s_dstrows, 16)
            sp.dma_start(m.src[:, :], io["src_t"]).then_inc(s_edges, 16)
            sp.dma_start(m.dst[:, :], io["dst_t"]).then_inc(s_edges, 16)
            sp.dma_start(m.sh[:, :], io["sh_t"]).then_inc(s_edges, 16)
            sp.wait_ge(s_zero, 1)
            todo = [(m.nvec[:, 0:NT], io["nvec_t"]),
                    (m.fc0[0:NBAS, 0:RN], io["fc_w0"]), (m.fc0[NBAS:2 * NBAS, RN:2 * RN], io["fc_w0"]),
                    (m.fc1[0:RN, :], io["fc_w1"]), (m.fc1[RN:2 * RN, :], io["fc_w1"])]
            for c in range(2):
                for half in range(2):
                    rows = slice(half * MUL, half * MUL + MUL)
                    at = half * MUL
                    scalar_part = c == 0 and half == 0
                    todo.append((m.lin1[rows, c, at:at + MUL], io["W_lin1_0" if scalar_part else "W_lin1_1"]))
                    todo.append((m.lin1[rows, c, 2 * MUL + at:2 * MUL + at + MUL],
                                 io["W_sc0" if scalar_part else "W_sc1"]))
            lo, hi = slice(0, MUL), slice(MUL, 2 * MUL)
            todo += [(m.lin2[lo, 0, lo], io["W_lin2_0"][lo, :]), (m.lin2[hi, 0, hi], io["W_lin2_1"][hi, :]),
                     (m.lin2[lo, 1, lo], io["W_lin2_1"][hi, :]), (m.lin2[hi, 1, hi], io["W_lin2_1"][hi, :])]
            for c in range(3):
                d_rows, b_rows = (lo, hi) if c == 0 else (hi, lo)
                todo += [(m.lin2[b_rows, 2 + c, hi], io["W_lin2_1"][lo, :]),
                         (m.lin2[d_rows, 2 + c, lo], io["W_lin2_0"][hi, :])]
            for l in range(2):
                todo.append((m.wz[l][:, :, 0:D], io[f"W{l}"].rearrange("(c p) n -> p c n", p=P)))
                todo.append((m.bias[l][:, :], io[f"b{l}_t"]))
                todo.append((att[:, (2 * l) * D:(2 * l + 1) * D], io[f"al{l}"].partition_broadcast(P)))
                todo.append((att[:, (2 * l + 1) * D:(2 * l + 2) * D], io[f"ar{l}"].partition_broadcast(P)))
            for dst, src in todo:
                sp.dma_start(dst, src).then_inc(s_w, 16)
            loads[0] = len(todo)
            sp.wait_ge(s_dve, FLAGS_DONE)
            sp.dma_start(m.same_seg.rearrange("(p j) -> p j", j=GE), differ).then_inc(s_flags, 16)
            sp.wait_ge(s_dve, TABLE_DONE)
            for q in range(2):
                at = slice(q * HALF_V, (q + 1) * HALF_V)
                for k in range(2):
                    sp.dma_start(m.steps_i[k:k + 1, at].rearrange("o v -> v o"),
                                 step_i[:, 2 * q + k:2 * q + k + 1]).then_inc(s_tab, 16)
                sp.dma_start(m.steps_f[0:1, at].rearrange("o v -> v o"),
                             step[:, 6 * q + 5:6 * q + 6]).then_inc(s_tab, 16)
            sp.wait_ge(s_tab, 6 * 16)
            sp.dma_start(m.tab[:, 0:VT], m.steps_i[0:1, :]).then_inc(s_tabback, 16)
            sp.dma_start(m.tab[:, VT + 1:2 * VT + 1], m.steps_i[1:2, :]).then_inc(s_tabback, 16)
            sp.dma_start(m.base_col[:, :], m.steps_f[0, :].partition_broadcast(P)).then_inc(s_tabback, 16)
            sp.wait_ge(s_tabback, 48)
            sp.wait_ge(s_flags, 16)
            sp.wait_ge(s_edges, 48)

        @block.gpsimd
        def _(pool):
            nc.gpsimd.memset(m.ident[:], 0.0)
            nc.gpsimd.memset(m.headsel[:], 0.0).then_inc(s_pool, 1)
            pool.wait_ge(s_pool, 1)
            nc.gpsimd.affine_select(out=m.ident[:], in_=m.ident[:], compare_op=ALU.not_equal, fill=1.0, base=0,
                                    pattern=[[-1, P]], channel_multiplier=1)
            sel = m.headsel[:, :, :].rearrange("h c (a f) -> h (c a) f", a=2)
            nc.gpsimd.affine_select(out=sel, in_=sel, compare_op=ALU.not_equal, fill=1.0, base=0,
                                    pattern=[[-1, HEADS], [0, HF]], channel_multiplier=1)
            nc.gpsimd.iota(m.cols[:], [[1, NW]], base=0, channel_multiplier=0, allow_small_or_imprecise_dtypes=True)
            nc.gpsimd.iota(gcols, [[1, NG]], base=0, channel_multiplier=0, allow_small_or_imprecise_dtypes=True)
            nc.gpsimd.iota(vcol, [[HALF_V, 2]], base=0, channel_multiplier=1,
                           allow_small_or_imprecise_dtypes=True).then_inc(s_pool, 1)

        @block.tensor
        def _(pe):
            pe.wait_ge(s_dve, ROWS_DONE)
            nc.tensor.matmul(ps_rows[:, :], ones_lhs, rows2, start=True, stop=True).then_inc(s_bc, 1)

        marks = {}

        @block.vector
        def _(dve):
            count = [0]

            def done(ins):
                count[0] += 1
                ins.then_inc(s_dve, 1)
                dve.wait_ge(s_dve, count[0])

            V = nc.vector
            V.memset(m.fc0[:], 0.0)
            V.memset(m.lin1[:], 0.0)
            V.memset(m.lin2[:], 0.0).then_inc(s_zero, 1)
            V.memset(m.eps[:], EPS)
            V.memset(m.carry[:], LOW)
            V.memset(m.tab[:, VT:VT + 1], SPARE)
            V.memset(ones_lhs, 1.0)
            done(V.memset(ones_row, 1.0))
            dve.wait_ge(s_ends, 16)
            done(V.tensor_tensor(span, ends[:, NG:2 * NG], ends[:, 0:NG], ALU.subtract))
            done(V.tensor_scalar(span7, span, NW.bit_length() - 1, None, ALU.arith_shift_right))
            done(V.tensor_scalar(wins, span7, 1.0, None, ALU.add))
            done(V.tensor_tensor_scan(incl, ones_row, wins, 0.0, ALU.mult, ALU.add))
            done(V.tensor_tensor(rows2[:, 0:NG], incl, wins, ALU.subtract))
            done(V.scalar_tensor_tensor(rows2[:, NG:2 * NG], rows2[:, 0:NG], -float(NW), ends[:, 0:NG],
                                        ALU.mult, ALU.add))
            marks["rows"] = count[0]
            done(V.tensor_copy(total, incl[:, NG - 1:NG]))
            done(V.tensor_scalar(odd, total, 1, None, ALU.bitwise_and))
            done(V.tensor_tensor(total, total, odd, ALU.add))
            V.tensor_scalar(m.nsteps[:, 0:1], total, 1, None, ALU.arith_shift_right)
            dve.wait_ge(s_pool, 2)
            dve.wait_ge(s_bc, 1)
            for q in range(2):
                h = hit[:, q * NG:(q + 1) * NG]
                c = step[:, 6 * q:6 * q + 6]
                done(V.tensor_scalar(h, ps_rows[:, 0:NG], vcol[:, q:q + 1], None, ALU.is_le))
                done(V.tensor_reduce(c[:, 0:1], h, AX.X, ALU.add))
                done(V.tensor_scalar(c[:, 1:2], c[:, 0:1], -1.0, None, ALU.add))
                done(V.scalar_tensor_tensor(h, gcols, c[:, 1:2], ps_rows[:, NG:2 * NG], ALU.is_equal, ALU.mult))
                done(V.tensor_reduce(c[:, 2:3], h, AX.X, ALU.add))
                done(V.scalar_tensor_tensor(c[:, 3:4], vcol[:, q:q + 1], float(NW), c[:, 2:3], ALU.mult, ALU.add))
                done(V.tensor_scalar(c[:, 5:6], c[:, 3:4], float(SPARE), None, ALU.min))
                V.tensor_copy(step_i[:, 2 * q:2 * q + 1], c[:, 1:2])
                done(V.tensor_copy(step_i[:, 2 * q + 1:2 * q + 2], c[:, 5:6]))
            marks["table"] = count[0]
            dve.wait_ge(s_dstrows, 32)
            done(V.tensor_tensor(differ, dst_a, dst_b, ALU.not_equal))
            done(V.tensor_scalar(differ, differ, LOW, None, ALU.mult))
            marks["flags"] = count[0]
            assert (marks["rows"], marks["table"], marks["flags"]) == (ROWS_DONE, TABLE_DONE, FLAGS_DONE), marks
            dve.wait_ge(s_w, 16 * SETUP_LOADS)
            V.tensor_scalar(m.nvec[:, NT:2 * NT], m.nvec[:, 0:NT], INV_M, None, ALU.mult)
            V.tensor_scalar(m.nvec[:, 2 * NT:3 * NT], m.nvec[:, 0:NT], C_S * INV_M, None, ALU.mult)
            done(V.tensor_scalar(m.lin2[:], m.lin2[:], OUT_SCALE, None, ALU.mult))
            V.tensor_scalar(m.lin2[0:MUL, 2, 0:MUL], m.lin2[0:MUL, 2, 0:MUL], INV_SQRT3, None, ALU.mult)
            V.tensor_scalar(m.lin2[MUL:2 * MUL, 3:5, 0:MUL], m.lin2[MUL:2 * MUL, 3:5, 0:MUL], INV_SQRT3, None, ALU.mult)
            for l in range(2):
                for k in range(2):
                    a = att[:, (2 * l + k) * D:(2 * l + k + 1) * D].rearrange("p (o d) -> p o d", o=1)
                    w = att_w.rearrange("p (c d) -> p c d", c=2)
                    done(V.tensor_tensor(w, m.wz[l][:, :, 0:D], a.broadcast_to([P, 2, D]), ALU.mult))
                    done(V.tensor_reduce(m.wz[l][:, :, D + k * HEADS:D + (k + 1) * HEADS],
                                         att_w.rearrange("p (c h f) -> p c h f", c=2, h=HEADS), AX.X, ALU.add))

        assert loads[0] == SETUP_LOADS, loads


ROWS_DONE = 7
TABLE_DONE = ROWS_DONE + 3 + 2 * 8
FLAGS_DONE = TABLE_DONE + 2
SETUP_LOADS = 5 + 8 + 4 + 6 + 8


def node_buffers(nc, m, ctx, tag):
    b = Mem()
    free = [0]

    def part(width):
        a = [m.scratch[:, free[0] + u * width:free[0] + (u + 1) * width] for u in range(2)]
        free[0] += 2 * width
        return a

    b.x = part(2 * D)
    b.h = part(2 * D)
    b.hT = part(2 * PB)
    b.rows = part(2 * ZW)
    b.skip = part(2 * D)
    b.y = part(5 * PB) if tag == "l0out" else None
    b.stat = part(12)
    b.mv = part(4)
    b.sd = part(2)
    b.rs = part(2)
    b.nm = part(2)
    assert free[0] <= SCRATCH
    return b


def input_stage(nc, m):
    with ExitStack() as ctx:
        def sem(name):
            return m.sems.enter_context(nc.semaphore(name))

        def ps(name, cols):
            return ctx.enter_context(nc.psum_tensor(name, [P, cols], F32))

        b = node_buffers(nc, m, ctx, "in")
        pT = [ps(f"in_pT{u}", 512) for u in range(2)]
        pO = [[ps(f"in_pO{u}{t}", 512) for t in range(2)] for u in range(2)]

        x_in = [sem(f"in_x{u}") for u in range(2)]
        s_go, s_bn, s_mv, s_sd, s_rs, s_nm, s_h, s_pT, s_hT, s_pO, s_rows, s_skip = [
            sem("in_" + n) for n in ("go", "bn", "mv", "sd", "rs", "nm", "h", "pT", "hT", "pO", "rows", "skip")]
        st_rows = [sem(f"in_strows{u}") for u in range(2)]
        st_skip = [sem(f"in_stskip{u}") for u in range(2)]
        block = ctx.enter_context(nc.Block())

        def rows_of(t, i):
            return t[bass.ds(i * PB, PB), :].rearrange("(t p) d -> p t d", p=P)

        def tile(a, w=D):
            return a[:, 0:2 * w].rearrange("p (t d) -> p t d", t=2)

        @block.sync
        def _(sp):
            def step(i, u, last):
                sp.wait_ge(s_rows, i + (u + 1))
                sp.dma_start(rows_of(m.h_rows, i + u), tile(b.rows[u])).then_inc(st_rows[u], 16)
                sp.wait_ge(s_skip, i + (u + 1))
                sp.dma_start(rows_of(m.x_skip, i + u), tile(b.skip[u])).then_inc(st_skip[u], 16)
                sp.wait_ge(st_rows[u], i * 8 + 16)
                sp.wait_ge(st_skip[u], i * 8 + 16)
                if not last:
                    sp.dma_start(tile(b.x[u]), rows_of(m.io["x"], i + (u + 2))).then_inc(x_in[u], 16)

            for u in range(2):
                sp.dma_start(tile(b.x[u]), rows_of(m.io["x"], u)).then_inc(x_in[u], 16)
            with sp.Fori(0, NPB // 2 - 1) as half:
                i = half * 2
                for u in range(2):
                    step(i, u, False)
            for u in range(2):
                step(NPB - 2, u, True)

        @block.gpsimd
        def _(pool):
            nc.gpsimd.memset(m.nodes[:], 0.0)

        @block.vector
        def _(dve):
            V = nc.vector
            with dve.Fori(0, NPB // 2) as half:
                i = half * 2
                for u in range(2):
                    n = i + (u + 1)
                    x = tile(b.x[u])
                    dve.wait_ge(x_in[u], i * 8 + 16)
                    for t in range(2):
                        ins = V.bn_stats(b.stat[u][:, 6 * t:6 * t + 6], x[:, t, :])
                    ins.then_inc(s_bn, 1)
                    dve.wait_ge(s_bn, n).then_inc(s_go, 1)
                    for t in range(2):
                        ins = V.bn_aggr(b.mv[u][:, 2 * t:2 * t + 2], b.stat[u][:, 6 * t:6 * t + 6])
                    ins.then_inc(s_mv, 1)
                    dve.wait_ge(s_sd, n)
                    V.reciprocal(b.rs[u], b.sd[u]).then_inc(s_rs, 1)
                    dve.wait_ge(s_rs, n)
                    mean = b.mv[u].rearrange("p (t k) -> p t k", k=2)[:, :, 0]
                    V.scalar_tensor_tensor(b.nm[u], mean, -1.0, b.rs[u], ALU.mult, ALU.mult).then_inc(s_nm, 1)
                    dve.wait_ge(s_pT, n)
                    V.tensor_copy(b.hT[u], pT[u][:]).then_inc(s_hT, 1)
                    dve.wait_ge(s_pO, n)
                    for t in range(2):
                        zc = m.nvec[:, bass.ds(i * 2 + (2 * NT + 2 * u + t), 1)]
                        sk = tile(b.skip[u])
                        V.scalar_tensor_tensor(sk[:, t, 0:MUL], pO[u][t][:, D:D + MUL], zc, x[:, t, 0:MUL],
                                               ALU.mult, ALU.add)
                        ins = V.scalar_tensor_tensor(
                            sk[:, t, MUL:D].rearrange("p (v c) -> p v c", c=3),
                            pO[u][t][:, D + MUL:2 * D].rearrange("p (c v) -> p v c", c=3), zc,
                            x[:, t, MUL:D].rearrange("p (v c) -> p v c", c=3), ALU.mult, ALU.add)
                    ins.then_inc(s_skip, 1)

        @block.scalar
        def _(act):
            with act.Fori(0, NPB // 2) as half:
                i = half * 2
                for u in range(2):
                    n = i + (u + 1)
                    var = b.mv[u].rearrange("p (t k) -> p t k", k=2)[:, :, 1]
                    act.wait_ge(s_mv, n)
                    nc.scalar.activation(b.sd[u], var, ACT.Sqrt, bias=m.eps[:, 0:1]).then_inc(s_sd, 1)
                    act.wait_ge(s_nm, n)
                    x = tile(b.x[u])
                    h = tile(b.h[u])
                    for t in range(2):
                        nc.scalar.activation(h[:, t, 0:MUL], x[:, t, 0:MUL], ACT.Relu,
                                             bias=b.nm[u][:, t:t + 1], scale=b.rs[u][:, t:t + 1])
                        ins = nc.scalar.activation(h[:, t, MUL:D].rearrange("p (c v) -> p v c", c=3),
                                                   x[:, t, MUL:D].rearrange("p (v c) -> p v c", c=3), ACT.Relu,
                                                   bias=b.nm[u][:, t:t + 1], scale=b.rs[u][:, t:t + 1])
                    ins.then_inc(s_h, 1)
                    act.wait_ge(s_skip, n)
                    for t in range(2):
                        zs = m.nvec[:, bass.ds(i * 2 + (NT + 2 * u + t), 1)]
                        ins = nc.scalar.activation(tile(b.rows[u])[:, t, :], pO[u][t][:, 0:D], ACT.Copy, scale=zs)
                    ins.then_inc(s_rows, 1)

        @block.tensor
        def _(pe):
            with pe.Fori(0, NPB // 2) as half:
                i = half * 2
                for u in range(2):
                    n = i + (u + 1)
                    h = tile(b.h[u])
                    pe.wait_ge(s_h, n)
                    for c in range(2):
                        for t in range(2):
                            ins = nc.tensor.transpose(pT[u][:, c * PB + t * P:c * PB + (t + 1) * P],
                                                      h[:, t, c * P:(c + 1) * P], m.ident[:])
                    ins.then_inc(s_pT, 1)
                    pe.wait_ge(s_hT, n)
                    for t in range(2):
                        for c in range(2):
                            out = pO[u][t][:, :].rearrange("p (k f) -> p k f", k=2)[:, :, c * P:(c + 1) * P]
                            ins = nc.tensor.matmul(out, b.hT[u][:, c * PB + t * P:c * PB + (t + 1) * P],
                                                   m.lin1[:, c, :], start=(c == 0), stop=True, skip_group_check=True)
                    ins.then_inc(s_pO, 1)



def conv_edge_stage(nc, m):
    V = nc.vector
    with ExitStack() as ctx:
        def sem(name):
            return m.sems.enter_context(nc.semaphore("ce_" + name))

        free = [0]

        def part(width, parts=P):
            a = [m.scratch[0:parts, free[0] + u * width:free[0] + (u + 1) * width] for u in range(2)]
            free[0] += 2 * width
            return a

        xg = part(G * D)
        prod = part(2 * 9 * MUL)
        sel = part(2 * 4 * NW)
        hidT = part(GE // 2)
        ea8 = part(GE // 2, 2 * NBAS)
        idx = ctx.enter_context(nc.sbuf_tensor("ce_idx", [P, 2, G], I32))
        rel = ctx.enter_context(nc.sbuf_tensor("ce_rel", [P, 2, G], F32))
        ps_w = [ctx.enter_context(nc.psum_tensor(f"ce_w{k}", [P, 2, 4, MUL], F32)) for k in range(2)]
        ps_hid = ctx.enter_context(nc.psum_tensor("ce_hid", [P, GE // 2], F32))
        ps_sum = [ctx.enter_context(nc.psum_tensor(f"ce_sum{u}", [P, 4, NW], F32)) for u in range(2)]
        ps_sum4 = [ctx.enter_context(nc.psum_tensor(f"ce_sumd{u}", [P, NW], F32)) for u in range(2)]

        ea8_in = [sem(f"ea8_in{u}") for u in range(2)]
        got = [sem(f"gathered{u}") for u in range(2)]
        sp_done, idx_ready, pool_go, hid_ps, hid_ready, w_ready, rel_ready = [
            sem(n) for n in ("sp_done", "idx_ready", "pool_go", "hid_ps", "hid_ready", "w_ready", "rel_ready")]
        msg_ready = sem("msg_ready")
        pair_summed = sem("pair_summed")
        b_again = sem("b_again")
        added = sem("added")
        block = ctx.enter_context(nc.Block())

        @block.sync
        def _(sp):
            def load(v, u):
                g = load_group(sp, m, v)
                sp.dma_start(ea8[u], m.io["ea8_t"][bass.ds(g * 2 * NBAS, 2 * NBAS), :]).then_inc(ea8_in[u], 16)

            pairs, steps = load_steps(sp, m)
            for u in range(2):
                load(u, u)
            with sp.Fori(0, pairs) as half:
                i = half * 2
                for u in range(2):
                    sp.wait_ge(hid_ps, i + (u + 1))
                    load(i + (u + 2), u)
            for u in range(2):
                sp.wait_ge(ea8_in[u], pairs * 16 + 16).then_inc(sp_done, 1)

        @block.scalar
        def _(act):
            pairs, steps = load_steps(act, m)

            def stage_idx(v, u):
                g = load_group(act, m, v)
                nc.scalar.copy(idx[:, u, :], m.src[:, bass.ds(g * G, G)]).then_inc(idx_ready, 1)

            def silu(v, u):
                act.wait_ge(hid_ps, v + 1)
                nc.scalar.activation(hidT[u], ps_hid[:, :], ACT.Silu, scale=NBAS ** -0.5).then_inc(hid_ready, 1)

            def copy_b(v, j):
                act.wait_ge(msg_ready, v * 4 + (j + 1))
                blocks = prod[j % 2].rearrange("p (t b f) -> p t b f", t=2, b=9)
                nc.scalar.copy(blocks[:, :, 7, :], blocks[:, :, 5, :]).then_inc(b_again, 1)

            stage_idx(0, 0)
            stage_idx(1, 1)
            silu(0, 0)
            with act.Fori(0, pairs) as half:
                i = half * 2
                for u in range(2):
                    copy_b(i + u, 0)
                    copy_b(i + u, 1)
                    silu(i + (u + 1), 1 - u)
                    copy_b(i + u, 2)
                    copy_b(i + u, 3)
                    stage_idx(i + (u + 2), u)

        @block.gpsimd
        def _(pool):
            pairs, steps = load_steps(pool, m)
            with pool.Fori(0, pairs) as half:
                i = half * 2
                for u in range(2):
                    pool.wait_ge(idx_ready, i + (u + 1)).then_inc(pool_go, 1)
                    for k in range(G):
                        nc.gpsimd.indirect_dma_start(
                            xg[u][:, k * D:(k + 1) * D], None, m.h_rows,
                            bass.IndirectOffsetOnAxis(ap=idx[:, u, k:k + 1], axis=0)).then_inc(got[u], 16)

        @block.tensor
        def _(pe):
            pairs, steps = load_steps(pe, m)

            def hidden(v, u):
                pe.wait_ge(ea8_in[u], (v - u) * 8 + 16)
                nc.tensor.matmul(ps_hid[:, :], m.fc0[:, :], ea8[u], start=True, stop=True).then_inc(hid_ps, 1)

            def weights(v, u, j):
                if j == 0:
                    pe.wait_ge(hid_ready, v + 1)
                for t in range(2):
                    half, col = divmod((2 * j + t) * P, GE // 2)
                    rows = slice(half * RN, half * RN + RN)
                    ins = nc.tensor.matmul(ps_w[j % 2][:, t, :, :].rearrange("p k f -> p (k f)"),
                                           hidT[u][rows, col:col + P], m.fc1[rows, :], start=True, stop=True)
                ins.then_inc(w_ready, 1)

            def sums(v, u, j):
                pe.wait_ge(msg_ready, v * 4 + (j + 1))
                if j == 0:
                    pe.wait_ge(added, v + 1)
                blocks = prod[j % 2].rearrange("p (t b f) -> p t b f", t=2, b=9)
                s = sel[j % 2].rearrange("p (t s n) -> p t s n", t=2, s=4)
                for t in range(2):
                    first = j == 0 and t == 0
                    last = j == 3 and t == 1
                    for c in range(2):
                        nc.tensor.matmul(ps_sum[u][:, c, :], blocks[:, t, 2 * c:2 * c + 2, :].rearrange("p b f -> p (b f)"),
                                         s[:, t, 0, :], start=first and c == 0, stop=last, skip_group_check=True)
                    for c in range(3):
                        out = ps_sum[u][:, 2 + c, :] if c < 2 else ps_sum4[u][:, :]
                        at = (4, 5, 7)[c]
                        if c == 2 and t == 0:
                            pe.wait_ge(b_again, v * 4 + (j + 1))
                        ins = nc.tensor.matmul(out, blocks[:, t, at:at + 2, :].rearrange("p b f -> p (b f)"), s[:, t, 1 + c, :],
                                               start=first and c == 2, stop=last, skip_group_check=True)
                ins.then_inc(pair_summed, 1)

            pe.sem_inc(pair_summed, 2)
            hidden(0, 0)
            weights(0, 0, 0)
            with pe.Fori(0, pairs) as half:
                i = half * 2
                for u in range(2):
                    for j in range(4):
                        if j < 3:
                            weights(i + u, u, j + 1)
                        else:
                            weights(i + (u + 1), 1 - u, 0)
                        sums(i + u, u, j)
                        if j == 1:
                            pe.wait_ge(hid_ready, i + (u + 1))
                            hidden(i + (u + 1), 1 - u)

        @block.vector
        def _(dve):
            pairs, steps = load_steps(dve, m)

            def pair(v, u, j, g):
                tiles = xg[u].rearrange("p (k b f) -> p k b f", k=G, b=4)
                blocks = prod[j % 2].rearrange("p (t b f) -> p t b f", t=2, b=9)
                s = sel[j % 2].rearrange("p (t s n) -> p t s n", t=2, s=4)
                dve.wait_ge(pair_summed, v * 4 + (j + 1))
                for t in range(2):
                    k = 2 * j + t
                    for c in range(4):
                        V.tensor_scalar(s[:, t, c, :], m.cols[:, :], rel[:, u, k:k + 1],
                                        m.sh[:, bass.ds(g * (4 * G) + (4 * k + c), 1)], ALU.is_equal, ALU.mult)
                dve.wait_ge(w_ready, v * 4 + (j + 1))
                if j == 0:
                    dve.wait_ge(got[u], (v - u) * 64 + 16 * G)
                for t in range(2):
                    k = 2 * j + t
                    w = ps_w[j % 2][:, t, :, :]
                    V.tensor_tensor(blocks[:, t, 0:6:5, :], w[:, 0:2, :],
                                    tiles[:, k, 0:1, :].broadcast_to([P, 2, MUL]), ALU.mult)
                    for a, out in ((2, blocks[:, t, 1:4, :]), (3, blocks[:, t, 4:9:2, :])):
                        ins = V.tensor_tensor(out, w[:, a:a + 1, :].broadcast_to([P, 3, MUL]), tiles[:, k, 1:4, :], ALU.mult)
                ins.then_inc(msg_ready, 1)

            def add_window(v, u):
                base = load_base(dve, m, v)
                dve.wait_ge(pair_summed, v * 4 + (2 + 4))
                dve.wait_ge(added, v + 2)
                cols = m.nodes[:, :].rearrange("p (c n) -> p c n", c=5)[:, :, bass.ds(base, NW)]
                V.tensor_tensor(cols[:, 0:4, :], cols[:, 0:4, :], ps_sum[u][:, :, :], ALU.add)
                V.tensor_tensor(cols[:, 4, :], cols[:, 4, :], ps_sum4[u][:, :], ALU.add).then_inc(added, 1)

            V.memset(ps_sum[1][:], 0.0)
            V.memset(ps_sum4[1][:], 0.0).then_inc(added, 1)
            with dve.Fori(0, pairs) as half:
                i = half * 2
                for u in range(2):
                    v = i + u
                    g = load_group(dve, m, v)
                    V.tensor_scalar(rel[:, u, :], m.dst[:, bass.ds(g * G, G)], m.base_col[:, bass.ds(v, 1)], None,
                                    ALU.subtract).then_inc(rel_ready, 1)
                    dve.wait_ge(rel_ready, v + 1)
                    for j in range(4):
                        pair(v, u, j, g)
                        if j == 1:
                            add_window(v - 1, 1 - u)
            add_window(steps - 1, 1)


def conv_node_stage(nc, m):
    V = nc.vector
    with ExitStack() as ctx:
        def sem(name):
            return m.sems.enter_context(nc.semaphore("cn_" + name))

        def ps(name, cols):
            return ctx.enter_context(nc.psum_tensor("cn_" + name, [P, cols], F32))

        b = node_buffers(nc, m, ctx, "l0out")
        pX = ps("pX", 512)
        pT = ps("pT", 512)
        pZ = [ps(f"pZ{t}", ZW) for t in range(2)]
        x_in = [sem(f"x_in{u}") for u in range(2)]
        y_in, pool_go, s_pX, s_x1, s_go, s_bn, s_mv, s_sd, s_rs, s_nm, s_h, s_pT, s_hT, s_pZ, s_rows = [
            sem(n) for n in ("y", "pool_go", "pX", "x1", "go", "bn", "mv", "sd", "rs", "nm", "h", "pT", "hT", "pZ", "rows")]
        st = [sem(f"stored{u}") for u in range(2)]
        block = ctx.enter_context(nc.Block())

        def rows_of(t, i):
            return t[bass.ds(i * PB, PB), :].rearrange("(t p) d -> p t d", p=P)

        def tile(a, w=D):
            return a[:, 0:2 * w].rearrange("p (t d) -> p t d", t=2)

        @block.sync
        def _(sp):
            def step(i, u, last):
                sp.wait_ge(s_x1, i + (u + 1))
                sp.dma_start(rows_of(m.x1_rows, i + u), tile(b.skip[u])).then_inc(st[u], 16)
                sp.wait_ge(s_hT, i + (u + 1))
                sp.dma_start(m.hT[0][bass.ds(i + u, 1), :, :].rearrange("o p n -> (o p) n"), b.hT[u]).then_inc(st[u], 16)
                sp.wait_ge(s_rows, i + (u + 1))
                sp.dma_start(rows_of(m.z_rows[0], i + u), tile(b.rows[u], ZW)).then_inc(st[u], 16)
                sp.wait_ge(st[u], i * 24 + 48)
                if not last:
                    sp.dma_start(tile(b.x[u]), rows_of(m.x_skip, i + (u + 2))).then_inc(x_in[u], 16)

            for u in range(2):
                sp.dma_start(tile(b.x[u]), rows_of(m.x_skip, u)).then_inc(x_in[u], 16)
            with sp.Fori(0, NPB // 2 - 1) as half:
                i = half * 2
                for u in range(2):
                    step(i, u, False)
            for u in range(2):
                step(NPB - 2, u, True)

        @block.gpsimd
        def _(pool):
            cols = m.nodes[:, :].rearrange("p (c n) -> p c n", c=5)
            with pool.Fori(0, NPB // 2) as half:
                i = half * 2
                for u in range(2):
                    pool.wait_ge(x_in[u], i * 8 + 16).then_inc(pool_go, 1)
                    nc.gpsimd.tensor_copy(b.y[u].rearrange("p (c n) -> p c n", c=5),
                                          cols[:, :, bass.ds((i + u) * PB, PB)]).then_inc(y_in, 1)

        @block.tensor
        def _(pe):
            with pe.Fori(0, NPB // 2) as half:
                i = half * 2
                for u in range(2):
                    n = i + (u + 1)
                    y = b.y[u].rearrange("p (c n) -> p c n", c=5)
                    pe.wait_ge(y_in, n)
                    for t in range(2):
                        out = pX[:, t * D:(t + 1) * D].rearrange("p (b f) -> p b f", b=4)
                        for c in range(5):
                            blocks = [out[:, 0:2, :], out[:, 2:4, :], out[:, 0:2, :], out[:, 0:3:2, :],
                                      out[:, 0:4:3, :]][c]
                            ins = nc.tensor.matmul(blocks, y[:, c, t * P:(t + 1) * P], m.lin2[:, c, :],
                                                   start=(t == 0 and c == 0), stop=(c == 4), skip_group_check=True)
                    ins.then_inc(s_pX, 1)
                    node_pe_tail(nc, pe, m, b, u, n, pT, pZ, s_h, s_pT, s_hT, s_pZ, 0)

        @block.vector
        def _(dve):
            with dve.Fori(0, NPB // 2) as half:
                i = half * 2
                for u in range(2):
                    n = i + (u + 1)
                    x = tile(b.x[u])
                    x1 = tile(b.skip[u])
                    dve.wait_ge(x_in[u], i * 8 + 16)
                    dve.wait_ge(s_pX, n)
                    for t in range(2):
                        zc = m.nvec[:, bass.ds(i * 2 + (2 * u + t), 1)]
                        V.scalar_tensor_tensor(x1[:, t, 0:MUL], pX[:, t * D:t * D + MUL], zc, x[:, t, 0:MUL],
                                               ALU.mult, ALU.add)
                        ins = V.scalar_tensor_tensor(
                            x1[:, t, MUL:D].rearrange("p (v c) -> p v c", c=3),
                            pX[:, t * D + MUL:(t + 1) * D].rearrange("p (c v) -> p v c", c=3), zc,
                            x[:, t, MUL:D].rearrange("p (v c) -> p v c", c=3), ALU.mult, ALU.add)
                    ins.then_inc(s_x1, 1)
                    dve.wait_ge(s_x1, n)
                    for t in range(2):
                        ins = V.bn_stats(b.stat[u][:, 6 * t:6 * t + 6], x1[:, t, :])
                    ins.then_inc(s_bn, 1)
                    dve.wait_ge(s_bn, n).then_inc(s_go, 1)
                    for t in range(2):
                        ins = V.bn_aggr(b.mv[u][:, 2 * t:2 * t + 2], b.stat[u][:, 6 * t:6 * t + 6])
                    ins.then_inc(s_mv, 1)
                    dve.wait_ge(s_sd, n)
                    V.reciprocal(b.rs[u], b.sd[u]).then_inc(s_rs, 1)
                    dve.wait_ge(s_rs, n)
                    mean = b.mv[u].rearrange("p (t k) -> p t k", k=2)[:, :, 0]
                    V.scalar_tensor_tensor(b.nm[u], mean, -1.0, b.rs[u], ALU.mult, ALU.mult).then_inc(s_nm, 1)
                    dve.wait_ge(s_pT, n)
                    V.tensor_copy(b.hT[u], pT[:]).then_inc(s_hT, 1)

        @block.scalar
        def _(act):
            with act.Fori(0, NPB // 2) as half:
                i = half * 2
                for u in range(2):
                    n = i + (u + 1)
                    var = b.mv[u].rearrange("p (t k) -> p t k", k=2)[:, :, 1]
                    act.wait_ge(s_mv, n)
                    nc.scalar.activation(b.sd[u], var, ACT.Sqrt, bias=m.eps[:, 0:1]).then_inc(s_sd, 1)
                    act.wait_ge(s_nm, n)
                    for t in range(2):
                        ins = nc.scalar.activation(tile(b.h[u])[:, t, :], tile(b.skip[u])[:, t, :], ACT.Relu,
                                                   bias=b.nm[u][:, t:t + 1], scale=b.rs[u][:, t:t + 1])
                    ins.then_inc(s_h, 1)
                    node_act_tail(nc, act, m, b, u, n, pZ, s_pZ, s_rows)


def node_pe_tail(nc, pe, m, b, u, n, pT, pZ, s_h, s_pT, s_hT, s_pZ, layer):
    if pT is not None:
        h = b.h[u].rearrange("p (t d) -> p t d", t=2)
        pe.wait_ge(s_h, n)
        for c in range(2):
            for t in range(2):
                ins = nc.tensor.transpose(pT[:, c * PB + t * P:c * PB + (t + 1) * P], h[:, t, c * P:(c + 1) * P],
                                          m.ident[:])
        ins.then_inc(s_pT, 1)
    pe.wait_ge(s_hT, n)
    for t in range(2):
        for c in range(2):
            ins = nc.tensor.matmul(pZ[t][:, :], b.hT[u][:, c * PB + t * P:c * PB + (t + 1) * P], m.wz[layer][:, c, :],
                                   start=(c == 0), stop=(c == 1))
    ins.then_inc(s_pZ, 1)


def node_act_tail(nc, act, m, b, u, n, pZ, s_pZ, s_rows):
    act.wait_ge(s_pZ, n)
    for t in range(2):
        ins = nc.scalar.copy(b.rows[u][:, t * ZW:(t + 1) * ZW], pZ[t][:, :])
    ins.then_inc(s_rows, 1)


def gat_edge_stage(nc, m, layer):
    V = nc.vector
    with ExitStack() as ctx:
        def sem(name):
            return m.sems.enter_context(nc.semaphore(f"ge{layer}_" + name))

        def sb(name, shape, dt=F32):
            return ctx.enter_context(nc.sbuf_tensor(f"ge{layer}_" + name, shape, dt))

        def ps(name, shape):
            return ctx.enter_context(nc.psum_tensor(f"ge{layer}_" + name, shape, F32))

        free = [3 * NC]

        def part(width, parts=P):
            a = m.nodes[0:parts, free[0]:free[0] + width]
            free[0] += width
            return a

        zg = [part(G * ZW) for u in range(2)]
        sel = [part(G * NW) for u in range(2)]
        selT = [part(GE) for _ in range(1)][0]
        zs = m.scratch[:, 0:G * D]
        seg = [m.scratch[0:HEADS, G * D + u * (GE + 2):G * D + u * (GE + 2) + GE + 1] for u in range(2)]
        top = m.scratch[0:HEADS, G * D + 2 * (GE + 2):G * D + 2 * (GE + 2) + GE]
        idx = sb("idx", [P, 2, G], I32)
        rel = sb("rel", [P, 2, G])
        erw = [sb(f"erw{u}", [P, HEADS]) for u in range(2)]
        raw = sb("raw", [P, G * HEADS])
        score = [sb(f"score{u}", [P, G * HEADS]) for u in range(2)]
        diff = [sb(f"diff{u}", [P, G * HEADS]) for u in range(2)]
        ex = [sb(f"ex{u}", [P, G * HEADS]) for u in range(2)]
        fd = [sb(f"fd{u}", [HEADS, 1]) for u in range(2)]
        fac = [sb(f"fac{u}", [HEADS, 1]) for u in range(2)]

        ps_eT = ps("eT", [HEADS, GE])
        ps_selT = ps("selT", [P, GE])
        ps_er = ps("er", [P, G * HEADS])
        ps_max = ps("max", [P, G * HEADS])
        ps_sum = [ps(f"sum{u}", [P, 512]) for u in range(2)]

        er_in = [sem(f"er_in{u}") for u in range(2)]
        seg_in = [sem(f"seg_in{u}") for u in range(2)]
        got = [sem(f"gathered{u}") for u in range(2)]
        (sp_done, pe_go, idx_ready, pool_go, rel_ready, sel_ready, selT_ps, selT_ready, er_ready, raw_ready, score_ready, eT_ready,
         fwd_ready, max_ready, carry_ready, maxT_ready, diff_ready, ex_ready, zs_ready, scaled, summed, added) = [
            sem(n) for n in ("sp_done", "pe_go", "idx_ready", "pool_go", "rel_ready", "sel_ready", "selT_ps", "selT_ready", "er_ready",
                             "raw_ready", "score_ready", "eT_ready", "fwd_ready", "max_ready", "carry_ready",
                             "maxT_ready", "diff_ready", "ex_ready", "zs_ready", "scaled", "summed", "added")]
        block = ctx.enter_context(nc.Block())

        def per_head(a):
            return a.rearrange("p (k h) -> p k h", k=G)

        @block.sync
        def _(sp):
            pairs, steps = load_steps(sp, m)

            def load_er(v, u):
                base = load_base(sp, m, v)
                sp.dma_start(erw[u][:, :], m.z_rows[layer][bass.ds(base, NW), D + HEADS:ZW]).then_inc(er_in[u], 16)

            def load_seg(v, u):
                g = load_group(sp, m, v)
                sp.dma_start(seg[u], m.same_seg[bass.ds(g * GE, GE + 1)].partition_broadcast(HEADS)).then_inc(seg_in[u], 16)

            for u in range(2):
                load_er(u, u)
                load_seg(u, u)
            with sp.Fori(0, pairs) as half:
                i = half * 2
                for u in range(2):
                    sp.wait_ge(er_ready, i + (u + 1))
                    load_er(i + (u + 2), u)
                    sp.wait_ge(carry_ready, i + (u + 2))
                    load_seg(i + (u + 2), u)
            for u in range(2):
                sp.wait_ge(er_in[u], pairs * 16 + 16)
                sp.wait_ge(seg_in[u], pairs * 16 + 16).then_inc(sp_done, 1)

        @block.scalar
        def _(act):
            pairs, steps = load_steps(act, m)

            def stage_idx(v, u):
                g = load_group(act, m, v)
                nc.scalar.copy(idx[:, u, :], m.src[:, bass.ds(g * G, G)]).then_inc(idx_ready, 1)

            def copy_selT(v):
                act.wait_ge(selT_ps, v + 1)
                for k in range(2):
                    ins = nc.scalar.copy(selT[:, k * 512:(k + 1) * 512], ps_selT[:, k * 512:(k + 1) * 512])
                ins.then_inc(selT_ready, 1)

            for u in range(2):
                stage_idx(u, u)
            copy_selT(0)
            with act.Fori(0, pairs) as half:
                i = half * 2
                for u in range(2):
                    v = i + u
                    act.wait_ge(diff_ready, v + 1)
                    nc.scalar.activation(fac[u][:, :], fd[u][:, :], ACT.Exp)
                    nc.scalar.activation(ex[u][:, :], diff[u][:, :], ACT.Exp).then_inc(ex_ready, 1)
                    copy_selT(v + 1)
                    act.wait_ge(zs_ready, v * 2 + 2)
                    stage_idx(v + 2, u)

        @block.gpsimd
        def _(pool):
            pairs, steps = load_steps(pool, m)
            with pool.Fori(0, pairs) as half:
                i = half * 2
                for u in range(2):
                    pool.wait_ge(idx_ready, i + (u + 1)).then_inc(pool_go, 1)
                    for k in range(G):
                        nc.gpsimd.indirect_dma_start(
                            zg[u][:, k * ZW:(k + 1) * ZW], None, m.z_rows[layer],
                            bass.IndirectOffsetOnAxis(ap=idx[:, u, k:k + 1], axis=0)).then_inc(got[u], 16)

        @block.tensor
        def _(pe):
            pairs, steps = load_steps(pe, m)

            def transpose_sel(v, u):
                pe.wait_ge(sel_ready, v + 1)
                for k in range(G):
                    ins = nc.tensor.transpose(ps_selT[:, k * P:(k + 1) * P], sel[u][:, k * NW:(k + 1) * NW], m.ident[:])
                ins.then_inc(selT_ps, 1)

            def spread_er(v, u):
                pe.wait_ge(selT_ready, v + 1)
                pe.wait_ge(er_in[u], (v - u) * 8 + 16)
                for k in range(G):
                    ins = nc.tensor.matmul(ps_er[:, k * HEADS:(k + 1) * HEADS], selT[:, k * P:(k + 1) * P], erw[u][:, :],
                                           start=(k == 0), stop=(k == G - 1), skip_group_check=True)
                ins.then_inc(er_ready, 1)

            transpose_sel(0, 0)
            spread_er(0, 0)
            with pe.Fori(0, pairs) as half:
                i = half * 2
                for u in range(2):
                    v = i + u
                    pe.wait_ge(score_ready, v + 1)
                    for k in range(G):
                        ins = nc.tensor.transpose(ps_eT[:, k * P:(k + 1) * P], per_head(score[u][:, :])[:, k, :], m.ident[:])
                    ins.then_inc(eT_ready, 1)
                    pe.wait_ge(max_ready, v + 1).then_inc(pe_go, 1)
                    for k in range(G):
                        ins = nc.tensor.transpose(ps_max[:, k * HEADS:(k + 1) * HEADS], top[:, k * P:(k + 1) * P],
                                                  m.ident[0:HEADS, 0:HEADS])
                    ins.then_inc(maxT_ready, 1)
                    transpose_sel(v + 1, 1 - u)
                    spread_er(v + 1, 1 - u)
                    pe.wait_ge(ex_ready, v + 1)
                    pe.wait_ge(added, v + 1)
                    for c in range(2):
                        nc.tensor.matmul(ps_sum[u][:, 3 * NW + c:3 * NW + c + 1], m.headsel[:, c, :], fac[u][:, :],
                                         start=(c == 0), stop=True, skip_group_check=True)
                    for k in range(G):
                        s = sel[u][:, k * NW:(k + 1) * NW]
                        if k % 4 == 0:
                            pe.wait_ge(zs_ready, v * 2 + (k // 4 + 1))
                        for c in range(2):
                            nc.tensor.matmul(ps_sum[u][:, c * NW:(c + 1) * NW], zs[:, k * D + c * P:k * D + (c + 1) * P], s,
                                             start=False, stop=(k == G - 1), skip_group_check=True)
                        ins = nc.tensor.matmul(ps_sum[u][0:HEADS, 2 * NW:3 * NW], per_head(ex[u][:, :])[:, k, :], s,
                                               start=False, stop=(k == G - 1), skip_group_check=True)
                    ins.then_inc(summed, 1)

        @block.vector
        def _(dve):
            pairs, steps = load_steps(dve, m)
            cols = m.nodes[:, 0:2 * NC].rearrange("p (c n) -> p c n", c=2)
            den = m.nodes[0:HEADS, 2 * NC:3 * NC]

            def one_hots(v, u):
                g = load_group(dve, m, v)
                V.tensor_scalar(rel[:, u, :], m.dst[:, bass.ds(g * G, G)], m.base_col[:, bass.ds(v, 1)], None,
                                ALU.subtract).then_inc(rel_ready, 1)
                dve.wait_ge(rel_ready, v + 1)
                for k in range(G):
                    ins = V.tensor_scalar(sel[u][:, k * NW:(k + 1) * NW], m.cols[:, :], rel[:, u, k:k + 1], None,
                                          ALU.is_equal)
                ins.then_inc(sel_ready, 1)

            def add_window(v, u):
                base = load_base(dve, m, v)
                dve.wait_ge(summed, v + 2)
                dve.wait_ge(added, v + 2)
                first = cols[:, :, bass.ds(base, 1)]
                V.tensor_tensor(first, first, ps_sum[u][:, 3 * NW:3 * NW + 2].rearrange("p (c o) -> p c o", o=1), ALU.mult)
                V.tensor_scalar(den[:, bass.ds(base, 1)], den[:, bass.ds(base, 1)], fac[u][:, :], None,
                                ALU.mult).then_inc(scaled, 1)
                dve.wait_ge(scaled, v + 2)
                window = cols[:, :, bass.ds(base, NW)]
                V.tensor_tensor(window, window, ps_sum[u][:, 0:2 * NW].rearrange("p (c n) -> p c n", c=2), ALU.add)
                dwin = den[:, bass.ds(base, NW)]
                V.tensor_tensor(dwin, dwin, ps_sum[u][0:HEADS, 2 * NW:3 * NW], ALU.add).then_inc(added, 1)

            V.memset(m.nodes[:, 0:3 * NC], 0.0)
            V.memset(m.carry[:], LOW).then_inc(carry_ready, 1)
            V.memset(fac[1][:, :], 1.0)
            V.memset(ps_sum[1][:], 0.0).then_inc(added, 1)
            one_hots(0, 0)
            dve.sem_inc(summed, 1)
            with dve.Fori(0, pairs) as half:
                i = half * 2
                for u in range(2):
                    v = i + u
                    dve.wait_ge(er_ready, v + 1)
                    dve.wait_ge(got[u], i * 64 + 16 * G)
                    rows = zg[u].rearrange("p (k w) -> p k w", k=G)
                    V.tensor_tensor(per_head(raw[:, :]), rows[:, :, D:D + HEADS], per_head(ps_er[:, :]), ALU.add
                                    ).then_inc(raw_ready, 1)
                    dve.wait_ge(raw_ready, v + 1)
                    V.scalar_tensor_tensor(score[u][:, :], raw[:, :], NEG_SLOPE, raw[:, :], ALU.mult, ALU.max
                                           ).then_inc(score_ready, 1)
                    add_window(v - 1, 1 - u)
                    dve.wait_ge(eT_ready, v + 1)
                    dve.wait_ge(seg_in[u], i * 8 + 16)
                    dve.wait_ge(carry_ready, v + 1)
                    V.tensor_tensor_scan(top, seg[u][:, 0:GE], ps_eT[:, :], m.carry[:, u:u + 1], ALU.add, ALU.max
                                         ).then_inc(fwd_ready, 1)
                    dve.wait_ge(fwd_ready, v + 1)
                    V.tensor_tensor_scan(top[:, ::-1], seg[u][:, GE:0:-1], top[:, ::-1], LOW, ALU.add, ALU.max
                                         ).then_inc(max_ready, 1)
                    dve.wait_ge(max_ready, v + 1)
                    V.scalar_tensor_tensor(fd[u][:, :], m.carry[:, u:u + 1], seg[u][:, 0:1], top[:, 0:1],
                                           ALU.add, ALU.subtract)
                    V.tensor_copy(m.carry[:, 1 - u:2 - u], top[:, GE - 1:GE]).then_inc(carry_ready, 1)
                    one_hots(v + 1, 1 - u)
                    dve.wait_ge(maxT_ready, v + 1)
                    V.tensor_tensor(diff[u][:, :], score[u][:, :], ps_max[:, :], ALU.subtract).then_inc(diff_ready, 1)
                    dve.wait_ge(ex_ready, v + 1)
                    out = zs.rearrange("p (k h f) -> p k h f", k=G, h=HEADS)
                    z = rows[:, :, 0:D].rearrange("p k (h f) -> p k h f", h=HEADS)
                    weight = ex[u][:, :].rearrange("p (k h o) -> p k h o", k=G, o=1).broadcast_to([P, G, HEADS, HF])
                    for q in range(2):
                        k = slice(4 * q, 4 * q + 4)
                        V.tensor_tensor(out[:, k], z[:, k], weight[:, k], ALU.mult).then_inc(zs_ready, 1)
            add_window(steps - 1, 1)


def gat_node_stage(nc, m, layer):
    V = nc.vector
    with ExitStack() as ctx:
        def sem(name):
            return m.sems.enter_context(nc.semaphore(f"gn{layer}_" + name))

        def ps(name, cols):
            return ctx.enter_context(nc.psum_tensor(f"gn{layer}_" + name, [P, cols], F32))

        b = node_buffers(nc, m, ctx, "gat")
        den = [m.scratch[0:HEADS, 9000 + u * PB:9000 + (u + 1) * PB] for u in range(2)]
        pR = [ps(f"pR{u}", 512) for u in range(2)]
        pT = ps("pT", 512)
        pZ = [ps(f"pZ{t}", ZW) for t in range(2)]
        in_ = [sem(f"in{u}") for u in range(2)]
        st = [sem(f"stored{u}") for u in range(2)]
        s_max, s_den, s_pR, s_t, s_v, s_neg, s_ex, s_em, s_hT, s_pT, s_pZ, s_rows = [
            sem(n) for n in ("max", "den", "pR", "t", "v", "neg", "ex", "em", "hT", "pT", "pZ", "rows")]
        block = ctx.enter_context(nc.Block())
        LOADS = 1 + layer

        def rows_of(t, i):
            return t[bass.ds(i * PB, PB), :].rearrange("(t p) d -> p t d", p=P)

        def tile(a, w=D):
            return a[:, 0:2 * w].rearrange("p (t d) -> p t d", t=2)

        @block.sync
        def _(sp):
            def load(i, u):
                sp.dma_start(b.x[u], m.hT[layer][bass.ds(i, 1), :, :].rearrange("o p n -> (o p) n")).then_inc(in_[u], 16)
                if layer == 1:
                    sp.dma_start(tile(b.skip[u]), rows_of(m.x1_rows, i)).then_inc(in_[u], 16)

            def step(i, u, last):
                if layer == 0:
                    sp.wait_ge(s_hT, i + (u + 1))
                    sp.dma_start(m.hT[1][bass.ds(i + u, 1), :, :].rearrange("o p n -> (o p) n"), b.hT[u]).then_inc(st[u], 16)
                sp.wait_ge(s_rows, i + (u + 1))
                if layer == 0:
                    sp.dma_start(rows_of(m.z_rows[1], i + u), tile(b.rows[u], ZW)).then_inc(st[u], 16)
                else:
                    sp.dma_start(rows_of(m.io["out"], i + u), tile(b.rows[u])).then_inc(st[u], 16)
                sp.wait_ge(st[u], (i * 8 + 16) * (2 - layer))
                if not last:
                    load(i + (u + 2), u)

            for u in range(2):
                load(u, u)
            with sp.Fori(0, NPB // 2 - 1) as half:
                i = half * 2
                for u in range(2):
                    step(i, u, False)
            for u in range(2):
                step(NPB - 2, u, True)

        @block.tensor
        def _(pe):
            with pe.Fori(0, NPB // 2) as half:
                i = half * 2
                for u in range(2):
                    n = i + (u + 1)
                    pe.wait_ge(s_den, n)
                    for c in range(2):
                        ins = nc.tensor.matmul(pR[u][:, c * PB:(c + 1) * PB], m.headsel[:, c, :], den[u],
                                               start=(c == 0), stop=True, skip_group_check=True)
                    ins.then_inc(s_pR, 1)
                    if layer == 0:
                        node_pe_tail(nc, pe, m, b, u, n, None, pZ, None, None, s_hT, s_pZ, 1)
                    else:
                        pe.wait_ge(s_hT, n)
                        for t in range(2):
                            for c in range(2):
                                ins = nc.tensor.transpose(pT[:, t * D + c * P:t * D + (c + 1) * P],
                                                          b.hT[u][:, c * PB + t * P:c * PB + (t + 1) * P], m.ident[:])
                        ins.then_inc(s_pT, 1)

        @block.vector
        def _(dve):
            cols = m.nodes[:, 0:2 * NC].rearrange("p (c n) -> p c n", c=2)
            with dve.Fori(0, NPB // 2) as half:
                i = half * 2
                for u in range(2):
                    n = i + (u + 1)
                    at = bass.ds((i + u) * PB, PB)
                    dve.wait_ge(in_[u], (i * 8 + 16) * LOADS)
                    V.tensor_scalar(den[u], m.nodes[0:HEADS, 2 * NC:3 * NC][:, at], 1e-30, None, ALU.max).then_inc(s_max, 1)
                    dve.wait_ge(s_max, n)
                    V.reciprocal(den[u], den[u]).then_inc(s_den, 1)
                    dve.wait_ge(s_pR, n)
                    t = b.h[u].rearrange("p (c n) -> p c n", c=2)
                    x = b.x[u].rearrange("p (c n) -> p c n", c=2)
                    V.tensor_tensor(t, cols[:, :, at], pR[u][:, :].rearrange("p (c n) -> p c n", c=2), ALU.mult
                                    ).then_inc(s_t, 1)
                    dve.wait_ge(s_t, n)
                    for c in range(2):
                        ins = V.scalar_tensor_tensor(x[:, c, :], x[:, c, :], m.bias[layer][:, c:c + 1], t[:, c, :],
                                                     ALU.add, ALU.add)
                    ins.then_inc(s_v, 1)
                    dve.wait_ge(s_v, n)
                    V.tensor_scalar(b.h[u], b.x[u], 0.0, None, ALU.min).then_inc(s_neg, 1)
                    dve.wait_ge(s_ex, n)
                    V.tensor_scalar(b.h[u], b.h[u], -1.0, None, ALU.add).then_inc(s_em, 1)
                    dve.wait_ge(s_em, n)
                    V.scalar_tensor_tensor(b.hT[u], b.x[u], 0.0, b.h[u], ALU.max, ALU.add).then_inc(s_hT, 1)
                    if layer == 1:
                        dve.wait_ge(s_pT, n)
                        V.tensor_tensor(b.rows[u][:, 0:2 * D], pT[:, :], b.skip[u], ALU.add).then_inc(s_rows, 1)

        @block.scalar
        def _(act):
            with act.Fori(0, NPB // 2) as half:
                i = half * 2
                for u in range(2):
                    n = i + (u + 1)
                    act.wait_ge(s_neg, n)
                    nc.scalar.activation(b.h[u], b.h[u], ACT.Exp).then_inc(s_ex, 1)
                    if layer == 0:
                        node_act_tail(nc, act, m, b, u, n, pZ, s_pZ, s_rows)


def build(nc, io):
    with ExitStack() as ctx:
        m = allocate(nc, ctx, io)
        setup_stage(nc, m)
        input_stage(nc, m)
        conv_edge_stage(nc, m)
        conv_node_stage(nc, m)
        for layer in range(2):
            gat_edge_stage(nc, m, layer)
            gat_node_stage(nc, m, layer)


def kernel(**inputs):
    import numpy as np
    import concourse.bacc as bacc
    from concourse.bass_utils import run_bass_kernel_spmd as run

    a = {k: np.ascontiguousarray(v) for k, v in inputs.items()}

    def padded(rows, n, fill=0):
        out = np.full((n,) + rows.shape[1:], fill, rows.dtype)
        out[:rows.shape[0]] = rows
        return out

    dst = padded(a["dst"], EP, N)
    line = np.full((NG + 1) * GE + 1, N, dst.dtype)
    line[0] = -1
    line[1:1 + EP] = dst
    arrays = {
        "x": padded(a["x"], NC),
        "nvec_t": np.ascontiguousarray(padded(a["node_vec1"], NC).reshape(NT, P).T),
        "src_t": np.ascontiguousarray(padded(a["src"], EP).reshape(NTILES, P).T),
        "dst_t": np.ascontiguousarray(dst.reshape(NTILES, P).T),
        "dst_line": line,
        "dst_ends": np.concatenate([dst[0::GE], dst[GE - 1::GE]]).reshape(1, 2 * NG),
        "sh_t": np.ascontiguousarray(padded(a["edge_attr_4"], EP).reshape(NTILES, P, 4).transpose(1, 0, 2)).reshape(P, 4 * NTILES),
        "ea8_t": np.ascontiguousarray(padded(a["edge_attr_8"], EP).reshape(NG, 2, GE // 2, NBAS).transpose(0, 1, 3, 2)).reshape(NG * 2 * NBAS, GE // 2),
    }
    for name in ("W_sc0", "W_sc1", "W_lin1_0", "W_lin1_1", "fc_w0", "fc_w1", "W_lin2_0", "W_lin2_1"):
        arrays[name] = a["L0_gnn_" + name]
    for l in range(2):
        arrays[f"W{l}"] = a[f"L1_gnn_W{l}"]
        arrays[f"al{l}"] = a[f"L1_gnn_al{l}"].reshape(D)
        arrays[f"ar{l}"] = a[f"L1_gnn_ar{l}"].reshape(D)
        arrays[f"b{l}_t"] = np.ascontiguousarray(a[f"L1_gnn_b{l}"].reshape(2, P).T)

    nc = bacc.Bacc("TRN2", target_bir_lowering=False, num_devices=1)
    io = {k: nc.dram_tensor(k, v.shape, mybir.dt.from_np(v.dtype), kind="ExternalInput").ap() for k, v in arrays.items()}
    io["out"] = nc.dram_tensor("out", (NC, D), F32, kind="ExternalOutput").ap()
    build(nc, io)
    r = run(nc, [arrays], core_ids=[0])
    return r.results[0]["out"][:N]
```

```python
from contextlib import ExitStack

import concourse.bass as bass
from concourse import mybir

F32 = mybir.dt.float32
I32 = mybir.dt.int32
ACT = mybir.ActivationFunctionType
ALU = mybir.AluOpType
AX = mybir.AxisListType

P = 128
N = 6250
E = 106250
D = 256
MUL = 64
HEADS = 4
HF = D // HEADS
NBAS = 8
RN = 64
G = 8
GE = G * P
NG = -(-E // GE)
NTILES = NG * G
EP = NG * GE
NW = 128
PB = 2 * P
NPB = 2 * -(-(N + NW) // (2 * PB))
NC = NPB * PB
NT = NC // P
SPARE = NC - NW
QV = 2
VP = -(-(NG + NC // NW + 12) // QV)
VT = QV * VP
MIN_QUADS, MAX_QUADS = -(-NG // 4), -(-(NG + N // NW) // 4)
FLAG_COLS = (NG + 1) * GE // P
SCRATCH = 10240 + 256
ZW = D + 2 * HEADS
LOW = -1.0e38
EPS = 1e-5
INV_M = MUL ** -0.5
C_S = 0.3826834261417389
C_X = 0.9238795042037964
OUT_SCALE = C_X * (2 * MUL) ** -0.5 / 4.0 * RN ** -0.5
INV_SQRT3 = 3.0 ** -0.5
NEG_SLOPE = 0.2


class Mem:
    pass


def allocate(nc, ctx, io):
    m = Mem()
    m.io = io
    m.sems = ctx

    def sb(name, shape, dt=F32):
        return ctx.enter_context(nc.sbuf_tensor(name, shape, dt))

    def dram(name, shape, dt=F32):
        return nc.dram_tensor(name, shape, dt, kind="Internal").ap()

    m.h_rows = dram("h_rows", (NC, D))
    m.x_skip = dram("x_skip", (NC, D))
    m.x1_rows = dram("x1_rows", (NC, D))
    m.hT = [dram(f"hT{l}", (NPB, P, 2 * PB)) for l in range(2)]
    m.z_rows = [dram(f"z_rows{l}", (NC, ZW)) for l in range(2)]
    m.er_parts = [dram(f"er_parts{l}", (NC, 12), mybir.dt.bfloat16) for l in range(2)]
    m.same_seg = dram("same_seg", ((NG + 1) * GE,))
    m.steps_i = dram("steps_i", (2, VT), I32)
    m.steps_f = dram("steps_f", (1, VT))

    m.nodes = sb("nodes", [P, 5 * NC])
    m.scratch = sb("scratch", [P, SCRATCH])
    m.src = sb("src_sb", [P, NTILES], I32)
    m.dst = sb("dst_sb", [P, NTILES], I32)
    m.sh = sb("sh_sb", [P, NTILES * 4])
    m.base_col = sb("base_col", [P, VT])
    m.tab = sb("tab", [1, 2 * VT + 1], I32)
    m.nsteps = sb("nsteps", [1, 2], I32)
    m.nvec = sb("nvec", [P, 3 * NT])
    m.ident = sb("ident", [P, P])
    m.cols = sb("cols", [P, NW])
    m.fc0 = sb("fc0_sb", [2 * NBAS, P])
    m.fc1 = sb("fc1_sb", [P, 4 * MUL])
    m.lin1 = sb("lin1_sb", [P, 2, 4 * MUL])
    m.lin2 = sb("lin2_sb", [P, 5, P])
    m.wz = [sb(f"wz{l}", [P, 2, ZW]) for l in range(2)]
    m.bias = [sb(f"bias{l}", [P, 2]) for l in range(2)]
    m.headsel = sb("headsel", [HEADS, 2, P])
    m.eps = sb("eps", [P, 1])
    m.carry = sb("carry", [HEADS, 2])
    return m


def table_group(m, v):
    return m.tab[0:1, bass.ds(v, 1)]


def table_base(m, v):
    return m.tab[0:1, bass.ds(v + (VT + 1), 1)]


def load_group(eng, m, v):
    return eng.value_load(table_group(m, v), min_val=0, max_val=NG - 1)


def load_base(eng, m, v):
    return eng.value_load(table_base(m, v), min_val=0, max_val=SPARE)


def load_steps(eng, m):
    return eng.value_load(m.nsteps[0:1, 0:1], min_val=MIN_QUADS, max_val=MAX_QUADS)


def setup_stage(nc, m):
    io = m.io
    with ExitStack() as ctx:
        def sb(name, shape, dt=F32):
            return ctx.enter_context(nc.sbuf_tensor(name, shape, dt))

        def sem(name):
            return m.sems.enter_context(nc.semaphore(name))

        free = [0]

        def part(parts, width, dt=F32):
            a = m.scratch[0:parts, free[0]:free[0] + width]
            free[0] += width
            return a if dt == F32 else a.bitcast(dt)

        ends = part(1, 2 * NG, I32)
        span = part(1, NG, I32)
        span7 = part(1, NG, I32)
        wins = part(1, NG)
        ones_row = part(1, NG)
        incl = part(1, NG)
        rows2 = part(1, 2 * NG)
        total = part(1, 1, I32)
        ones_lhs = part(1, VP)
        vcol = part(VP, QV)
        gcols = part(VP, NG)
        hit = part(VP, QV * NG)
        step = part(VP, QV * 6)
        step_i = part(VP, QV * 2, I32)
        dst_a = part(P, FLAG_COLS, I32)
        dst_b = part(P, FLAG_COLS, I32)
        differ = part(P, FLAG_COLS)
        att = part(P, 4 * D)
        att_w = part(P, 2 * D)
        ps_rows = ctx.enter_context(nc.psum_tensor("ps_rows", [VP, 2 * NG], F32))

        s_ends = sem("su_ends")
        s_edges = sem("su_edges")
        s_dstrows = sem("su_dstrows")
        s_w = sem("su_weights")
        s_zero = sem("su_zeroed")
        s_pool = sem("su_pool")
        s_dve = sem("su_dve")
        s_bc = sem("su_rows_broadcast")
        s_tab = sem("su_table_stored")
        s_tabback = sem("su_table_loaded")
        s_flags = sem("su_flags_stored")

        loads = [0]
        block = ctx.enter_context(nc.Block())

        @block.sync
        def _(sp):
            sp.dma_start(ends, io["dst_ends"]).then_inc(s_ends, 16)
            sp.dma_start(dst_a, io["dst_line"][0:(NG + 1) * GE].rearrange("(p j) -> p j", p=P)).then_inc(s_dstrows, 16)
            sp.dma_start(dst_b, io["dst_line"][1:(NG + 1) * GE + 1].rearrange("(p j) -> p j", p=P)).then_inc(s_dstrows, 16)
            sp.dma_start(m.src[:, :], io["src_t"]).then_inc(s_edges, 16)
            sp.dma_start(m.dst[:, :], io["dst_t"]).then_inc(s_edges, 16)
            sp.dma_start(m.sh[:, :], io["sh_t"]).then_inc(s_edges, 16)
            sp.wait_ge(s_zero, 1)
            todo = [(m.nvec[:, 0:NT], io["nvec_t"]),
                    (m.fc0[0:NBAS, 0:RN], io["fc_w0"]), (m.fc0[NBAS:2 * NBAS, RN:2 * RN], io["fc_w0"]),
                    (m.fc1[0:RN, :], io["fc_w1"]), (m.fc1[RN:2 * RN, :], io["fc_w1"])]
            for c in range(2):
                for half in range(2):
                    rows = slice(half * MUL, half * MUL + MUL)
                    at = half * MUL
                    scalar_part = c == 0 and half == 0
                    todo.append((m.lin1[rows, c, at:at + MUL], io["W_lin1_0" if scalar_part else "W_lin1_1"]))
                    todo.append((m.lin1[rows, c, 2 * MUL + at:2 * MUL + at + MUL],
                                 io["W_sc0" if scalar_part else "W_sc1"]))
            lo, hi = slice(0, MUL), slice(MUL, 2 * MUL)
            todo += [(m.lin2[lo, 0, lo], io["W_lin2_0"][lo, :]), (m.lin2[hi, 0, hi], io["W_lin2_1"][hi, :]),
                     (m.lin2[lo, 1, lo], io["W_lin2_1"][hi, :]), (m.lin2[hi, 1, hi], io["W_lin2_1"][hi, :])]
            for c in range(3):
                d_rows, b_rows = (lo, hi) if c == 0 else (hi, lo)
                todo += [(m.lin2[b_rows, 2 + c, hi], io["W_lin2_1"][lo, :]),
                         (m.lin2[d_rows, 2 + c, lo], io["W_lin2_0"][hi, :])]
            for l in range(2):
                todo.append((m.wz[l][:, :, 0:D], io[f"W{l}"].rearrange("(c p) n -> p c n", p=P)))
                todo.append((m.bias[l][:, :], io[f"b{l}_t"]))
                todo.append((att[:, (2 * l) * D:(2 * l + 1) * D], io[f"al{l}"].partition_broadcast(P)))
                todo.append((att[:, (2 * l + 1) * D:(2 * l + 2) * D], io[f"ar{l}"].partition_broadcast(P)))
            for dst, src in todo:
                sp.dma_start(dst, src).then_inc(s_w, 16)
            loads[0] = len(todo)
            sp.wait_ge(s_dve, FLAGS_DONE)
            sp.dma_start(m.same_seg.rearrange("(p j) -> p j", p=P), differ).then_inc(s_flags, 16)
            sp.wait_ge(s_dve, TABLE_DONE)
            for q in range(QV):
                at = slice(q * VP, (q + 1) * VP)
                for k in range(2):
                    sp.dma_start(m.steps_i[k:k + 1, at].rearrange("o v -> v o"),
                                 step_i[:, 2 * q + k:2 * q + k + 1]).then_inc(s_tab, 16)
                sp.dma_start(m.steps_f[0:1, at].rearrange("o v -> v o"),
                             step[:, 6 * q + 5:6 * q + 6]).then_inc(s_tab, 16)
            sp.wait_ge(s_tab, 3 * QV * 16)
            sp.dma_start(m.tab[:, 0:VT], m.steps_i[0:1, :]).then_inc(s_tabback, 16)
            sp.dma_start(m.tab[:, VT + 1:2 * VT + 1], m.steps_i[1:2, :]).then_inc(s_tabback, 16)
            sp.dma_start(m.base_col[:, :], m.steps_f[0, :].partition_broadcast(P)).then_inc(s_tabback, 16)
            sp.wait_ge(s_tabback, 48)
            sp.wait_ge(s_flags, 16)
            sp.wait_ge(s_edges, 48)

        @block.gpsimd
        def _(pool):
            nc.gpsimd.memset(m.ident[:], 0.0)
            nc.gpsimd.memset(m.headsel[:], 0.0).then_inc(s_pool, 1)
            pool.wait_ge(s_pool, 1)
            nc.gpsimd.affine_select(out=m.ident[:], in_=m.ident[:], compare_op=ALU.not_equal, fill=1.0, base=0,
                                    pattern=[[-1, P]], channel_multiplier=1)
            sel = m.headsel[:, :, :].rearrange("h c (a f) -> h (c a) f", a=2)
            nc.gpsimd.affine_select(out=sel, in_=sel, compare_op=ALU.not_equal, fill=1.0, base=0,
                                    pattern=[[-1, HEADS], [0, HF]], channel_multiplier=1)
            nc.gpsimd.iota(m.cols[:], [[1, NW]], base=0, channel_multiplier=0, allow_small_or_imprecise_dtypes=True)
            nc.gpsimd.iota(gcols, [[1, NG]], base=0, channel_multiplier=0, allow_small_or_imprecise_dtypes=True)
            nc.gpsimd.iota(vcol, [[VP, QV]], base=0, channel_multiplier=1,
                           allow_small_or_imprecise_dtypes=True).then_inc(s_pool, 1)

        @block.tensor
        def _(pe):
            pe.wait_ge(s_dve, ROWS_DONE)
            nc.tensor.matmul(ps_rows[:, :], ones_lhs, rows2, start=True, stop=True).then_inc(s_bc, 1)

        marks = {}

        @block.vector
        def _(dve):
            count = [0]

            def done(ins):
                count[0] += 1
                ins.then_inc(s_dve, 1)
                dve.wait_ge(s_dve, count[0])

            V = nc.vector
            V.memset(m.fc0[:], 0.0)
            V.memset(m.lin1[:], 0.0)
            V.memset(m.lin2[:], 0.0).then_inc(s_zero, 1)
            V.memset(m.eps[:], EPS)
            V.memset(m.carry[:], LOW)
            V.memset(m.tab[:, VT:VT + 1], SPARE)
            V.memset(ones_lhs, 1.0)
            done(V.memset(ones_row, 1.0))
            dve.wait_ge(s_ends, 16)
            done(V.tensor_tensor(span, ends[:, NG:2 * NG], ends[:, 0:NG], ALU.subtract))
            done(V.tensor_scalar(span7, span, NW.bit_length() - 1, None, ALU.arith_shift_right))
            done(V.tensor_scalar(wins, span7, 1.0, None, ALU.add))
            done(V.tensor_tensor_scan(incl, ones_row, wins, 0.0, ALU.mult, ALU.add))
            done(V.tensor_tensor(rows2[:, 0:NG], incl, wins, ALU.subtract))
            done(V.scalar_tensor_tensor(rows2[:, NG:2 * NG], rows2[:, 0:NG], -float(NW), ends[:, 0:NG],
                                        ALU.mult, ALU.add))
            marks["rows"] = count[0]
            done(V.tensor_copy(total, incl[:, NG - 1:NG]))
            done(V.tensor_scalar(total, total, 3.0, None, ALU.add))
            V.tensor_scalar(m.nsteps[:, 0:1], total, 2, None, ALU.arith_shift_right)
            dve.wait_ge(s_pool, 2)
            dve.wait_ge(s_bc, 1)
            for q in range(QV):
                h = hit[:, q * NG:(q + 1) * NG]
                c = step[:, 6 * q:6 * q + 6]
                done(V.tensor_scalar(h, ps_rows[:, 0:NG], vcol[:, q:q + 1], None, ALU.is_le))
                done(V.tensor_reduce(c[:, 0:1], h, AX.X, ALU.add))
                done(V.tensor_scalar(c[:, 1:2], c[:, 0:1], -1.0, None, ALU.add))
                done(V.scalar_tensor_tensor(h, gcols, c[:, 1:2], ps_rows[:, NG:2 * NG], ALU.is_equal, ALU.mult))
                done(V.tensor_reduce(c[:, 2:3], h, AX.X, ALU.add))
                done(V.scalar_tensor_tensor(c[:, 3:4], vcol[:, q:q + 1], float(NW), c[:, 2:3], ALU.mult, ALU.add))
                done(V.tensor_scalar(c[:, 5:6], c[:, 3:4], float(SPARE), None, ALU.min))
                V.tensor_copy(step_i[:, 2 * q:2 * q + 1], c[:, 1:2])
                done(V.tensor_copy(step_i[:, 2 * q + 1:2 * q + 2], c[:, 5:6]))
            marks["table"] = count[0]
            dve.wait_ge(s_dstrows, 32)
            done(V.tensor_tensor(differ, dst_a, dst_b, ALU.not_equal))
            done(V.tensor_scalar(differ, differ, LOW, None, ALU.mult))
            marks["flags"] = count[0]
            assert (marks["rows"], marks["table"], marks["flags"]) == (ROWS_DONE, TABLE_DONE, FLAGS_DONE), marks
            dve.wait_ge(s_w, 16 * SETUP_LOADS)
            V.tensor_scalar(m.nvec[:, NT:2 * NT], m.nvec[:, 0:NT], INV_M, None, ALU.mult)
            V.tensor_scalar(m.nvec[:, 2 * NT:3 * NT], m.nvec[:, 0:NT], C_S * INV_M, None, ALU.mult)
            done(V.tensor_scalar(m.lin2[:], m.lin2[:], OUT_SCALE, None, ALU.mult))
            V.tensor_scalar(m.lin2[0:MUL, 2, 0:MUL], m.lin2[0:MUL, 2, 0:MUL], INV_SQRT3, None, ALU.mult)
            V.tensor_scalar(m.lin2[MUL:2 * MUL, 3:5, 0:MUL], m.lin2[MUL:2 * MUL, 3:5, 0:MUL], INV_SQRT3, None, ALU.mult)
            for l in range(2):
                for k in range(2):
                    a = att[:, (2 * l + k) * D:(2 * l + k + 1) * D].rearrange("p (o d) -> p o d", o=1)
                    w = att_w.rearrange("p (c d) -> p c d", c=2)
                    done(V.tensor_tensor(w, m.wz[l][:, :, 0:D], a.broadcast_to([P, 2, D]), ALU.mult))
                    done(V.tensor_reduce(m.wz[l][:, :, D + k * HEADS:D + (k + 1) * HEADS],
                                         att_w.rearrange("p (c h f) -> p c h f", c=2, h=HEADS), AX.X, ALU.add))

        assert loads[0] == SETUP_LOADS, loads


ROWS_DONE = 7
TABLE_DONE = ROWS_DONE + 2 + QV * 8
FLAGS_DONE = TABLE_DONE + 2
SETUP_LOADS = 5 + 8 + 4 + 6 + 8


QUADS = NPB // 4 - 1


def in_order(eng, *parts):
    def one_pass(t, r):
        for lag, part in parts:
            if not isinstance(t, int) or 0 <= t - lag < NPB:
                part(t - lag, (r - lag) % 4)

    for t in range(-2, 4):
        one_pass(t, t % 4)
    with eng.Fori(0, QUADS) as quad:
        for r in range(4):
            one_pass(quad * 4 + (4 + r), r)
    for t in range(4 + 4 * QUADS, NPB + 3):
        one_pass(t, t % 4)


def wait_slot(eng, used, n, slots=4):
    if not isinstance(n, int) or n >= slots:
        eng.wait_ge(used, n - (slots - 1))


def slot_loaded(n, r):
    return (n - r) * 4 + 16


def slot_stored(n, u):
    return (n - u) * 8 + 16


def rows_of(t, n):
    return t[bass.ds(n * PB, PB), :].rearrange("(t p) d -> p t d", p=P)


def tile(a, w=D):
    return a[:, 0:2 * w].rearrange("p (t d) -> p t d", t=2)


def chunks(a, c=2):
    return a.rearrange("p (c n) -> p c n", c=c)


def node_buffers(m, tag):
    b = Mem()
    free = [0]

    def part(width, slots=2):
        a = [m.scratch[:, free[0] + u * width:free[0] + (u + 1) * width] for u in range(slots)]
        free[0] += slots * width
        assert free[0] <= SCRATCH
        return a

    b.x = part(2 * D, 4)
    b.skip = part(2 * D, 4 if tag == "gat" else 2)
    b.h = part(2 * D)
    b.hT = part(2 * PB)
    b.rows = part(2 * ZW)
    b.y = part(5 * PB) if tag == "l0out" else None
    b.parts = [a.bitcast(mybir.dt.bfloat16) for a in part(12)]
    b.rest = part(2 * HEADS)
    b.zero = part(PB, 1)[0]
    b.den = [a[0:HEADS, :] for a in part(PB)]
    b.stat = part(12)
    b.mv = part(4)
    b.sd = part(2)
    b.rs = part(2)
    b.nm = part(2)
    return b


def moments(V, dve, b, u, n, x, s_bn, s_mv, s_go):
    for t in range(2):
        ins = V.bn_stats(b.stat[u][:, 6 * t:6 * t + 6], x[:, t, :])
    ins.then_inc(s_bn, 1)
    dve.wait_ge(s_bn, n + 1).then_inc(s_go, 1)
    for t in range(2):
        ins = V.bn_aggr(b.mv[u][:, 2 * t:2 * t + 2], b.stat[u][:, 6 * t:6 * t + 6])
    ins.then_inc(s_mv, 1)


def deviation(nc, act, m, b, u, n, s_mv, s_sd):
    act.wait_ge(s_mv, n + 1)
    var = b.mv[u].rearrange("p (t k) -> p t k", k=2)[:, :, 1]
    nc.scalar.activation(b.sd[u], var, ACT.Sqrt, bias=m.eps[:, 0:1]).then_inc(s_sd, 1)


def scale_and_shift(V, dve, b, u, n, s_sd, s_rs, s_nm):
    dve.wait_ge(s_sd, n + 1)
    V.reciprocal(b.rs[u], b.sd[u]).then_inc(s_rs, 1)
    dve.wait_ge(s_rs, n + 1)
    mean = b.mv[u].rearrange("p (t k) -> p t k", k=2)[:, :, 0]
    V.scalar_tensor_tensor(b.nm[u], mean, -1.0, b.rs[u], ALU.mult, ALU.mult).then_inc(s_nm, 1)


def input_stage(nc, m):
    V = nc.vector
    with ExitStack() as ctx:
        def sem(name):
            return m.sems.enter_context(nc.semaphore("in_" + name))

        def ps(name, cols):
            return ctx.enter_context(nc.psum_tensor("in_" + name, [P, cols], F32))

        b = node_buffers(m, "in")
        pT = [ps(f"pT{u}", 512) for u in range(2)]
        pO = [[ps(f"pO{u}{t}", 512) for t in range(2)] for u in range(2)]
        x_in = [sem(f"x_in{r}") for r in range(4)]
        s_go, s_bn, s_mv, s_sd, s_rs, s_nm, s_h, s_pT, s_hT, s_pO, s_rows, s_skip = [
            sem(n) for n in ("go", "bn", "mv", "sd", "rs", "nm", "h", "pT", "hT", "pO", "rows", "skip")]
        st_rows = [sem(f"strows{u}") for u in range(2)]
        st_skip = [sem(f"stskip{u}") for u in range(2)]
        block = ctx.enter_context(nc.Block())

        @block.sync
        def _(sp):
            def load(n, r):
                wait_slot(sp, s_skip, n)
                sp.dma_start(tile(b.x[r]), rows_of(m.io["x"], n)).then_inc(x_in[r], 16)

            def store(n, r):
                u = r % 2
                sp.wait_ge(s_rows, n + 1)
                sp.dma_start(rows_of(m.h_rows, n), tile(b.rows[u])).then_inc(st_rows[u], 16)
                sp.wait_ge(s_skip, n + 1)
                sp.dma_start(rows_of(m.x_skip, n), tile(b.skip[u])).then_inc(st_skip[u], 16)

            for u in range(2):
                sp.sem_inc(st_rows[u], 16)
                sp.sem_inc(st_skip[u], 16)
            in_order(sp, (-2, load), (2, store))
            for u in range(2):
                sp.wait_ge(st_rows[u], NPB * 8 + 16)
                sp.wait_ge(st_skip[u], NPB * 8 + 16)

        @block.gpsimd
        def _(pool):
            nc.gpsimd.memset(m.nodes[:], 0.0)

        @block.vector
        def _(dve):
            def statistics(n, r):
                dve.wait_ge(x_in[r], slot_loaded(n, r))
                moments(V, dve, b, r % 2, n, tile(b.x[r]), s_bn, s_mv, s_go)

            def scales(n, r):
                scale_and_shift(V, dve, b, r % 2, n, s_sd, s_rs, s_nm)

            def skip(n, r):
                u = r % 2
                x, sk = tile(b.x[r]), tile(b.skip[u])
                dve.wait_ge(s_pO, n + 1)
                dve.wait_ge(st_skip[u], slot_stored(n, u))
                for t in range(2):
                    zc = m.nvec[:, bass.ds(n * 2 + (2 * NT + t), 1)]
                    V.scalar_tensor_tensor(sk[:, t, 0:MUL], pO[u][t][:, D:D + MUL], zc, x[:, t, 0:MUL],
                                           ALU.mult, ALU.add)
                    ins = V.scalar_tensor_tensor(
                        sk[:, t, MUL:D].rearrange("p (v c) -> p v c", c=3),
                        pO[u][t][:, D + MUL:2 * D].rearrange("p (c v) -> p v c", c=3), zc,
                        x[:, t, MUL:D].rearrange("p (v c) -> p v c", c=3), ALU.mult, ALU.add)
                ins.then_inc(s_skip, 1)

            in_order(dve, (0, scales), (-1, statistics), (2, skip))

        @block.scalar
        def _(act):
            def sd(n, r):
                deviation(nc, act, m, b, r % 2, n, s_mv, s_sd)

            def hidden(n, r):
                u = r % 2
                x, h = tile(b.x[r]), tile(b.h[u])
                act.wait_ge(s_nm, n + 1)
                for t in range(2):
                    nc.scalar.activation(h[:, t, 0:MUL], x[:, t, 0:MUL], ACT.Relu,
                                         bias=b.nm[u][:, t:t + 1], scale=b.rs[u][:, t:t + 1])
                    ins = nc.scalar.activation(h[:, t, MUL:D].rearrange("p (c v) -> p v c", c=3),
                                               x[:, t, MUL:D].rearrange("p (v c) -> p v c", c=3), ACT.Relu,
                                               bias=b.nm[u][:, t:t + 1], scale=b.rs[u][:, t:t + 1])
                ins.then_inc(s_h, 1)

            def copy_hT(n, r):
                act.wait_ge(s_pT, n + 1)
                wait_slot(act, s_pO, n, 2)
                nc.scalar.copy(b.hT[r % 2], pT[r % 2][:]).then_inc(s_hT, 1)

            def rows(n, r):
                u = r % 2
                act.wait_ge(s_skip, n + 1)
                act.wait_ge(st_rows[u], slot_stored(n, u))
                for t in range(2):
                    zs = m.nvec[:, bass.ds(n * 2 + (NT + t), 1)]
                    ins = nc.scalar.activation(tile(b.rows[u])[:, t, :], pO[u][t][:, 0:D], ACT.Copy, scale=zs)
                ins.then_inc(s_rows, 1)

            in_order(act, (0, hidden), (-1, sd), (1, copy_hT), (2, rows))

        @block.tensor
        def _(pe):
            def transposes(n, r):
                u = r % 2
                h = tile(b.h[u])
                pe.wait_ge(s_h, n + 1)
                for c in range(2):
                    for t in range(2):
                        ins = nc.tensor.transpose(pT[u][:, c * PB + t * P:c * PB + (t + 1) * P],
                                                  h[:, t, c * P:(c + 1) * P], m.ident[:])
                ins.then_inc(s_pT, 1)

            def products(n, r):
                u = r % 2
                pe.wait_ge(s_hT, n + 1)
                wait_slot(pe, s_rows, n, 2)
                for t in range(2):
                    for c in range(2):
                        out = pO[u][t][:, :].rearrange("p (k f) -> p k f", k=2)[:, :, c * P:(c + 1) * P]
                        ins = nc.tensor.matmul(out, b.hT[u][:, c * PB + t * P:c * PB + (t + 1) * P],
                                               m.lin1[:, c, :], start=(c == 0), stop=True, skip_group_check=True)
                ins.then_inc(s_pO, 1)

            in_order(pe, (0, transposes), (1, products))


def conv_edge_stage(nc, m):
    V = nc.vector
    with ExitStack() as ctx:
        def sem(name):
            return m.sems.enter_context(nc.semaphore("ce_" + name))

        free = [0]

        def part(width, parts=P, slots=2):
            a = [m.scratch[0:parts, free[0] + u * width:free[0] + (u + 1) * width] for u in range(slots)]
            free[0] += slots * width
            assert free[0] <= SCRATCH
            return a

        xg = part(G * D)
        prod = part(2 * 9 * MUL)
        hot = part(2 * NW)
        sel0 = part(2 * NW)
        selv = part(2 * 3 * NW)
        hidT = part(GE // 2)
        ea8 = part(GE // 2, 2 * NBAS, 1)[0]
        idx = ctx.enter_context(nc.sbuf_tensor("ce_idx", [P, 2, G], I32))
        rel = ctx.enter_context(nc.sbuf_tensor("ce_rel", [P, 2, G], F32))
        ps_w = [ctx.enter_context(nc.psum_tensor(f"ce_w{k}", [P, 2, 4, MUL], F32)) for k in range(2)]
        ps_hid = ctx.enter_context(nc.psum_tensor("ce_hid", [P, GE // 2], F32))
        ps_sum = [ctx.enter_context(nc.psum_tensor(f"ce_sum{u}", [P, 4, NW], F32)) for u in range(2)]
        ps_sum4 = [ctx.enter_context(nc.psum_tensor(f"ce_sumd{u}", [P, NW], F32)) for u in range(2)]

        ea8_in = sem("ea8_in")
        got = [sem(f"gathered{u}") for u in range(2)]
        sp_done, idx_ready, pool_go, hid_ps, hid_ready, w_ready, rel_ready = [
            sem(n) for n in ("sp_done", "idx_ready", "pool_go", "hid_ps", "hid_ready", "w_ready", "rel_ready")]
        hot_ready = sem("hot_ready")
        sel0_ready = sem("sel0_ready")
        selv_ready = sem("selv_ready")
        msg_ready = sem("msg_ready")
        pair_summed = sem("pair_summed")
        b_again = sem("b_again")
        added = sem("added")
        block = ctx.enter_context(nc.Block())

        @block.sync
        def _(sp):
            def load(v):
                g = load_group(sp, m, v)
                sp.dma_start(ea8, m.io["ea8_t"][bass.ds(g * 2 * NBAS, 2 * NBAS), :]).then_inc(ea8_in, 16)

            quads = load_steps(sp, m)
            load(0)
            with sp.Fori(0, quads * 2) as half:
                for u in range(2):
                    sp.wait_ge(hid_ps, half * 2 + (u + 1))
                    load(half * 2 + (u + 1))
            sp.wait_ge(ea8_in, quads * 64 + 16).then_inc(sp_done, 1)

        @block.scalar
        def _(act):
            quads = load_steps(act, m)

            def stage_idx(v, u):
                g = load_group(act, m, v)
                nc.scalar.copy(idx[:, u, :], m.src[:, bass.ds(g * G, G)]).then_inc(idx_ready, 1)

            def silu(v, u):
                act.wait_ge(hid_ps, v + 1)
                nc.scalar.activation(hidT[u], ps_hid[:, :], ACT.Silu, scale=NBAS ** -0.5).then_inc(hid_ready, 1)

            def copy_b(v, j):
                act.wait_ge(msg_ready, v * 4 + (j + 1))
                blocks = prod[j % 2].rearrange("p (t b f) -> p t b f", t=2, b=9)
                nc.scalar.copy(blocks[:, :, 7, :], blocks[:, :, 5, :]).then_inc(b_again, 1)

            def scale_pair(v, j, g):
                act.wait_ge(hot_ready, v * 4 + (j + 1))
                for t in range(2):
                    for c in range(3):
                        ins = nc.scalar.activation(selv[j % 2][:, (3 * t + c) * NW:(3 * t + c + 1) * NW],
                                                   hot[j % 2][:, t * NW:(t + 1) * NW], ACT.Copy,
                                                   scale=m.sh[:, bass.ds(g * (4 * G) + (4 * (2 * j + t) + 1 + c), 1)])
                ins.then_inc(selv_ready, 1)

            for u in range(2):
                stage_idx(u, u)
            silu(0, 0)
            scale_pair(0, 0, load_group(act, m, 0))
            with act.Fori(0, quads * 2) as half:
                for u in range(2):
                    v = half * 2 + u
                    g = load_group(act, m, v)
                    for j in range(4):
                        copy_b(v, j)
                        if j == 1:
                            silu(v + 1, 1 - u)
                        if j < 3:
                            scale_pair(v, j + 1, g)
                        else:
                            stage_idx(v + 2, u)
                            scale_pair(v + 1, 0, load_group(act, m, v + 1))

        @block.gpsimd
        def _(pool):
            quads = load_steps(pool, m)
            with pool.Fori(0, quads * 2) as half:
                for u in range(2):
                    pool.wait_ge(idx_ready, half * 2 + (u + 1)).then_inc(pool_go, 1)
                    for k in range(G):
                        nc.gpsimd.indirect_dma_start(
                            xg[u][:, k * D:(k + 1) * D], None, m.h_rows,
                            bass.IndirectOffsetOnAxis(ap=idx[:, u, k:k + 1], axis=0)).then_inc(got[u], 16)

        @block.tensor
        def _(pe):
            quads = load_steps(pe, m)

            def hidden(v):
                pe.wait_ge(ea8_in, v * 16 + 16)
                nc.tensor.matmul(ps_hid[:, :], m.fc0[:, :], ea8, start=True, stop=True).then_inc(hid_ps, 1)

            def weights(v, u, j):
                if j == 0:
                    pe.wait_ge(hid_ready, v + 1)
                for t in range(2):
                    half, col = divmod((2 * j + t) * P, GE // 2)
                    rows = slice(half * RN, half * RN + RN)
                    ins = nc.tensor.matmul(ps_w[j % 2][:, t, :, :].rearrange("p k f -> p (k f)"),
                                           hidT[u][rows, col:col + P], m.fc1[rows, :], start=True, stop=True)
                ins.then_inc(w_ready, 1)

            def sums(v, u, j):
                pe.wait_ge(msg_ready, v * 4 + (j + 1))
                pe.wait_ge(sel0_ready, v * 4 + (j + 1))
                if j == 0:
                    pe.wait_ge(added, v + 1)
                blocks = prod[j % 2].rearrange("p (t b f) -> p t b f", t=2, b=9)
                for t in range(2):
                    first = j == 0 and t == 0
                    last = j == 3 and t == 1
                    for c in range(2):
                        nc.tensor.matmul(ps_sum[u][:, c, :], blocks[:, t, 2 * c:2 * c + 2, :].rearrange("p b f -> p (b f)"),
                                         sel0[j % 2][:, t * NW:(t + 1) * NW], start=first and c == 0, stop=last,
                                         skip_group_check=True)
                    if t == 0:
                        pe.wait_ge(selv_ready, v * 4 + (j + 1))
                    for c in range(3):
                        out = ps_sum[u][:, 2 + c, :] if c < 2 else ps_sum4[u][:, :]
                        at = (4, 5, 7)[c]
                        if c == 2 and t == 0:
                            pe.wait_ge(b_again, v * 4 + (j + 1))
                        ins = nc.tensor.matmul(out, blocks[:, t, at:at + 2, :].rearrange("p b f -> p (b f)"),
                                               selv[j % 2][:, (3 * t + c) * NW:(3 * t + c + 1) * NW],
                                               start=first and c == 2, stop=last, skip_group_check=True)
                ins.then_inc(pair_summed, 1)

            pe.sem_inc(pair_summed, 2)
            hidden(0)
            weights(0, 0, 0)
            with pe.Fori(0, quads * 2) as half:
                for u in range(2):
                    v = half * 2 + u
                    for j in range(4):
                        if j < 3:
                            weights(v, u, j + 1)
                        else:
                            weights(v + 1, 1 - u, 0)
                        sums(v, u, j)
                        if j == 0:
                            hidden(v + 1)

        @block.vector
        def _(dve):
            quads = load_steps(dve, m)

            def messages(v, u, j):
                tiles = xg[u].rearrange("p (k b f) -> p k b f", k=G, b=4)[:, 2 * j:2 * j + 2, :, :]
                blocks = prod[j % 2].rearrange("p (t b f) -> p t b f", t=2, b=9)
                dve.wait_ge(pair_summed, v * 4 + (j + 1))
                dve.wait_ge(w_ready, v * 4 + (j + 1))
                if j == 0:
                    dve.wait_ge(got[u], (v - u) * 64 + 16 * G)
                w = ps_w[j % 2][:, :, :, :]
                V.tensor_tensor(blocks[:, :, 0:6:5, :], w[:, :, 0:2, :],
                                tiles[:, :, 0:1, :].broadcast_to([P, 2, 2, MUL]), ALU.mult)
                for a, out in ((2, blocks[:, :, 1:4, :]), (3, blocks[:, :, 4:9:2, :])):
                    ins = V.tensor_tensor(out, w[:, :, a:a + 1, :].broadcast_to([P, 2, 3, MUL]), tiles[:, :, 1:4, :], ALU.mult)
                ins.then_inc(msg_ready, 1)

            def relative(v, u, g):
                V.tensor_scalar(rel[:, u, :], m.dst[:, bass.ds(g * G, G)], m.base_col[:, bass.ds(v, 1)], None,
                                ALU.subtract).then_inc(rel_ready, 1)

            def one_hots(v, u, j):
                if j == 0:
                    dve.wait_ge(rel_ready, v + 1)
                V.tensor_tensor(hot[j % 2].rearrange("p (k n) -> p k n", k=2),
                                m.cols[:, :].rearrange("p (o n) -> p o n", o=1).broadcast_to([P, 2, NW]),
                                rel[:, u, 2 * j:2 * j + 2].rearrange("p (k o) -> p k o", o=1).broadcast_to([P, 2, NW]),
                                ALU.is_equal).then_inc(hot_ready, 1)

            def scale0(v, j, g):
                dve.wait_ge(hot_ready, v * 4 + (j + 1))
                for t in range(2):
                    ins = V.tensor_scalar(sel0[j % 2][:, t * NW:(t + 1) * NW], hot[j % 2][:, t * NW:(t + 1) * NW],
                                          m.sh[:, bass.ds(g * (4 * G) + 4 * (2 * j + t), 1)], None, ALU.mult)
                ins.then_inc(sel0_ready, 1)

            def add_window(v, u):
                base = load_base(dve, m, v)
                dve.wait_ge(pair_summed, v * 4 + (2 + 4))
                dve.wait_ge(added, v + 2)
                cols = m.nodes[:, :].rearrange("p (c n) -> p c n", c=5)[:, :, bass.ds(base, NW)]
                V.tensor_tensor(cols[:, 0:4, :], cols[:, 0:4, :], ps_sum[u][:, :, :], ALU.add)
                V.tensor_tensor(cols[:, 4, :], cols[:, 4, :], ps_sum4[u][:, :], ALU.add).then_inc(added, 1)

            V.memset(ps_sum[1][:], 0.0)
            V.memset(ps_sum4[1][:], 0.0).then_inc(added, 1)
            g = load_group(dve, m, 0)
            relative(0, 0, g)
            one_hots(0, 0, 0)
            scale0(0, 0, g)
            with dve.Fori(0, quads * 2) as half:
                for u in range(2):
                    v = half * 2 + u
                    g = load_group(dve, m, v)
                    for j in range(4):
                        messages(v, u, j)
                        dve.wait_ge(pair_summed, v * 4 + (j + 2))
                        if j < 3:
                            one_hots(v, u, j + 1)
                            if j == 0:
                                add_window(v - 1, 1 - u)
                            if j == 2:
                                g_next = load_group(dve, m, v + 1)
                                relative(v + 1, 1 - u, g_next)
                            scale0(v, j + 1, g)
                        else:
                            one_hots(v + 1, 1 - u, 0)
                            scale0(v + 1, 0, g_next)
            add_window(quads * 4 - 1, 1)


def conv_node_stage(nc, m):
    V = nc.vector
    with ExitStack() as ctx:
        def sem(name):
            return m.sems.enter_context(nc.semaphore("cn_" + name))

        def ps(name, cols):
            return ctx.enter_context(nc.psum_tensor("cn_" + name, [P, cols], F32))

        b = node_buffers(m, "l0out")
        pX = [ps(f"pX{u}", 512) for u in range(2)]
        pT = [ps(f"pT{u}", 512) for u in range(2)]
        pZ = [[ps(f"pZ{u}{t}", ZW) for t in range(2)] for u in range(2)]
        x_in = [sem(f"x_in{r}") for r in range(4)]
        y_in, s_parts, s_zero, pool_go, s_pX, s_x1, s_go, s_bn, s_mv, s_sd, s_rs, s_nm, s_h, s_pT, s_hT, s_pZ, s_rows = [
            sem(n) for n in ("y", "parts", "zeroed", "pool_go", "pX", "x1", "go", "bn", "mv", "sd", "rs", "nm", "h", "pT", "hT",
                             "pZ", "rows")]
        st_x1, st_hT, st_rows, st_parts = [[sem(f"st_{n}{u}") for u in range(2)] for n in ("x1", "hT", "rows", "parts")]
        cols = chunks(m.nodes[:, :], 5)
        block = ctx.enter_context(nc.Block())

        @block.sync
        def _(sp):
            def load(n, r):
                wait_slot(sp, s_x1, n)
                sp.dma_start(tile(b.x[r]), rows_of(m.x_skip, n)).then_inc(x_in[r], 16)

            def store_x1(n, r):
                u = r % 2
                sp.wait_ge(s_x1, n + 1)
                sp.dma_start(rows_of(m.x1_rows, n), tile(b.skip[u])).then_inc(st_x1[u], 16)

            def store_hT(n, r):
                u = r % 2
                sp.wait_ge(s_hT, n + 1)
                sp.dma_start(m.hT[0][bass.ds(n, 1), :, :].rearrange("o p n -> (o p) n"), b.hT[u]).then_inc(st_hT[u], 16)

            def store_rows(n, r):
                store_table(sp, m, b, 0, n, r % 2, s_rows, s_parts, st_rows, st_parts)

            for st in (st_x1, st_hT, st_rows, st_parts):
                for u in range(2):
                    sp.sem_inc(st[u], 16)
            in_order(sp, (-2, load), (0, store_x1), (2, store_hT), (3, store_rows))
            for st in (st_x1, st_hT, st_rows, st_parts):
                for u in range(2):
                    sp.wait_ge(st[u], NPB * 8 + 16)

        @block.gpsimd
        def _(pool):
            def zero_columns(n, r):
                pool.wait_ge(y_in, n + 1).then_inc(pool_go, 1)
                nc.gpsimd.tensor_copy(cols[:, 0:3, bass.ds(n * PB, PB)], zeros_of(b))

            def parts(n, r):
                er_in_parts(nc, pool, b, n, r % 2, s_rows, s_parts, st_parts, pool_go)

            nc.gpsimd.memset(b.zero, 0.0).then_inc(s_zero, 1)
            pool.wait_ge(s_zero, 1)
            in_order(pool, (-1, zero_columns), (3, parts))

        @block.tensor
        def _(pe):
            def outputs(n, r):
                u = r % 2
                y = chunks(b.y[u], 5)
                pe.wait_ge(y_in, n + 1)
                for t in range(2):
                    out = pX[u][:, t * D:(t + 1) * D].rearrange("p (b f) -> p b f", b=4)
                    for c in range(5):
                        blocks = [out[:, 0:2, :], out[:, 2:4, :], out[:, 0:2, :], out[:, 0:3:2, :],
                                  out[:, 0:4:3, :]][c]
                        ins = nc.tensor.matmul(blocks, y[:, c, t * P:(t + 1) * P], m.lin2[:, c, :],
                                               start=(t == 0 and c == 0), stop=(c == 4), skip_group_check=True)
                ins.then_inc(s_pX, 1)

            def transposes(n, r):
                u = r % 2
                h = tile(b.h[u])
                pe.wait_ge(s_h, n + 1)
                for c in range(2):
                    for t in range(2):
                        ins = nc.tensor.transpose(pT[u][:, c * PB + t * P:c * PB + (t + 1) * P],
                                                  h[:, t, c * P:(c + 1) * P], m.ident[:])
                ins.then_inc(s_pT, 1)

            def table(n, r):
                table_products(nc, pe, m, b, 0, n, r % 2, pZ, s_hT, s_rows, s_pZ)

            in_order(pe, (-1, outputs), (1, transposes), (2, table))

        @block.vector
        def _(dve):
            def fixed(n, r):
                wait_slot(dve, s_pX, n, 2)
                V.tensor_copy(chunks(b.y[r % 2], 5), cols[:, :, bass.ds(n * PB, PB)]).then_inc(y_in, 1)

            def state(n, r):
                u = r % 2
                x, x1 = tile(b.x[r]), tile(b.skip[u])
                dve.wait_ge(x_in[r], slot_loaded(n, r))
                dve.wait_ge(s_pX, n + 1)
                dve.wait_ge(st_x1[u], slot_stored(n, u))
                wait_slot(dve, s_h, n, 2)
                for t in range(2):
                    zc = m.nvec[:, bass.ds(n * 2 + t, 1)]
                    V.scalar_tensor_tensor(x1[:, t, 0:MUL], pX[u][:, t * D:t * D + MUL], zc, x[:, t, 0:MUL],
                                           ALU.mult, ALU.add)
                    ins = V.scalar_tensor_tensor(
                        x1[:, t, MUL:D].rearrange("p (v c) -> p v c", c=3),
                        pX[u][:, t * D + MUL:(t + 1) * D].rearrange("p (c v) -> p v c", c=3), zc,
                        x[:, t, MUL:D].rearrange("p (v c) -> p v c", c=3), ALU.mult, ALU.add)
                ins.then_inc(s_x1, 1)
                dve.wait_ge(s_x1, n + 1)
                moments(V, dve, b, u, n, x1, s_bn, s_mv, s_go)

            def scales(n, r):
                scale_and_shift(V, dve, b, r % 2, n, s_sd, s_rs, s_nm)

            in_order(dve, (1, scales), (-1, fixed), (0, state))

        @block.scalar
        def _(act):
            def sd(n, r):
                deviation(nc, act, m, b, r % 2, n, s_mv, s_sd)

            def hidden(n, r):
                u = r % 2
                act.wait_ge(s_nm, n + 1)
                for t in range(2):
                    ins = nc.scalar.activation(tile(b.h[u])[:, t, :], tile(b.skip[u])[:, t, :], ACT.Relu,
                                               bias=b.nm[u][:, t:t + 1], scale=b.rs[u][:, t:t + 1])
                ins.then_inc(s_h, 1)

            def copy_hT(n, r):
                u = r % 2
                act.wait_ge(s_pT, n + 1)
                act.wait_ge(st_hT[u], slot_stored(n, u))
                wait_slot(act, s_pZ, n, 2)
                nc.scalar.copy(b.hT[u], pT[u][:]).then_inc(s_hT, 1)

            def rows(n, r):
                table_rows(nc, act, b, n, r % 2, pZ, s_pZ, s_parts, st_rows, s_rows)

            in_order(act, (1, hidden), (0, sd), (2, copy_hT), (3, rows))


def table_products(nc, pe, m, b, layer, n, u, pZ, s_hT, s_rows, s_pZ):
    pe.wait_ge(s_hT, n + 1)
    wait_slot(pe, s_rows, n, 2)
    for t in range(2):
        for c in range(2):
            ins = nc.tensor.matmul(pZ[u][t][:, :], b.hT[u][:, c * PB + t * P:c * PB + (t + 1) * P], m.wz[layer][:, c, :],
                                   start=(c == 0), stop=(c == 1))
    ins.then_inc(s_pZ, 1)


def table_rows(nc, act, b, n, u, pZ, s_pZ, s_parts, st_rows, s_rows):
    act.wait_ge(s_pZ, n + 1)
    act.wait_ge(st_rows[u], slot_stored(n, u))
    if not isinstance(n, int) or n >= 2:
        act.wait_ge(s_parts, (n - 1) * 5)
    for t in range(2):
        ins = nc.scalar.copy(b.rows[u][:, t * ZW:(t + 1) * ZW], pZ[u][t][:, :])
    ins.then_inc(s_rows, 1)


def store_table(sp, m, b, layer, n, u, s_rows, s_parts, st_rows, st_parts):
    sp.wait_ge(s_rows, n + 1)
    sp.dma_start(rows_of(m.z_rows[layer], n), tile(b.rows[u], ZW)).then_inc(st_rows[u], 16)
    sp.wait_ge(s_parts, n * 5 + 5)
    sp.dma_start(rows_of(m.er_parts[layer], n), tile(b.parts[u], 12)).then_inc(st_parts[u], 16)


def zeros_of(b):
    return b.zero.rearrange("p (o n) -> p o n", o=1).broadcast_to([P, 3, PB])


def er_in_parts(nc, pool, b, n, u, s_rows, s_parts, st_parts, go):
    er = b.rows[u].rearrange("p (t w) -> p t w", t=2)[:, :, D + HEADS:ZW]
    parts = b.parts[u][:, 0:2 * 3 * HEADS].rearrange("p (t a h) -> p t a h", t=2, a=3)
    rest = b.rest[u].rearrange("p (t h) -> p t h", t=2)
    pool.wait_ge(s_rows, n + 1).then_inc(go, 1)
    pool.wait_ge(st_parts[u], slot_stored(n, u)).then_inc(go, 1)
    done = n * 5
    nc.gpsimd.tensor_copy(parts[:, :, 0, :], er).then_inc(s_parts, 1)
    for a in (1, 2):
        pool.wait_ge(s_parts, done + (2 * a - 1)).then_inc(go, 1)
        nc.gpsimd.tensor_tensor(rest, er if a == 1 else rest, parts[:, :, a - 1, :], ALU.subtract).then_inc(s_parts, 1)
        pool.wait_ge(s_parts, done + 2 * a).then_inc(go, 1)
        nc.gpsimd.tensor_copy(parts[:, :, a, :], rest).then_inc(s_parts, 1)


def gat_edge_stage(nc, m, layer):
    V = nc.vector
    BF = mybir.dt.bfloat16
    PARTS = 3
    ACT_TILES = 2
    SPLIT = (G - ACT_TILES) // 2
    with ExitStack() as ctx:
        def sem(name):
            return m.sems.enter_context(nc.semaphore(f"ge{layer}_" + name))

        def sb(name, shape, dt=F32):
            return ctx.enter_context(nc.sbuf_tensor(f"ge{layer}_" + name, shape, dt))

        def ps(name, shape):
            return ctx.enter_context(nc.psum_tensor(f"ge{layer}_" + name, shape, F32))

        free, free_scratch = [3 * NC], [0]

        def part(width, parts=P):
            a = m.nodes[0:parts, free[0]:free[0] + width]
            free[0] += width
            assert free[0] <= 5 * NC
            return a

        def scratch(width, parts=P):
            a = m.scratch[0:parts, free_scratch[0]:free_scratch[0] + width]
            free_scratch[0] += width
            assert free_scratch[0] <= SCRATCH
            return a

        zg = [part(G * ZW) for r in range(4)]
        sel = [part(G * NW) if r < 3 else scratch(G * NW) for r in range(4)]
        selT = part(GE // 2).bitcast(BF)
        zs = [scratch(G * D) for u in range(2)]
        seg = [scratch(GE + 2, HEADS) for u in range(2)]
        top = scratch(GE, HEADS)
        idx = part(4 * G).bitcast(I32).rearrange("p (r k) -> p r k", r=4)
        rel = part(2 * G).rearrange("p (u k) -> p u k", u=2)
        erw = sb("erw", [P, 2, PARTS * HEADS], BF)
        raw = part(G * HEADS)
        part_sum = part(G * HEADS)
        score = [part(G * HEADS) for u in range(2)]
        diff = [part(G * HEADS) for u in range(2)]
        ex = [part(G * HEADS) for u in range(2)]
        fd = [sb(f"fd{u}", [HEADS, 1]) for u in range(2)]
        fac = [sb(f"fac{u}", [HEADS, 1]) for u in range(2)]

        ps_eT = ps("eT", [HEADS, GE])
        ps_selT = ps("selT", [P, GE])
        ps_er = ps("er", [P, G * PARTS * HEADS])
        ps_max = ps("max", [P, G * HEADS])
        ps_sum = [ps(f"sum{u}", [P, 512]) for u in range(2)]
        FAC = 3 * NW

        er_in = [sem(f"er_in{u}") for u in range(2)]
        seg_in = [sem(f"seg_in{u}") for u in range(2)]
        got = [sem(f"gathered{r}") for r in range(4)]
        (sp_done, pe_go, low_ready, idx_ready, pool_go, rel_ready, sel_ready, selT_ps, selT_ready, er_ready, raw_ready,
         score_ready, eT_ready, fwd_ready, max_ready, carry_ready, maxT_ready, diff_ready, ex_ready, zs_ready,
         zs_act_ready, scaled, summed, added) = [
            sem(n) for n in ("sp_done", "pe_go", "low_ready", "idx_ready", "pool_go", "rel_ready", "sel_ready", "selT_ps",
                             "selT_ready", "er_ready", "raw_ready", "score_ready", "eT_ready", "fwd_ready", "max_ready",
                             "carry_ready", "maxT_ready", "diff_ready", "ex_ready", "zs_ready", "zs_act_ready", "scaled", "summed", "added")]
        block = ctx.enter_context(nc.Block())

        def per_head(a):
            return a.rearrange("p (k h) -> p k h", k=G)

        @block.sync
        def _(sp):
            quads = load_steps(sp, m)

            def load_er(v, u):
                base = load_base(sp, m, v)
                sp.dma_start(erw[:, u, :], m.er_parts[layer][bass.ds(base, NW), :]).then_inc(er_in[u], 16)

            def load_seg(v, u):
                g = load_group(sp, m, v)
                sp.dma_start(seg[u][:, 0:GE + 1],
                             m.same_seg[bass.ds(g * GE, GE + 1)].partition_broadcast(HEADS)).then_inc(seg_in[u], 16)

            for u in range(2):
                load_er(u, u)
                load_seg(u, u)
            with sp.Fori(0, quads) as quad:
                for r in range(4):
                    v = quad * 4 + r
                    sp.wait_ge(er_ready, v + 1)
                    load_er(v + 2, r % 2)
                    sp.wait_ge(carry_ready, v + 2)
                    load_seg(v + 2, r % 2)
            for u in range(2):
                sp.wait_ge(er_in[u], quads * 32 + 16)
                sp.wait_ge(seg_in[u], quads * 32 + 16).then_inc(sp_done, 1)

        @block.scalar
        def _(act):
            quads = load_steps(act, m)

            def stage_idx(v, r):
                g = load_group(act, m, v)
                nc.scalar.copy(idx[:, r, :], m.src[:, bass.ds(g * G, G)]).then_inc(idx_ready, 1)

            def copy_selT(v):
                act.wait_ge(selT_ps, v + 1)
                for k in range(2):
                    at = slice(k * GE // 2, (k + 1) * GE // 2)
                    nc.scalar.copy(selT[:, at], ps_selT[:, at]).then_inc(selT_ready, 1)

            for r in range(4):
                stage_idx(r, r)
            copy_selT(0)
            copy_selT(1)
            with act.Fori(0, quads) as quad:
                for r in range(4):
                    v = quad * 4 + r
                    u = r % 2
                    act.wait_ge(diff_ready, v + 1)
                    nc.scalar.activation(ex[u][:, :], diff[u][:, :], ACT.Exp).then_inc(ex_ready, 1)
                    nc.scalar.activation(fac[u][:, :], fd[u][:, :], ACT.Exp).then_inc(ex_ready, 1)
                    act.wait_ge(ex_ready, v * 2 + 2)
                    for k in range(G - ACT_TILES, G):
                        for h in range(HEADS):
                            ins = nc.scalar.activation(zs[u][:, k * D + h * HF:k * D + (h + 1) * HF],
                                                       zg[r][:, k * ZW + h * HF:k * ZW + (h + 1) * HF], ACT.Copy,
                                                       scale=ex[u][:, k * HEADS + h:k * HEADS + h + 1])
                    ins.then_inc(zs_act_ready, 1)
                    copy_selT(v + 2)
                    act.wait_ge(zs_ready, v * 2 + 2)
                    act.wait_ge(zs_act_ready, v + 1)
                    stage_idx(v + 4, r)

        @block.gpsimd
        def _(pool):
            quads = load_steps(pool, m)

            def gather(r):
                for k in range(G):
                    nc.gpsimd.indirect_dma_start(
                        zg[r][:, k * ZW:(k + 1) * ZW], None, m.z_rows[layer],
                        bass.IndirectOffsetOnAxis(ap=idx[:, r, k:k + 1], axis=0)).then_inc(got[r], 16)

            with pool.Fori(0, quads) as quad:
                for r in range(4):
                    pool.wait_ge(idx_ready, quad * 4 + (r + 1)).then_inc(pool_go, 1)
                    gather(r)
            pool.wait_ge(idx_ready, quads * 4 + 1).then_inc(pool_go, 1)
            gather(0)

        @block.tensor
        def _(pe):
            quads = load_steps(pe, m)

            def transpose_sel(v, r):
                pe.wait_ge(sel_ready, v + 1)
                for k in range(G):
                    ins = nc.tensor.transpose(ps_selT[:, k * P:(k + 1) * P], sel[r][:, k * P:(k + 1) * P], m.ident[:])
                ins.then_inc(selT_ps, 1)

            def spread_er(v, u, er_loads):
                pe.wait_ge(er_in[u], er_loads)
                W = PARTS * HEADS
                for k in range(G):
                    if k % (G // 2) == 0:
                        pe.wait_ge(selT_ready, v * 2 + (k // (G // 2) + 1))
                    ins = nc.tensor.matmul(ps_er[:, k * W:(k + 1) * W], selT[:, k * P:(k + 1) * P], erw[:, u, :],
                                           start=(k == 0), stop=(k == G - 1), skip_group_check=True)
                ins.then_inc(er_ready, 1)

            def transpose_scores(v, u):
                pe.wait_ge(score_ready, v + 1)
                for k in range(G):
                    ins = nc.tensor.transpose(ps_eT[:, k * P:(k + 1) * P], per_head(score[u][:, :])[:, k, :], m.ident[:])
                ins.then_inc(eT_ready, 1)

            transpose_sel(0, 0)
            spread_er(0, 0, 16)
            transpose_sel(1, 1)
            transpose_scores(0, 0)
            spread_er(1, 1, 16)
            with pe.Fori(0, quads) as quad:
                for r in range(4):
                    v = quad * 4 + r
                    u = r % 2
                    pe.wait_ge(max_ready, v + 1).then_inc(pe_go, 1)
                    for k in range(G):
                        ins = nc.tensor.transpose(ps_max[:, k * HEADS:(k + 1) * HEADS], top[:, k * P:(k + 1) * P],
                                                  m.ident[0:HEADS, 0:HEADS])
                    ins.then_inc(maxT_ready, 1)
                    transpose_scores(v + 1, 1 - u)
                    transpose_sel(v + 2, (r + 2) % 4)
                    pe.wait_ge(ex_ready, v * 2 + 2)
                    pe.wait_ge(added, v + 1)
                    for c in range(2):
                        nc.tensor.matmul(ps_sum[u][:, FAC + c:FAC + c + 1], m.headsel[:, c, :], fac[u][:, :],
                                         start=(c == 0), stop=True, skip_group_check=True)
                    for k in range(G):
                        if k == 0:
                            pe.wait_ge(zs_ready, v * 2 + 1)
                        if k == SPLIT:
                            pe.wait_ge(zs_ready, v * 2 + 2)
                        if k == G - ACT_TILES:
                            pe.wait_ge(zs_act_ready, v + 1)
                        s = sel[r][:, k * NW:(k + 1) * NW]
                        for c in range(2):
                            nc.tensor.matmul(ps_sum[u][:, c * NW:(c + 1) * NW],
                                             zs[u][:, k * D + c * P:k * D + (c + 1) * P], s,
                                             start=False, stop=(k == G - 1), skip_group_check=True)
                        ins = nc.tensor.matmul(ps_sum[u][0:HEADS, 2 * NW:3 * NW], per_head(ex[u][:, :])[:, k, :], s,
                                               start=False, stop=(k == G - 1), skip_group_check=True)
                    ins.then_inc(summed, 1)
                    spread_er(v + 2, u, quad * 32 + (r // 2 + 2) * 16)

        @block.vector
        def _(dve):
            quads = load_steps(dve, m)
            cols = m.nodes[:, 0:2 * NC].rearrange("p (c n) -> p c n", c=2)
            den = m.nodes[0:HEADS, 2 * NC:3 * NC]

            def relative(v, u):
                g = load_group(dve, m, v)
                V.tensor_scalar(rel[:, u, :], m.dst[:, bass.ds(g * G, G)], m.base_col[:, bass.ds(v, 1)], None,
                                ALU.subtract).then_inc(rel_ready, 1)

            def one_hots(v, r):
                dve.wait_ge(rel_ready, v + 1)
                V.tensor_tensor(sel[r].rearrange("p (k n) -> p k n", k=G),
                                m.cols[:, :].rearrange("p (o n) -> p o n", o=1).broadcast_to([P, G, NW]),
                                rel[:, r % 2, :].rearrange("p (k o) -> p k o", o=1).broadcast_to([P, G, NW]),
                                ALU.is_equal).then_inc(sel_ready, 1)

            def scores(v, r, gathered, between=None):
                dve.wait_ge(er_ready, v + 1)
                part_of = ps_er[:, :].rearrange("p (k a h) -> p k a h", k=G, a=PARTS)
                V.tensor_copy(per_head(part_sum[:, :]), part_of[:, :, 2, :]).then_inc(low_ready, 1)
                dve.wait_ge(low_ready, v * 3 + 1)
                for n, a in enumerate((1, 0)):
                    V.tensor_tensor(per_head(part_sum[:, :]), per_head(part_sum[:, :]), part_of[:, :, a, :], ALU.add
                                    ).then_inc(low_ready, 1)
                    dve.wait_ge(low_ready, v * 3 + (2 + n))
                dve.wait_ge(got[r], gathered)
                rows = zg[r].rearrange("p (k w) -> p k w", k=G)
                V.tensor_tensor(per_head(raw[:, :]), rows[:, :, D:D + HEADS], per_head(part_sum[:, :]), ALU.add
                                ).then_inc(raw_ready, 1)
                dve.wait_ge(raw_ready, v + 1)
                V.scalar_tensor_tensor(score[r % 2][:, :], raw[:, :], NEG_SLOPE, raw[:, :], ALU.mult, ALU.max
                                       ).then_inc(score_ready, 1)

            def scale_first(v, u):
                base = load_base(dve, m, v)
                dve.wait_ge(summed, v + 2)
                dve.wait_ge(added, v + 2)
                first = cols[:, :, bass.ds(base, 1)]
                V.tensor_tensor(first, first, ps_sum[u][:, FAC:FAC + 2].rearrange("p (c o) -> p c o", o=1), ALU.mult)
                V.tensor_scalar(den[:, bass.ds(base, 1)], den[:, bass.ds(base, 1)], fac[u][:, :], None,
                                ALU.mult).then_inc(scaled, 1)

            def add_window(v, u):
                base = load_base(dve, m, v)
                dve.wait_ge(scaled, v + 2)
                window = cols[:, :, bass.ds(base, NW)]
                V.tensor_tensor(window, window, ps_sum[u][:, 0:2 * NW].rearrange("p (c n) -> p c n", c=2), ALU.add)
                dwin = den[:, bass.ds(base, NW)]
                V.tensor_tensor(dwin, dwin, ps_sum[u][0:HEADS, 2 * NW:3 * NW], ALU.add).then_inc(added, 1)

            V.memset(fac[1][:, :], 1.0)
            V.memset(ps_sum[1][:], 0.0).then_inc(added, 1)
            V.memset(m.carry[:], LOW).then_inc(carry_ready, 1)
            dve.sem_inc(summed, 1)
            for u in range(2):
                relative(u, u)
                one_hots(u, u)
            scores(0, 0, 16 * G)
            with dve.Fori(0, quads) as quad:
                for r in range(4):
                    v = quad * 4 + r
                    u = r % 2
                    dve.wait_ge(eT_ready, v + 1)
                    dve.wait_ge(seg_in[u], quad * 32 + (r // 2 + 1) * 16)
                    dve.wait_ge(carry_ready, v + 1)
                    V.tensor_tensor_scan(top, seg[u][:, 0:GE], ps_eT[:, :], m.carry[:, u:u + 1], ALU.add, ALU.max
                                         ).then_inc(fwd_ready, 1)
                    dve.wait_ge(fwd_ready, v + 1)
                    V.tensor_tensor_scan(top[:, ::-1], seg[u][:, GE:0:-1], top[:, ::-1], LOW, ALU.add, ALU.max
                                         ).then_inc(max_ready, 1)
                    dve.wait_ge(max_ready, v + 1)
                    V.scalar_tensor_tensor(fd[u][:, :], m.carry[:, u:u + 1], seg[u][:, 0:1], top[:, 0:1],
                                           ALU.add, ALU.subtract)
                    V.tensor_copy(m.carry[:, 1 - u:2 - u], top[:, GE - 1:GE]).then_inc(carry_ready, 1)
                    relative(v + 2, u)
                    scores(v + 1, (r + 1) % 4, quad * 128 + (128 if r < 3 else 256))
                    one_hots(v + 2, (r + 2) % 4)
                    dve.wait_ge(maxT_ready, v + 1)
                    V.tensor_tensor(diff[u][:, :], score[u][:, :], ps_max[:, :], ALU.subtract).then_inc(diff_ready, 1)
                    scale_first(v - 1, 1 - u)
                    dve.wait_ge(ex_ready, v * 2 + 1)
                    out = zs[u].rearrange("p (k h f) -> p k h f", k=G, h=HEADS)
                    z = zg[r].rearrange("p (k w) -> p k w", k=G)[:, :, 0:D].rearrange("p k (h f) -> p k h f", h=HEADS)
                    weight = ex[u][:, :].rearrange("p (k h o) -> p k h o", k=G, o=1).broadcast_to([P, G, HEADS, HF])
                    for k in (slice(0, SPLIT), slice(SPLIT, G - ACT_TILES)):
                        V.tensor_tensor(out[:, k], z[:, k], weight[:, k], ALU.mult).then_inc(zs_ready, 1)
                    add_window(v - 1, 1 - u)
            last = quads * 4 - 1
            scale_first(last, 1)
            add_window(last, 1)


def gat_node_stage(nc, m, layer):
    V = nc.vector
    with ExitStack() as ctx:
        def sem(name):
            return m.sems.enter_context(nc.semaphore(f"gn{layer}_" + name))

        def ps(name, cols):
            return ctx.enter_context(nc.psum_tensor(f"gn{layer}_" + name, [P, cols], F32))

        b = node_buffers(m, "gat")
        pR = [ps(f"pR{u}", 512) for u in range(2)]
        pT = [ps(f"pT{u}", 512) for u in range(2)]
        pZ = [[ps(f"pZ{u}{t}", ZW) for t in range(2)] for u in range(2)]
        in_ = [sem(f"in{r}") for r in range(4)]
        s_max, s_den, s_pR, s_t, s_v, s_neg, s_ex, s_em, s_hT, s_pT, s_pZ, s_rows, s_parts, s_zero, pool_go = [
            sem(n) for n in ("max", "den", "pR", "t", "v", "neg", "ex", "em", "hT", "pT", "pZ", "rows", "parts", "zeroed", "pool_go")]
        st_hT, st_rows, st_parts = [[sem(f"st_{n}{u}") for u in range(2)] for n in ("hT", "rows", "parts")]
        stores = (st_hT, st_rows, st_parts) if layer == 0 else (st_rows,)
        block = ctx.enter_context(nc.Block())
        LOADS = 1 + layer

        @block.sync
        def _(sp):
            def load(n, r):
                wait_slot(sp, s_rows if layer else s_hT, n)
                sp.dma_start(b.x[r], m.hT[layer][bass.ds(n, 1), :, :].rearrange("o p n -> (o p) n")).then_inc(in_[r], 16)
                if layer == 1:
                    sp.dma_start(tile(b.skip[r]), rows_of(m.x1_rows, n)).then_inc(in_[r], 16)

            def store_hT(n, r):
                u = r % 2
                if layer == 0:
                    sp.wait_ge(s_hT, n + 1)
                    sp.dma_start(m.hT[1][bass.ds(n, 1), :, :].rearrange("o p n -> (o p) n"), b.hT[u]).then_inc(st_hT[u], 16)

            def store_rows(n, r):
                u = r % 2
                if layer == 0:
                    store_table(sp, m, b, 1, n, u, s_rows, s_parts, st_rows, st_parts)
                else:
                    sp.wait_ge(s_rows, n + 1)
                    sp.dma_start(rows_of(m.io["out"], n), tile(b.rows[u])).then_inc(st_rows[u], 16)

            for st in stores:
                for u in range(2):
                    sp.sem_inc(st[u], 16)
            in_order(sp, (-2, load), (1, store_hT), (2, store_rows))
            for st in stores:
                for u in range(2):
                    sp.wait_ge(st[u], NPB * 8 + 16)

        @block.gpsimd
        def _(pool):
            cols = chunks(m.nodes[:, 0:3 * NC], 3)

            def zero_columns(n, r):
                pool.wait_ge(s_t, n + 1).then_inc(pool_go, 1)
                nc.gpsimd.tensor_copy(cols[:, :, bass.ds(n * PB, PB)], zeros_of(b))

            def parts(n, r):
                er_in_parts(nc, pool, b, n, r % 2, s_rows, s_parts, st_parts, pool_go)

            if layer == 0:
                nc.gpsimd.memset(b.zero, 0.0).then_inc(s_zero, 1)
                pool.wait_ge(s_zero, 1)
                in_order(pool, (0, zero_columns), (2, parts))

        @block.tensor
        def _(pe):
            def spread(n, r):
                u = r % 2
                pe.wait_ge(s_den, n + 1)
                wait_slot(pe, s_t, n, 2)
                for c in range(2):
                    ins = nc.tensor.matmul(pR[u][:, c * PB:(c + 1) * PB], m.headsel[:, c, :], b.den[u],
                                           start=(c == 0), stop=True, skip_group_check=True)
                ins.then_inc(s_pR, 1)

            def table(n, r):
                table_products(nc, pe, m, b, 1, n, r % 2, pZ, s_hT, s_rows, s_pZ)

            def to_rows(n, r):
                u = r % 2
                pe.wait_ge(s_hT, n + 1)
                wait_slot(pe, s_rows, n, 2)
                for t in range(2):
                    for c in range(2):
                        ins = nc.tensor.transpose(pT[u][:, t * D + c * P:t * D + (c + 1) * P],
                                                  b.hT[u][:, c * PB + t * P:c * PB + (t + 1) * P], m.ident[:])
                ins.then_inc(s_pT, 1)

            in_order(pe, (-1, spread), (1, to_rows if layer else table))

        @block.vector
        def _(dve):
            cols = chunks(m.nodes[:, 0:2 * NC])
            den = m.nodes[0:HEADS, 2 * NC:3 * NC]

            def denominators(n, r):
                u = r % 2
                wait_slot(dve, s_pR, n, 2)
                V.tensor_scalar(b.den[u], den[:, bass.ds(n * PB, PB)], 1e-30, None, ALU.max).then_inc(s_max, 1)
                dve.wait_ge(s_max, n + 1)
                V.reciprocal(b.den[u], b.den[u]).then_inc(s_den, 1)

            def state(n, r):
                u = r % 2
                x, t = chunks(b.x[r]), chunks(b.h[u])
                dve.wait_ge(in_[r], slot_loaded(n, r) * LOADS)
                dve.wait_ge(s_pR, n + 1)
                wait_slot(dve, s_hT, n, 2)
                V.tensor_tensor(t, cols[:, :, bass.ds(n * PB, PB)], chunks(pR[u][:, :]), ALU.mult).then_inc(s_t, 1)
                dve.wait_ge(s_t, n + 1)
                for c in range(2):
                    ins = V.scalar_tensor_tensor(x[:, c, :], x[:, c, :], m.bias[layer][:, c:c + 1], t[:, c, :],
                                                 ALU.add, ALU.add)
                ins.then_inc(s_v, 1)

            def elu(n, r):
                u = r % 2
                dve.wait_ge(s_em, n + 1)
                if layer == 0:
                    dve.wait_ge(st_hT[u], slot_stored(n, u))
                    wait_slot(dve, s_pZ, n, 2)
                else:
                    wait_slot(dve, s_pT, n, 2)
                V.scalar_tensor_tensor(b.hT[u], b.x[r], 0.0, b.h[u], ALU.max, ALU.add).then_inc(s_hT, 1)

            def output(n, r):
                u = r % 2
                dve.wait_ge(s_pT, n + 1)
                dve.wait_ge(st_rows[u], slot_stored(n, u))
                V.tensor_tensor(b.rows[u][:, 0:2 * D], pT[u][:, :], b.skip[r], ALU.add).then_inc(s_rows, 1)

            if layer == 0:
                in_order(dve, (-1, denominators), (0, state), (1, elu))
            else:
                in_order(dve, (-1, denominators), (0, state), (1, elu), (2, output))

        @block.scalar
        def _(act):
            def exponential(n, r):
                h = b.h[r % 2]
                act.wait_ge(s_v, n + 1)
                nc.scalar.activation(h, b.x[r], ACT.Relu, scale=-1.0).then_inc(s_neg, 1)
                act.wait_ge(s_neg, n + 1)
                nc.scalar.activation(h, h, ACT.Exp, scale=-1.0).then_inc(s_ex, 1)
                act.wait_ge(s_ex, n + 1)
                nc.scalar.activation(h, h, ACT.Copy, bias=-1.0).then_inc(s_em, 1)

            def rows(n, r):
                table_rows(nc, act, b, n, r % 2, pZ, s_pZ, s_parts, st_rows, s_rows)

            if layer == 0:
                in_order(act, (0, exponential), (2, rows))
            else:
                in_order(act, (0, exponential))


def build(nc, io):
    with ExitStack() as ctx:
        m = allocate(nc, ctx, io)
        setup_stage(nc, m)
        input_stage(nc, m)
        conv_edge_stage(nc, m)
        conv_node_stage(nc, m)
        for layer in range(2):
            with nc.cleanup_on_exit():
                m.sems = ExitStack()
                gat_edge_stage(nc, m, layer)
                gat_node_stage(nc, m, layer)


def kernel(**inputs):
    import numpy as np
    import concourse.bacc as bacc
    from concourse.bass_utils import run_bass_kernel_spmd as run

    a = {k: np.ascontiguousarray(v) for k, v in inputs.items()}

    def padded(rows, n, fill=0):
        out = np.full((n,) + rows.shape[1:], fill, rows.dtype)
        out[:rows.shape[0]] = rows
        return out

    dst = padded(a["dst"], EP, N)
    line = np.full((NG + 1) * GE + 1, N, dst.dtype)
    line[0] = -1
    line[1:1 + EP] = dst
    arrays = {
        "x": padded(a["x"], NC),
        "nvec_t": np.ascontiguousarray(padded(a["node_vec1"], NC).reshape(NT, P).T),
        "src_t": np.ascontiguousarray(padded(a["src"], EP).reshape(NTILES, P).T),
        "dst_t": np.ascontiguousarray(dst.reshape(NTILES, P).T),
        "dst_line": line,
        "dst_ends": np.concatenate([dst[0::GE], dst[GE - 1::GE]]).reshape(1, 2 * NG),
        "sh_t": np.ascontiguousarray(padded(a["edge_attr_4"], EP).reshape(NTILES, P, 4).transpose(1, 0, 2)).reshape(P, 4 * NTILES),
        "ea8_t": np.ascontiguousarray(padded(a["edge_attr_8"], EP).reshape(NG, 2, GE // 2, NBAS).transpose(0, 1, 3, 2)).reshape(NG * 2 * NBAS, GE // 2),
    }
    for name in ("W_sc0", "W_sc1", "W_lin1_0", "W_lin1_1", "fc_w0", "fc_w1", "W_lin2_0", "W_lin2_1"):
        arrays[name] = a["L0_gnn_" + name]
    for l in range(2):
        arrays[f"W{l}"] = a[f"L1_gnn_W{l}"]
        arrays[f"al{l}"] = a[f"L1_gnn_al{l}"].reshape(D)
        arrays[f"ar{l}"] = a[f"L1_gnn_ar{l}"].reshape(D)
        arrays[f"b{l}_t"] = np.ascontiguousarray(a[f"L1_gnn_b{l}"].reshape(2, P).T)

    nc = bacc.Bacc("TRN2", target_bir_lowering=False, num_devices=1)
    io = {k: nc.dram_tensor(k, v.shape, mybir.dt.from_np(v.dtype), kind="ExternalInput").ap() for k, v in arrays.items()}
    io["out"] = nc.dram_tensor("out", (NC, D), F32, kind="ExternalOutput").ap()
    build(nc, io)
    r = run(nc, [arrays], core_ids=[0])
    return r.results[0]["out"][:N]
```

```python
from contextlib import ExitStack

import concourse.bass as bass
from concourse import mybir

F32 = mybir.dt.float32
I32 = mybir.dt.int32
ACT = mybir.ActivationFunctionType
ALU = mybir.AluOpType
AX = mybir.AxisListType

P = 128
N = 6250
E = 106250
D = 256
MUL = 64
HEADS = 4
HF = D // HEADS
NBAS = 8
RN = 64
G = 8
GE = G * P
NG = -(-E // GE)
NTILES = NG * G
EP = NG * GE
NW = 128
PB = 2 * P
NPB = 2 * -(-(N + NW) // (2 * PB))
NC = NPB * PB
NT = NC // P
SPARE = NC - NW
QV = 2
VP = -(-(NG + NC // NW + 12) // QV)
VT = QV * VP
MIN_QUADS, MAX_QUADS = -(-NG // 4), -(-(NG + N // NW) // 4)
FLAG_COLS = (NG + 1) * GE // P
SCRATCH = 10240 + 256
ZW = D + 2 * HEADS
LOW = -1.0e38
EPS = 1e-5
INV_M = MUL ** -0.5
C_S = 0.3826834261417389
C_X = 0.9238795042037964
OUT_SCALE = C_X * (2 * MUL) ** -0.5 / 4.0 * RN ** -0.5
INV_SQRT3 = 3.0 ** -0.5
NEG_SLOPE = 0.2


class Mem:
    pass


def allocate(nc, ctx, io):
    m = Mem()
    m.io = io
    m.sems = ctx

    def sb(name, shape, dt=F32):
        return ctx.enter_context(nc.sbuf_tensor(name, shape, dt))

    def dram(name, shape, dt=F32):
        return nc.dram_tensor(name, shape, dt, kind="Internal").ap()

    m.h_rows = dram("h_rows", (NC, D))
    m.x_skip = dram("x_skip", (NC, D))
    m.x1_rows = dram("x1_rows", (NC, D))
    m.hT = [dram(f"hT{l}", (NPB, P, 2 * PB)) for l in range(2)]
    m.z_rows = [dram(f"z_rows{l}", (NC, ZW)) for l in range(2)]
    m.den_rows = dram("den_rows", (HEADS, NC))
    m.er_parts = [dram(f"er_parts{l}", (NC, 12), mybir.dt.bfloat16) for l in range(2)]
    m.same_seg = dram("same_seg", ((NG + 1) * GE,))
    m.steps_i = dram("steps_i", (2, VT), I32)
    m.steps_f = dram("steps_f", (1, VT))

    m.nodes = sb("nodes", [P, 5 * NC])
    m.scratch = sb("scratch", [P, SCRATCH])
    m.src = sb("src_sb", [P, NTILES], I32)
    m.dst = sb("dst_sb", [P, NTILES], I32)
    m.sh = sb("sh_sb", [P, NTILES * 4])
    m.base_col = sb("base_col", [P, VT])
    m.tab = sb("tab", [1, 2 * VT + 1], I32)
    m.nsteps = sb("nsteps", [1, 2], I32)
    m.nvec = sb("nvec", [P, 3 * NT])
    m.ident = sb("ident", [P, P])
    m.cols = sb("cols", [P, NW])
    m.fc0 = sb("fc0_sb", [2 * NBAS, P])
    m.fc1 = sb("fc1_sb", [P, 4 * MUL])
    m.lin1 = sb("lin1_sb", [P, 2, 4 * MUL])
    m.lin2 = sb("lin2_sb", [P, 4, P])
    m.wz = [sb(f"wz{l}", [P, 2, ZW]) for l in range(2)]
    m.bias = [sb(f"bias{l}", [P, 2]) for l in range(2)]
    m.headsel = sb("headsel", [HEADS, 2, P])
    m.eps = sb("eps", [P, 1])
    m.carry = sb("carry", [HEADS, 2])
    return m


def table_group(m, v):
    return m.tab[0:1, bass.ds(v, 1)]


def table_base(m, v):
    return m.tab[0:1, bass.ds(v + (VT + 1), 1)]


def load_group(eng, m, v):
    return eng.value_load(table_group(m, v), min_val=0, max_val=NG - 1)


def load_base(eng, m, v):
    return eng.value_load(table_base(m, v), min_val=0, max_val=SPARE)


def load_steps(eng, m):
    return eng.value_load(m.nsteps[0:1, 0:1], min_val=MIN_QUADS, max_val=MAX_QUADS)


def setup_stage(nc, m):
    io = m.io
    with ExitStack() as ctx:
        def sb(name, shape, dt=F32):
            return ctx.enter_context(nc.sbuf_tensor(name, shape, dt))

        def sem(name):
            return m.sems.enter_context(nc.semaphore(name))

        free = [0]

        def part(parts, width, dt=F32):
            a = m.scratch[0:parts, free[0]:free[0] + width]
            free[0] += width
            return a if dt == F32 else a.bitcast(dt)

        ends = part(1, 2 * NG, I32)
        span = part(1, NG, I32)
        span7 = part(1, NG, I32)
        wins = part(1, NG)
        ones_row = part(1, NG)
        incl = part(1, NG)
        rows2 = part(1, 2 * NG)
        total = part(1, 1, I32)
        ones_lhs = part(1, VP)
        vcol = part(VP, QV)
        gcols = part(VP, NG)
        hit = part(VP, QV * NG)
        step = part(VP, QV * 6)
        step_i = part(VP, QV * 2, I32)
        dst_a = part(P, FLAG_COLS, I32)
        dst_b = part(P, FLAG_COLS, I32)
        differ = part(P, FLAG_COLS)
        att = part(P, 4 * D)
        att_w = part(P, 2 * D)
        ps_rows = ctx.enter_context(nc.psum_tensor("ps_rows", [VP, 2 * NG], F32))

        s_ends = sem("su_ends")
        s_edges = sem("su_edges")
        s_dstrows = sem("su_dstrows")
        s_w = sem("su_weights")
        s_zero = sem("su_zeroed")
        s_pool = sem("su_pool")
        s_dve = sem("su_dve")
        s_bc = sem("su_rows_broadcast")
        s_tab = sem("su_table_stored")
        s_tabback = sem("su_table_loaded")
        s_flags = sem("su_flags_stored")

        loads = [0]
        block = ctx.enter_context(nc.Block())

        @block.sync
        def _(sp):
            sp.dma_start(ends, io["dst_ends"]).then_inc(s_ends, 16)
            sp.dma_start(dst_a, io["dst_line"][0:(NG + 1) * GE].rearrange("(p j) -> p j", p=P)).then_inc(s_dstrows, 16)
            sp.dma_start(dst_b, io["dst_line"][1:(NG + 1) * GE + 1].rearrange("(p j) -> p j", p=P)).then_inc(s_dstrows, 16)
            sp.dma_start(m.src[:, :], io["src_t"]).then_inc(s_edges, 16)
            sp.dma_start(m.dst[:, :], io["dst_t"]).then_inc(s_edges, 16)
            sp.dma_start(m.sh[:, :], io["sh_t"]).then_inc(s_edges, 16)
            sp.wait_ge(s_zero, 1)
            todo = [(m.nvec[:, 0:NT], io["nvec_t"]),
                    (m.fc0[0:NBAS, 0:RN], io["fc_w0"]), (m.fc0[NBAS:2 * NBAS, RN:2 * RN], io["fc_w0"]),
                    (m.fc1[0:RN, :], io["fc_w1"]), (m.fc1[RN:2 * RN, :], io["fc_w1"])]
            for c in range(2):
                for half in range(2):
                    rows = slice(half * MUL, half * MUL + MUL)
                    at = half * MUL
                    scalar_part = c == 0 and half == 0
                    todo.append((m.lin1[rows, c, at:at + MUL], io["W_lin1_0" if scalar_part else "W_lin1_1"]))
                    todo.append((m.lin1[rows, c, 2 * MUL + at:2 * MUL + at + MUL],
                                 io["W_sc0" if scalar_part else "W_sc1"]))
            lo, hi = slice(0, MUL), slice(MUL, 2 * MUL)
            todo += [(m.lin2[lo, 0, lo], io["W_lin2_0"][lo, :]), (m.lin2[hi, 0, hi], io["W_lin2_1"][hi, :]),
                     (m.lin2[lo, 1, lo], io["W_lin2_1"][hi, :]), (m.lin2[hi, 1, hi], io["W_lin2_1"][hi, :])]
            todo += [(m.lin2[lo, 2, lo], io["W_lin2_0"][hi, :]), (m.lin2[hi, 2, hi], io["W_lin2_1"][lo, :]),
                     (m.lin2[lo, 3, lo], io["W_lin2_1"][lo, :]), (m.lin2[hi, 3, hi], io["W_lin2_1"][lo, :])]
            for l in range(2):
                todo.append((m.wz[l][:, :, 0:D], io[f"W{l}"].rearrange("(c p) n -> p c n", p=P)))
                todo.append((m.bias[l][:, :], io[f"b{l}_t"]))
                todo.append((att[:, (2 * l) * D:(2 * l + 1) * D], io[f"al{l}"].partition_broadcast(P)))
                todo.append((att[:, (2 * l + 1) * D:(2 * l + 2) * D], io[f"ar{l}"].partition_broadcast(P)))
            for dst, src in todo:
                sp.dma_start(dst, src).then_inc(s_w, 16)
            loads[0] = len(todo)
            sp.wait_ge(s_dve, FLAGS_DONE)
            sp.dma_start(m.same_seg.rearrange("(p j) -> p j", p=P), differ).then_inc(s_flags, 16)
            sp.wait_ge(s_dve, TABLE_DONE)
            for q in range(QV):
                at = slice(q * VP, (q + 1) * VP)
                for k in range(2):
                    sp.dma_start(m.steps_i[k:k + 1, at].rearrange("o v -> v o"),
                                 step_i[:, 2 * q + k:2 * q + k + 1]).then_inc(s_tab, 16)
                sp.dma_start(m.steps_f[0:1, at].rearrange("o v -> v o"),
                             step[:, 6 * q + 5:6 * q + 6]).then_inc(s_tab, 16)
            sp.wait_ge(s_tab, 3 * QV * 16)
            sp.dma_start(m.tab[:, 0:VT], m.steps_i[0:1, :]).then_inc(s_tabback, 16)
            sp.dma_start(m.tab[:, VT + 1:2 * VT + 1], m.steps_i[1:2, :]).then_inc(s_tabback, 16)
            sp.dma_start(m.base_col[:, :], m.steps_f[0, :].partition_broadcast(P)).then_inc(s_tabback, 16)
            sp.wait_ge(s_tabback, 48)
            sp.wait_ge(s_flags, 16)
            sp.wait_ge(s_edges, 48)

        @block.gpsimd
        def _(pool):
            nc.gpsimd.memset(m.ident[:], 0.0)
            nc.gpsimd.memset(m.headsel[:], 0.0).then_inc(s_pool, 1)
            pool.wait_ge(s_pool, 1)
            nc.gpsimd.affine_select(out=m.ident[:], in_=m.ident[:], compare_op=ALU.not_equal, fill=1.0, base=0,
                                    pattern=[[-1, P]], channel_multiplier=1)
            sel = m.headsel[:, :, :].rearrange("h c (a f) -> h (c a) f", a=2)
            nc.gpsimd.affine_select(out=sel, in_=sel, compare_op=ALU.not_equal, fill=1.0, base=0,
                                    pattern=[[-1, HEADS], [0, HF]], channel_multiplier=1)
            nc.gpsimd.iota(m.cols[:], [[1, NW]], base=0, channel_multiplier=0, allow_small_or_imprecise_dtypes=True)
            nc.gpsimd.iota(gcols, [[1, NG]], base=0, channel_multiplier=0, allow_small_or_imprecise_dtypes=True)
            nc.gpsimd.iota(vcol, [[VP, QV]], base=0, channel_multiplier=1,
                           allow_small_or_imprecise_dtypes=True).then_inc(s_pool, 1)

        @block.tensor
        def _(pe):
            pe.wait_ge(s_dve, ROWS_DONE)
            nc.tensor.matmul(ps_rows[:, :], ones_lhs, rows2, start=True, stop=True).then_inc(s_bc, 1)

        marks = {}

        @block.vector
        def _(dve):
            count = [0]

            def done(ins):
                count[0] += 1
                ins.then_inc(s_dve, 1)
                dve.wait_ge(s_dve, count[0])

            V = nc.vector
            V.memset(m.fc0[:], 0.0)
            V.memset(m.lin1[:], 0.0)
            V.memset(m.lin2[:], 0.0).then_inc(s_zero, 1)
            V.memset(m.eps[:], EPS)
            V.memset(m.carry[:], LOW)
            V.memset(m.tab[:, VT:VT + 1], SPARE)
            V.memset(ones_lhs, 1.0)
            done(V.memset(ones_row, 1.0))
            dve.wait_ge(s_ends, 16)
            done(V.tensor_tensor(span, ends[:, NG:2 * NG], ends[:, 0:NG], ALU.subtract))
            done(V.tensor_scalar(span7, span, NW.bit_length() - 1, None, ALU.arith_shift_right))
            done(V.tensor_scalar(wins, span7, 1.0, None, ALU.add))
            done(V.tensor_tensor_scan(incl, ones_row, wins, 0.0, ALU.mult, ALU.add))
            done(V.tensor_tensor(rows2[:, 0:NG], incl, wins, ALU.subtract))
            done(V.scalar_tensor_tensor(rows2[:, NG:2 * NG], rows2[:, 0:NG], -float(NW), ends[:, 0:NG],
                                        ALU.mult, ALU.add))
            marks["rows"] = count[0]
            done(V.tensor_copy(total, incl[:, NG - 1:NG]))
            done(V.tensor_scalar(total, total, 3.0, None, ALU.add))
            V.tensor_scalar(m.nsteps[:, 0:1], total, 2, None, ALU.arith_shift_right)
            dve.wait_ge(s_pool, 2)
            dve.wait_ge(s_bc, 1)
            for q in range(QV):
                h = hit[:, q * NG:(q + 1) * NG]
                c = step[:, 6 * q:6 * q + 6]
                done(V.tensor_scalar(h, ps_rows[:, 0:NG], vcol[:, q:q + 1], None, ALU.is_le))
                done(V.tensor_reduce(c[:, 0:1], h, AX.X, ALU.add))
                done(V.tensor_scalar(c[:, 1:2], c[:, 0:1], -1.0, None, ALU.add))
                done(V.scalar_tensor_tensor(h, gcols, c[:, 1:2], ps_rows[:, NG:2 * NG], ALU.is_equal, ALU.mult))
                done(V.tensor_reduce(c[:, 2:3], h, AX.X, ALU.add))
                done(V.scalar_tensor_tensor(c[:, 3:4], vcol[:, q:q + 1], float(NW), c[:, 2:3], ALU.mult, ALU.add))
                done(V.tensor_scalar(c[:, 5:6], c[:, 3:4], float(SPARE), None, ALU.min))
                V.tensor_copy(step_i[:, 2 * q:2 * q + 1], c[:, 1:2])
                done(V.tensor_copy(step_i[:, 2 * q + 1:2 * q + 2], c[:, 5:6]))
            marks["table"] = count[0]
            dve.wait_ge(s_dstrows, 32)
            done(V.tensor_tensor(differ, dst_a, dst_b, ALU.not_equal))
            done(V.tensor_scalar(differ, differ, LOW, None, ALU.mult))
            marks["flags"] = count[0]
            assert (marks["rows"], marks["table"], marks["flags"]) == (ROWS_DONE, TABLE_DONE, FLAGS_DONE), marks
            dve.wait_ge(s_w, 16 * SETUP_LOADS)
            V.tensor_scalar(m.nvec[:, NT:2 * NT], m.nvec[:, 0:NT], INV_M, None, ALU.mult)
            V.tensor_scalar(m.nvec[:, 2 * NT:3 * NT], m.nvec[:, 0:NT], C_S * INV_M, None, ALU.mult)
            done(V.tensor_scalar(m.lin2[:], m.lin2[:], OUT_SCALE, None, ALU.mult))
            V.tensor_scalar(m.lin2[0:MUL, 2, 0:MUL], m.lin2[0:MUL, 2, 0:MUL], INV_SQRT3, None, ALU.mult)
            for l in range(2):
                for k in range(2):
                    a = att[:, (2 * l + k) * D:(2 * l + k + 1) * D].rearrange("p (o d) -> p o d", o=1)
                    w = att_w.rearrange("p (c d) -> p c d", c=2)
                    done(V.tensor_tensor(w, m.wz[l][:, :, 0:D], a.broadcast_to([P, 2, D]), ALU.mult))
                    done(V.tensor_reduce(m.wz[l][:, :, D + k * HEADS:D + (k + 1) * HEADS],
                                         att_w.rearrange("p (c h f) -> p c h f", c=2, h=HEADS), AX.X, ALU.add))

        assert loads[0] == SETUP_LOADS, loads


ROWS_DONE = 7
TABLE_DONE = ROWS_DONE + 2 + QV * 8
FLAGS_DONE = TABLE_DONE + 2
SETUP_LOADS = 5 + 8 + 4 + 4 + 8


QUADS = (NPB - 3) // 4 - 1


def in_order(eng, *parts):
    def one_pass(t, r):
        for lag, part in parts:
            if not isinstance(t, int) or 0 <= t - lag < NPB:
                part(t - lag, (r - lag) % 4)

    for t in range(-3, 4):
        one_pass(t, t % 4)
    with eng.Fori(0, QUADS) as quad:
        for r in range(4):
            one_pass(quad * 4 + (4 + r), r)
    for t in range(4 + 4 * QUADS, NPB + 3):
        one_pass(t, t % 4)


def wait_slot(eng, used, n, slots=4):
    if not isinstance(n, int) or n >= slots:
        eng.wait_ge(used, n - (slots - 1))


def slot_loaded(n, r):
    return (n - r) * 4 + 16


def slot_stored(n, u):
    return (n - u) * 8 + 16


def rows_of(t, n):
    return t[bass.ds(n * PB, PB), :].rearrange("(t p) d -> p t d", p=P)


def tile(a, w=D):
    return a[:, 0:2 * w].rearrange("p (t d) -> p t d", t=2)


def chunks(a, c=2):
    return a.rearrange("p (c n) -> p c n", c=c)


def node_buffers(m, tag):
    b = Mem()
    free = [0]

    def part(width, slots=2):
        a = [m.scratch[:, free[0] + u * width:free[0] + (u + 1) * width] for u in range(slots)]
        free[0] += slots * width
        assert free[0] <= SCRATCH
        return a

    b.x = part(2 * D, 4)
    b.skip = part(2 * D, 2 if tag == "l0out" else 4)
    b.h = part(2 * D)
    b.hT = part(2 * PB)
    b.rows = part(2 * ZW)
    b.y = part(4 * PB) if tag == "l0out" else None
    b.parts = [a.bitcast(mybir.dt.bfloat16) for a in part(12)]
    b.rest = part(2 * HEADS)
    b.zero = part(PB, 1)[0]
    b.den = [a[0:HEADS, :] for a in part(PB, 4)]
    b.all_den = part(PB, 1)[0][0:HEADS * NPB, :]
    b.stat = part(12)
    b.mv = part(4)
    b.sd = part(2)
    b.rs = part(2)
    b.nm = part(2)
    return b


def moments(V, dve, b, u, n, x, s_bn, s_mv, s_go):
    for t in range(2):
        ins = V.bn_stats(b.stat[u][:, 6 * t:6 * t + 6], x[:, t, :])
    ins.then_inc(s_bn, 1)
    dve.wait_ge(s_bn, n + 1).then_inc(s_go, 1)
    for t in range(2):
        ins = V.bn_aggr(b.mv[u][:, 2 * t:2 * t + 2], b.stat[u][:, 6 * t:6 * t + 6])
    ins.then_inc(s_mv, 1)


def deviation(nc, act, m, b, u, n, s_mv, s_sd):
    act.wait_ge(s_mv, n + 1)
    var = b.mv[u].rearrange("p (t k) -> p t k", k=2)[:, :, 1]
    nc.scalar.activation(b.sd[u], var, ACT.Sqrt, bias=m.eps[:, 0:1]).then_inc(s_sd, 1)


def scale_and_shift(V, dve, b, u, n, s_sd, s_rs, s_nm):
    dve.wait_ge(s_sd, n + 1)
    V.reciprocal(b.rs[u], b.sd[u]).then_inc(s_rs, 1)
    dve.wait_ge(s_rs, n + 1)
    mean = b.mv[u].rearrange("p (t k) -> p t k", k=2)[:, :, 0]
    V.scalar_tensor_tensor(b.nm[u], mean, -1.0, b.rs[u], ALU.mult, ALU.mult).then_inc(s_nm, 1)


def input_stage(nc, m):
    V = nc.vector
    with ExitStack() as ctx:
        def sem(name):
            return m.sems.enter_context(nc.semaphore("in_" + name))

        def ps(name, cols):
            return ctx.enter_context(nc.psum_tensor("in_" + name, [P, cols], F32))

        b = node_buffers(m, "in")
        pT = [ps(f"pT{u}", 512) for u in range(2)]
        pO = [[ps(f"pO{u}{t}", 512) for t in range(2)] for u in range(2)]
        x_in = [sem(f"x_in{r}") for r in range(4)]
        s_go, s_bn, s_mv, s_sd, s_rs, s_nm, s_h, s_pT, s_hT, s_pO, s_rows, s_skip = [
            sem(n) for n in ("go", "bn", "mv", "sd", "rs", "nm", "h", "pT", "hT", "pO", "rows", "skip")]
        st_rows = [sem(f"strows{u}") for u in range(2)]
        st_skip = [sem(f"stskip{r}") for r in range(4)]
        skip_in = [sem(f"skip_in{r}") for r in range(4)]
        block = ctx.enter_context(nc.Block())

        @block.sync
        def _(sp):
            def load(n, r):
                wait_slot(sp, s_h, n)
                sp.dma_start(tile(b.x[r]), rows_of(m.io["x"], n)).then_inc(x_in[r], 16)

            def load_skip(n, r):
                sp.wait_ge(st_skip[r], slot_loaded(n, r))
                sp.dma_start(tile(b.skip[r]), rows_of(m.io["x"], n)).then_inc(skip_in[r], 16)

            def store(n, r):
                u = r % 2
                sp.wait_ge(s_rows, n + 1)
                sp.dma_start(rows_of(m.h_rows, n), tile(b.rows[u])).then_inc(st_rows[u], 16)
                sp.wait_ge(s_skip, n + 1)
                sp.dma_start(rows_of(m.x_skip, n), tile(b.skip[r])).then_inc(st_skip[r], 16)

            for st in st_rows + st_skip:
                sp.sem_inc(st, 16)
            in_order(sp, (-3, load), (0, load_skip), (2, store))
            for u in range(2):
                sp.wait_ge(st_rows[u], NPB * 8 + 16)
            for r in range(4):
                sp.wait_ge(st_skip[r], 16 * len(range(r, NPB, 4)) + 16)

        @block.gpsimd
        def _(pool):
            nc.gpsimd.memset(m.nodes[:], 0.0)

        @block.vector
        def _(dve):
            def statistics(n, r):
                dve.wait_ge(x_in[r], slot_loaded(n, r))
                moments(V, dve, b, r % 2, n, tile(b.x[r]), s_bn, s_mv, s_go)

            def scales(n, r):
                scale_and_shift(V, dve, b, r % 2, n, s_sd, s_rs, s_nm)

            def skip(n, r):
                u = r % 2
                sk = tile(b.skip[r])
                dve.wait_ge(s_pO, n + 1)
                dve.wait_ge(skip_in[r], slot_loaded(n, r))
                for t in range(2):
                    zc = m.nvec[:, bass.ds(n * 2 + (2 * NT + t), 1)]
                    V.scalar_tensor_tensor(sk[:, t, 0:MUL], pO[u][t][:, D:D + MUL], zc, sk[:, t, 0:MUL],
                                           ALU.mult, ALU.add)
                    ins = V.scalar_tensor_tensor(
                        sk[:, t, MUL:D].rearrange("p (v c) -> p v c", c=3),
                        pO[u][t][:, D + MUL:2 * D].rearrange("p (c v) -> p v c", c=3), zc,
                        sk[:, t, MUL:D].rearrange("p (v c) -> p v c", c=3), ALU.mult, ALU.add)
                ins.then_inc(s_skip, 1)

            in_order(dve, (0, scales), (-1, statistics), (2, skip))

        @block.scalar
        def _(act):
            def sd(n, r):
                deviation(nc, act, m, b, r % 2, n, s_mv, s_sd)

            def hidden(n, r):
                u = r % 2
                x, h = tile(b.x[r]), tile(b.h[u])
                act.wait_ge(s_nm, n + 1)
                for t in range(2):
                    nc.scalar.activation(h[:, t, 0:MUL], x[:, t, 0:MUL], ACT.Relu,
                                         bias=b.nm[u][:, t:t + 1], scale=b.rs[u][:, t:t + 1])
                    ins = nc.scalar.activation(h[:, t, MUL:D].rearrange("p (c v) -> p v c", c=3),
                                               x[:, t, MUL:D].rearrange("p (v c) -> p v c", c=3), ACT.Relu,
                                               bias=b.nm[u][:, t:t + 1], scale=b.rs[u][:, t:t + 1])
                ins.then_inc(s_h, 1)

            def copy_hT(n, r):
                act.wait_ge(s_pT, n + 1)
                wait_slot(act, s_pO, n, 2)
                nc.scalar.copy(b.hT[r % 2], pT[r % 2][:]).then_inc(s_hT, 1)

            def rows(n, r):
                u = r % 2
                act.wait_ge(s_skip, n + 1)
                act.wait_ge(st_rows[u], slot_stored(n, u))
                for t in range(2):
                    zs = m.nvec[:, bass.ds(n * 2 + (NT + t), 1)]
                    ins = nc.scalar.activation(tile(b.rows[u])[:, t, :], pO[u][t][:, 0:D], ACT.Copy, scale=zs)
                ins.then_inc(s_rows, 1)

            in_order(act, (0, hidden), (-1, sd), (1, copy_hT), (2, rows))

        @block.tensor
        def _(pe):
            def transposes(n, r):
                u = r % 2
                h = tile(b.h[u])
                pe.wait_ge(s_h, n + 1)
                for c in range(2):
                    for t in range(2):
                        ins = nc.tensor.transpose(pT[u][:, c * PB + t * P:c * PB + (t + 1) * P],
                                                  h[:, t, c * P:(c + 1) * P], m.ident[:])
                ins.then_inc(s_pT, 1)

            def products(n, r):
                u = r % 2
                pe.wait_ge(s_hT, n + 1)
                wait_slot(pe, s_rows, n, 2)
                for t in range(2):
                    for c in range(2):
                        out = pO[u][t][:, :].rearrange("p (k f) -> p k f", k=2)[:, :, c * P:(c + 1) * P]
                        ins = nc.tensor.matmul(out, b.hT[u][:, c * PB + t * P:c * PB + (t + 1) * P],
                                               m.lin1[:, c, :], start=(c == 0), stop=True, skip_group_check=True)
                ins.then_inc(s_pO, 1)

            in_order(pe, (0, transposes), (1, products))


def conv_edge_stage(nc, m):
    V = nc.vector
    with ExitStack() as ctx:
        def sem(name):
            return m.sems.enter_context(nc.semaphore("ce_" + name))

        free, free_nodes = [0], [4 * NC]

        def part(width, parts=P, slots=2):
            a = [m.scratch[0:parts, free[0] + u * width:free[0] + (u + 1) * width] for u in range(slots)]
            free[0] += slots * width
            assert free[0] <= SCRATCH
            return a

        def nodes_part(width, slots):
            a = [m.nodes[:, free_nodes[0] + u * width:free_nodes[0] + (u + 1) * width] for u in range(slots)]
            free_nodes[0] += slots * width
            assert free_nodes[0] <= 5 * NC
            return a

        xg = part(G * D)
        hot = part(4 * NW)
        hidT = part(GE // 2)
        ea8 = part(GE // 2, 2 * NBAS, 1)[0]
        msg = nodes_part(2 * 12 * MUL, 4)
        sh = part(4 * G)
        idx = ctx.enter_context(nc.sbuf_tensor("ce_idx", [P, 2, G], I32))
        rel = ctx.enter_context(nc.sbuf_tensor("ce_rel", [P, 2, G], F32))
        ps_w = [ctx.enter_context(nc.psum_tensor(f"ce_w{j}", [P, 2, 4, MUL], F32)) for j in range(4)]
        ps_hid = ctx.enter_context(nc.psum_tensor("ce_hid", [P, GE // 2], F32))
        ps_sum = [ctx.enter_context(nc.psum_tensor(f"ce_sum{u}", [P, 4, NW], F32)) for u in range(2)]

        ea8_in = sem("ea8_in")
        got = [sem(f"gathered{u}") for u in range(2)]
        sp_done, sh_ready, idx_ready, pool_go, hid_ps, hid_ready, w_ready, rel_ready = [
            sem(n) for n in ("sp_done", "sh_ready", "idx_ready", "pool_go", "hid_ps", "hid_ready", "w_ready", "rel_ready")]
        hot_ready = sem("hot_ready")
        d_raw = sem("d_raw")
        d_scaled = sem("d_scaled")
        d_two = sem("d_two")
        d_ready = sem("d_ready")
        msg_ready = sem("msg_ready")
        scaled = sem("scaled")
        pair_summed = sem("pair_summed")
        added = sem("added")
        block = ctx.enter_context(nc.Block())

        def blocks_of(a):
            return a.rearrange("p (t b f) -> p t b f", t=2, b=12)

        def harmonic(g, k, c):
            return m.sh[:, bass.ds(g * (4 * G) + (4 * k + c), 1)]

        @block.sync
        def _(sp):
            def load(v):
                g = load_group(sp, m, v)
                sp.dma_start(ea8, m.io["ea8_t"][bass.ds(g * 2 * NBAS, 2 * NBAS), :]).then_inc(ea8_in, 16)

            quads = load_steps(sp, m)
            load(0)
            with sp.Fori(0, quads * 2) as half:
                for u in range(2):
                    sp.wait_ge(hid_ps, half * 2 + (u + 1))
                    load(half * 2 + (u + 1))
            sp.wait_ge(ea8_in, quads * 64 + 16).then_inc(sp_done, 1)

        @block.scalar
        def _(act):
            quads = load_steps(act, m)

            def stage_idx(v, u):
                g = load_group(act, m, v)
                nc.scalar.copy(idx[:, u, :], m.src[:, bass.ds(g * G, G)]).then_inc(idx_ready, 1)

            def stage_sh(v, u):
                g = load_group(act, m, v)
                nc.scalar.copy(sh[u], m.sh[:, bass.ds(g * (4 * G), 4 * G)]).then_inc(sh_ready, 1)

            def silu(v, u):
                act.wait_ge(hid_ps, v + 1)
                nc.scalar.activation(hidT[u], ps_hid[:, :], ACT.Silu, scale=NBAS ** -0.5).then_inc(hid_ready, 1)

            def scale(v, j, g):
                act.wait_ge(msg_ready, v * 4 + (j + 1))
                for t in range(2):
                    out = blocks_of(msg[j])[:, t, :, :].rearrange("p b f -> p (b f)")
                    nc.scalar.activation(out[:, 0:4 * MUL], out[:, 0:4 * MUL], ACT.Copy, scale=harmonic(g, 2 * j + t, 0))
                    for c in range(3):
                        ins = nc.scalar.activation(out[:, (5 + c) * MUL:(6 + c) * MUL], out[:, 8 * MUL:9 * MUL], ACT.Copy,
                                                   scale=harmonic(g, 2 * j + t, 1 + c))
                ins.then_inc(scaled, 1)

            for u in range(2):
                stage_idx(u, u)
            stage_sh(0, 0)
            silu(0, 0)
            with act.Fori(0, quads * 2) as half:
                for u in range(2):
                    v = half * 2 + u
                    g = load_group(act, m, v)
                    for j in range(4):
                        scale(v, j, g)
                        if j == 0:
                            silu(v + 1, 1 - u)
                        if j == 1:
                            stage_sh(v + 1, 1 - u)
                    stage_idx(v + 2, u)

        @block.gpsimd
        def _(pool):
            quads = load_steps(pool, m)
            with pool.Fori(0, quads * 2) as half:
                for u in range(2):
                    pool.wait_ge(idx_ready, half * 2 + (u + 1)).then_inc(pool_go, 1)
                    for k in range(G):
                        nc.gpsimd.indirect_dma_start(
                            xg[u][:, k * D:(k + 1) * D], None, m.h_rows,
                            bass.IndirectOffsetOnAxis(ap=idx[:, u, k:k + 1], axis=0)).then_inc(got[u], 16)

        @block.tensor
        def _(pe):
            quads = load_steps(pe, m)

            def hidden(v):
                pe.wait_ge(ea8_in, v * 16 + 16)
                nc.tensor.matmul(ps_hid[:, :], m.fc0[:, :], ea8, start=True, stop=True).then_inc(hid_ps, 1)

            def weights(v, u, j):
                if j == 0:
                    pe.wait_ge(hid_ready, v + 1)
                for t in range(2):
                    half, col = divmod((2 * j + t) * P, GE // 2)
                    rows = slice(half * RN, half * RN + RN)
                    ins = nc.tensor.matmul(ps_w[j][:, t, :, :].rearrange("p k f -> p (k f)"),
                                           hidT[u][rows, col:col + P], m.fc1[rows, :], start=True, stop=True)
                ins.then_inc(w_ready, 1)

            def sums(v, u, j):
                pe.wait_ge(scaled, v * 4 + (j + 1))
                pe.wait_ge(d_ready, v * 4 + (j + 1))
                if j % 2 == 0:
                    pe.wait_ge(hot_ready, v * 2 + (j // 2 + 1))
                if j == 0:
                    pe.wait_ge(added, v + 1)
                for t in range(2):
                    at = 2 * (j % 2) + t
                    for c in range(4):
                        blocks = blocks_of(msg[j])[:, t, 2 * c:2 * c + 2, :].rearrange("p b f -> p (b f)")
                        ins = nc.tensor.matmul(ps_sum[u][:, c, :], blocks, hot[j // 2][:, at * NW:(at + 1) * NW],
                                               start=(j == 0 and t == 0 and c == 0), stop=(j == 3 and t == 1),
                                               skip_group_check=True)
                ins.then_inc(pair_summed, 1)

            pe.sem_inc(pair_summed, 4)
            hidden(0)
            weights(0, 0, 0)
            weights(0, 0, 1)
            with pe.Fori(0, quads * 2) as half:
                for u in range(2):
                    v = half * 2 + u
                    for j in range(4):
                        if j < 2:
                            weights(v, u, j + 2)
                        else:
                            weights(v + 1, 1 - u, j - 2)
                        if j == 0:
                            hidden(v + 1)
                        sums(v, u, j)

        @block.vector
        def _(dve):
            quads = load_steps(dve, m)

            def products(v, u, j):
                tiles = xg[u].rearrange("p (k b f) -> p k b f", k=G, b=4)[:, 2 * j:2 * j + 2, :, :]
                out = blocks_of(msg[j])
                d = out[:, :, 9:12, :]
                h1 = tiles[:, :, 1:4, :]
                w = ps_w[j]
                n = v * 4 + j
                dve.wait_ge(pair_summed, n + 1)
                dve.wait_ge(w_ready, n + 1)
                if j == 0:
                    dve.wait_ge(got[u], (v - u) * 64 + 16 * G)
                    dve.wait_ge(sh_ready, v + 1)
                V.tensor_tensor(d, w[:, :, 3:4, :].broadcast_to([P, 2, 3, MUL]), h1, ALU.mult).then_inc(d_raw, 1)
                V.tensor_tensor(out[:, :, 0:9:8, :], w[:, :, 0:2, :], tiles[:, :, 0:1, :].broadcast_to([P, 2, 2, MUL]), ALU.mult)
                V.tensor_tensor(out[:, :, 1:4, :], w[:, :, 2:3, :].broadcast_to([P, 2, 3, MUL]), h1, ALU.mult).then_inc(msg_ready, 1)
                dve.wait_ge(d_raw, n + 1)
                s = sh[u].rearrange("p (k c o) -> p k c o", c=4, o=1)[:, 2 * j:2 * j + 2, 1:4, :]
                V.tensor_tensor(d, d, s.broadcast_to([P, 2, 3, MUL]), ALU.mult).then_inc(d_scaled, 1)

            def sum_d(v, j, between=None):
                out = blocks_of(msg[j])
                dve.wait_ge(d_scaled, v * 4 + (j + 1))
                V.tensor_tensor(out[:, :, 9, :], out[:, :, 9, :], out[:, :, 10, :], ALU.add).then_inc(d_two, 1)
                if between is not None:
                    between()
                dve.wait_ge(d_two, v * 4 + (j + 1))
                V.tensor_tensor(out[:, :, 4, :], out[:, :, 9, :], out[:, :, 11, :], ALU.add).then_inc(d_ready, 1)

            def relative(v, u):
                g = load_group(dve, m, v)
                V.tensor_scalar(rel[:, u, :], m.dst[:, bass.ds(g * G, G)], m.base_col[:, bass.ds(v, 1)], None,
                                ALU.subtract).then_inc(rel_ready, 1)

            def one_hots(v, u, half):
                if half == 0:
                    dve.wait_ge(rel_ready, v + 1)
                V.tensor_tensor(hot[half].rearrange("p (k n) -> p k n", k=4),
                                m.cols[:, :].rearrange("p (o n) -> p o n", o=1).broadcast_to([P, 4, NW]),
                                rel[:, u, 4 * half:4 * half + 4].rearrange("p (k o) -> p k o", o=1).broadcast_to([P, 4, NW]),
                                ALU.is_equal).then_inc(hot_ready, 1)

            def add_window(v, u):
                base = load_base(dve, m, v)
                dve.wait_ge(pair_summed, v * 4 + (4 + 4))
                dve.wait_ge(added, v + 2)
                cols = m.nodes[:, 0:4 * NC].rearrange("p (c n) -> p c n", c=4)[:, :, bass.ds(base, NW)]
                V.tensor_tensor(cols, cols, ps_sum[u][:, :, :], ALU.add).then_inc(added, 1)

            V.memset(ps_sum[1][:], 0.0).then_inc(added, 1)
            relative(0, 0)
            one_hots(0, 0, 0)
            with dve.Fori(0, quads * 2) as half:
                for u in range(2):
                    v = half * 2 + u
                    for j in range(4):
                        products(v, u, j)
                        if j == 1:
                            add_window(v - 1, 1 - u)
                            sum_d(v, j, lambda: one_hots(v, u, 1))
                        elif j == 2:
                            sum_d(v, j, lambda: relative(v + 1, 1 - u))
                        else:
                            sum_d(v, j)
                        if j == 3:
                            dve.wait_ge(pair_summed, v * 4 + (2 + 4))
                            one_hots(v + 1, 1 - u, 0)
            add_window(quads * 4 - 1, 1)


def conv_node_stage(nc, m):
    V = nc.vector
    with ExitStack() as ctx:
        def sem(name):
            return m.sems.enter_context(nc.semaphore("cn_" + name))

        def ps(name, cols):
            return ctx.enter_context(nc.psum_tensor("cn_" + name, [P, cols], F32))

        b = node_buffers(m, "l0out")
        pX = [ps(f"pX{u}", 512) for u in range(2)]
        pT = [ps(f"pT{u}", 512) for u in range(2)]
        pZ = [[ps(f"pZ{u}{t}", ZW) for t in range(2)] for u in range(2)]
        x_in = [sem(f"x_in{r}") for r in range(4)]
        y_in, s_parts, s_zero, pool_go, s_pX, s_x1, s_go, s_bn, s_mv, s_sd, s_rs, s_nm, s_h, s_pT, s_hT, s_pZ, s_rows = [
            sem(n) for n in ("y", "parts", "zeroed", "pool_go", "pX", "x1", "go", "bn", "mv", "sd", "rs", "nm", "h", "pT", "hT",
                             "pZ", "rows")]
        st_x1, st_hT, st_rows, st_parts = [[sem(f"st_{n}{u}") for u in range(2)] for n in ("x1", "hT", "rows", "parts")]
        cols = chunks(m.nodes[:, 0:4 * NC], 4)
        block = ctx.enter_context(nc.Block())

        @block.sync
        def _(sp):
            def load(n, r):
                wait_slot(sp, s_x1, n)
                sp.dma_start(tile(b.x[r]), rows_of(m.x_skip, n)).then_inc(x_in[r], 16)

            def store_x1(n, r):
                u = r % 2
                sp.wait_ge(s_x1, n + 1)
                sp.dma_start(rows_of(m.x1_rows, n), tile(b.skip[u])).then_inc(st_x1[u], 16)

            def store_hT(n, r):
                u = r % 2
                sp.wait_ge(s_hT, n + 1)
                sp.dma_start(m.hT[0][bass.ds(n, 1), :, :].rearrange("o p n -> (o p) n"), b.hT[u]).then_inc(st_hT[u], 16)

            def store_rows(n, r):
                store_table(sp, m, b, 0, n, r % 2, s_rows, s_parts, st_rows, st_parts)

            for st in (st_x1, st_hT, st_rows, st_parts):
                for u in range(2):
                    sp.sem_inc(st[u], 16)
            in_order(sp, (-2, load), (0, store_x1), (2, store_hT), (3, store_rows))
            for st in (st_x1, st_hT, st_rows, st_parts):
                for u in range(2):
                    sp.wait_ge(st[u], NPB * 8 + 16)

        @block.gpsimd
        def _(pool):
            def zero_columns(n, r):
                pool.wait_ge(y_in, n + 1).then_inc(pool_go, 1)
                nc.gpsimd.tensor_copy(cols[:, 0:3, bass.ds(n * PB, PB)], zeros_of(b))

            def parts(n, r):
                er_in_parts(nc, pool, b, n, r % 2, s_rows, s_parts, st_parts, pool_go)

            nc.gpsimd.memset(b.zero, 0.0).then_inc(s_zero, 1)
            pool.wait_ge(s_zero, 1)
            in_order(pool, (-1, zero_columns), (3, parts))

        @block.tensor
        def _(pe):
            def outputs(n, r):
                u = r % 2
                y = chunks(b.y[u], 4)
                pe.wait_ge(y_in, n + 1)
                for t in range(2):
                    out = pX[u][:, t * D:(t + 1) * D].rearrange("p (b f) -> p b f", b=4)
                    for c in range(4):
                        blocks = out[:, 2 * (c % 2):2 * (c % 2) + 2, :]
                        ins = nc.tensor.matmul(blocks, y[:, c, t * P:(t + 1) * P], m.lin2[:, c, :],
                                               start=(t == 0 and c == 0), stop=(c >= 2), skip_group_check=True)
                ins.then_inc(s_pX, 1)

            def transposes(n, r):
                u = r % 2
                h = tile(b.h[u])
                pe.wait_ge(s_h, n + 1)
                for c in range(2):
                    for t in range(2):
                        ins = nc.tensor.transpose(pT[u][:, c * PB + t * P:c * PB + (t + 1) * P],
                                                  h[:, t, c * P:(c + 1) * P], m.ident[:])
                ins.then_inc(s_pT, 1)

            def table(n, r):
                table_products(nc, pe, m, b, 0, n, r % 2, pZ, s_hT, s_rows, s_pZ)

            in_order(pe, (-1, outputs), (1, transposes), (2, table))

        @block.vector
        def _(dve):
            def fixed(n, r):
                wait_slot(dve, s_pX, n, 2)
                V.tensor_copy(chunks(b.y[r % 2], 4), cols[:, :, bass.ds(n * PB, PB)]).then_inc(y_in, 1)

            def state(n, r):
                u = r % 2
                x, x1 = tile(b.x[r]), tile(b.skip[u])
                dve.wait_ge(x_in[r], slot_loaded(n, r))
                dve.wait_ge(s_pX, n + 1)
                dve.wait_ge(st_x1[u], slot_stored(n, u))
                wait_slot(dve, s_h, n, 2)
                for t in range(2):
                    zc = m.nvec[:, bass.ds(n * 2 + t, 1)]
                    V.scalar_tensor_tensor(x1[:, t, 0:MUL], pX[u][:, t * D:t * D + MUL], zc, x[:, t, 0:MUL],
                                           ALU.mult, ALU.add)
                    ins = V.scalar_tensor_tensor(
                        x1[:, t, MUL:D].rearrange("p (v c) -> p v c", c=3),
                        pX[u][:, t * D + MUL:(t + 1) * D].rearrange("p (c v) -> p v c", c=3), zc,
                        x[:, t, MUL:D].rearrange("p (v c) -> p v c", c=3), ALU.mult, ALU.add)
                ins.then_inc(s_x1, 1)
                dve.wait_ge(s_x1, n + 1)
                moments(V, dve, b, u, n, x1, s_bn, s_mv, s_go)

            def scales(n, r):
                scale_and_shift(V, dve, b, r % 2, n, s_sd, s_rs, s_nm)

            in_order(dve, (1, scales), (-1, fixed), (0, state))

        @block.scalar
        def _(act):
            def sd(n, r):
                deviation(nc, act, m, b, r % 2, n, s_mv, s_sd)

            def hidden(n, r):
                u = r % 2
                act.wait_ge(s_nm, n + 1)
                for t in range(2):
                    ins = nc.scalar.activation(tile(b.h[u])[:, t, :], tile(b.skip[u])[:, t, :], ACT.Relu,
                                               bias=b.nm[u][:, t:t + 1], scale=b.rs[u][:, t:t + 1])
                ins.then_inc(s_h, 1)

            def copy_hT(n, r):
                u = r % 2
                act.wait_ge(s_pT, n + 1)
                act.wait_ge(st_hT[u], slot_stored(n, u))
                wait_slot(act, s_pZ, n, 2)
                nc.scalar.copy(b.hT[u], pT[u][:]).then_inc(s_hT, 1)

            def rows(n, r):
                table_rows(nc, act, b, n, r % 2, pZ, s_pZ, s_parts, st_rows, s_rows)

            in_order(act, (1, hidden), (0, sd), (2, copy_hT), (3, rows))


def table_products(nc, pe, m, b, layer, n, u, pZ, s_hT, s_rows, s_pZ):
    pe.wait_ge(s_hT, n + 1)
    wait_slot(pe, s_rows, n, 2)
    for t in range(2):
        for c in range(2):
            ins = nc.tensor.matmul(pZ[u][t][:, :], b.hT[u][:, c * PB + t * P:c * PB + (t + 1) * P], m.wz[layer][:, c, :],
                                   start=(c == 0), stop=(c == 1))
    ins.then_inc(s_pZ, 1)


def table_rows(nc, act, b, n, u, pZ, s_pZ, s_parts, st_rows, s_rows):
    act.wait_ge(s_pZ, n + 1)
    act.wait_ge(st_rows[u], slot_stored(n, u))
    if not isinstance(n, int) or n >= 2:
        act.wait_ge(s_parts, (n - 1) * 5)
    for t in range(2):
        ins = nc.scalar.copy(b.rows[u][:, t * ZW:(t + 1) * ZW], pZ[u][t][:, :])
    ins.then_inc(s_rows, 1)


def store_table(sp, m, b, layer, n, u, s_rows, s_parts, st_rows, st_parts):
    sp.wait_ge(s_rows, n + 1)
    sp.dma_start(rows_of(m.z_rows[layer], n), tile(b.rows[u], ZW)).then_inc(st_rows[u], 16)
    sp.wait_ge(s_parts, n * 5 + 5)
    sp.dma_start(rows_of(m.er_parts[layer], n), tile(b.parts[u], 12)).then_inc(st_parts[u], 16)


def zeros_of(b):
    return b.zero.rearrange("p (o n) -> p o n", o=1).broadcast_to([P, 3, PB])


def er_in_parts(nc, pool, b, n, u, s_rows, s_parts, st_parts, go):
    er = b.rows[u].rearrange("p (t w) -> p t w", t=2)[:, :, D + HEADS:ZW]
    parts = b.parts[u][:, 0:2 * 3 * HEADS].rearrange("p (t a h) -> p t a h", t=2, a=3)
    rest = b.rest[u].rearrange("p (t h) -> p t h", t=2)
    pool.wait_ge(s_rows, n + 1).then_inc(go, 1)
    pool.wait_ge(st_parts[u], slot_stored(n, u)).then_inc(go, 1)
    done = n * 5
    nc.gpsimd.tensor_copy(parts[:, :, 0, :], er).then_inc(s_parts, 1)
    for a in (1, 2):
        pool.wait_ge(s_parts, done + (2 * a - 1)).then_inc(go, 1)
        nc.gpsimd.tensor_tensor(rest, er if a == 1 else rest, parts[:, :, a - 1, :], ALU.subtract).then_inc(s_parts, 1)
        pool.wait_ge(s_parts, done + 2 * a).then_inc(go, 1)
        nc.gpsimd.tensor_copy(parts[:, :, a, :], rest).then_inc(s_parts, 1)


def gat_edge_stage(nc, m, layer):
    V = nc.vector
    BF = mybir.dt.bfloat16
    PARTS = 3
    ACT_TILES = 3
    SPLIT = 2
    with ExitStack() as ctx:
        def sem(name):
            return m.sems.enter_context(nc.semaphore(f"ge{layer}_" + name))

        def sb(name, shape, dt=F32):
            return ctx.enter_context(nc.sbuf_tensor(f"ge{layer}_" + name, shape, dt))

        def ps(name, shape):
            return ctx.enter_context(nc.psum_tensor(f"ge{layer}_" + name, shape, F32))

        free, free_scratch = [3 * NC], [0]

        def part(width, parts=P):
            a = m.nodes[0:parts, free[0]:free[0] + width]
            free[0] += width
            assert free[0] <= 5 * NC
            return a

        def scratch(width, parts=P):
            a = m.scratch[0:parts, free_scratch[0]:free_scratch[0] + width]
            free_scratch[0] += width
            assert free_scratch[0] <= SCRATCH
            return a

        zg = [part(G * ZW) for r in range(4)]
        sel = [part(G * NW) if r < 3 else scratch(G * NW) for r in range(4)]
        selT = part(GE // 2).bitcast(BF)
        zs = [scratch(G * D) for u in range(2)]
        seg = [scratch(GE + 2, HEADS) for u in range(2)]
        top = scratch(GE, HEADS)
        idx = part(4 * G).bitcast(I32).rearrange("p (r k) -> p r k", r=4)
        rel = part(2 * G).rearrange("p (u k) -> p u k", u=2)
        erw = sb("erw", [P, 2, PARTS * HEADS], BF)
        raw = part(G * HEADS)
        part_sum = part(G * HEADS)
        score = [part(G * HEADS) for u in range(2)]
        diff = [part(G * HEADS) for u in range(2)]
        ex = [part(G * HEADS) for u in range(2)]
        fd = [sb(f"fd{u}", [HEADS, 1]) for u in range(2)]
        fac = [sb(f"fac{u}", [HEADS, 1]) for u in range(2)]

        ps_eT = ps("eT", [HEADS, GE])
        ps_selT = ps("selT", [P, GE])
        ps_er = ps("er", [P, G * PARTS * HEADS])
        ps_max = ps("max", [P, G * HEADS])
        ps_sum = [ps(f"sum{u}", [P, 512]) for u in range(2)]
        FAC = 3 * NW

        er_in = [sem(f"er_in{u}") for u in range(2)]
        seg_in = [sem(f"seg_in{u}") for u in range(2)]
        got = [sem(f"gathered{r}") for r in range(4)]
        (sp_done, pe_go, er_summed, idx_ready, pool_go, rel_ready, sel_ready, selT_ps, selT_ready, er_ready, raw_ready,
         score_ready, eT_ready, fwd_ready, max_ready, carry_ready, maxT_ready, diff_ready, ex_ready, zs_ready,
         zs_act_ready, scaled, summed, added) = [
            sem(n) for n in ("sp_done", "pe_go", "er_summed", "idx_ready", "pool_go", "rel_ready", "sel_ready", "selT_ps",
                             "selT_ready", "er_ready", "raw_ready", "score_ready", "eT_ready", "fwd_ready", "max_ready",
                             "carry_ready", "maxT_ready", "diff_ready", "ex_ready", "zs_ready", "zs_act_ready", "scaled", "summed", "added")]
        block = ctx.enter_context(nc.Block())

        def per_head(a):
            return a.rearrange("p (k h) -> p k h", k=G)

        @block.sync
        def _(sp):
            quads = load_steps(sp, m)

            def load_er(v, u):
                base = load_base(sp, m, v)
                sp.dma_start(erw[:, u, :], m.er_parts[layer][bass.ds(base, NW), :]).then_inc(er_in[u], 16)

            def load_seg(v, u):
                g = load_group(sp, m, v)
                sp.dma_start(seg[u][:, 0:GE + 1],
                             m.same_seg[bass.ds(g * GE, GE + 1)].partition_broadcast(HEADS)).then_inc(seg_in[u], 16)

            for u in range(2):
                load_er(u, u)
                load_seg(u, u)
            with sp.Fori(0, quads) as quad:
                for r in range(4):
                    v = quad * 4 + r
                    sp.wait_ge(er_ready, v + 1)
                    load_er(v + 2, r % 2)
                    sp.wait_ge(carry_ready, v + 2)
                    load_seg(v + 2, r % 2)
            for u in range(2):
                sp.wait_ge(er_in[u], quads * 32 + 16)
                sp.wait_ge(seg_in[u], quads * 32 + 16).then_inc(sp_done, 1)

        @block.scalar
        def _(act):
            quads = load_steps(act, m)

            def stage_idx(v, r):
                g = load_group(act, m, v)
                nc.scalar.copy(idx[:, r, :], m.src[:, bass.ds(g * G, G)]).then_inc(idx_ready, 1)

            def copy_selT(v):
                act.wait_ge(selT_ps, v + 1)
                for k in range(2):
                    at = slice(k * GE // 2, (k + 1) * GE // 2)
                    nc.scalar.copy(selT[:, at], ps_selT[:, at]).then_inc(selT_ready, 1)

            for r in range(4):
                stage_idx(r, r)
            copy_selT(0)
            copy_selT(1)
            with act.Fori(0, quads) as quad:
                for r in range(4):
                    v = quad * 4 + r
                    u = r % 2
                    act.wait_ge(diff_ready, v + 1)
                    nc.scalar.activation(ex[u][:, :], diff[u][:, :], ACT.Exp).then_inc(ex_ready, 1)
                    nc.scalar.activation(fac[u][:, :], fd[u][:, :], ACT.Exp).then_inc(ex_ready, 1)
                    act.wait_ge(ex_ready, v * 2 + 2)
                    for k in range(G - ACT_TILES, G):
                        for h in range(HEADS):
                            ins = nc.scalar.activation(zs[u][:, k * D + h * HF:k * D + (h + 1) * HF],
                                                       zg[r][:, k * ZW + h * HF:k * ZW + (h + 1) * HF], ACT.Copy,
                                                       scale=ex[u][:, k * HEADS + h:k * HEADS + h + 1])
                    ins.then_inc(zs_act_ready, 1)
                    copy_selT(v + 2)
                    act.wait_ge(zs_ready, v * 2 + 2)
                    act.wait_ge(zs_act_ready, v + 1)
                    stage_idx(v + 4, r)

        @block.gpsimd
        def _(pool):
            quads = load_steps(pool, m)

            def gather(r):
                for k in range(G):
                    nc.gpsimd.indirect_dma_start(
                        zg[r][:, k * ZW:(k + 1) * ZW], None, m.z_rows[layer],
                        bass.IndirectOffsetOnAxis(ap=idx[:, r, k:k + 1], axis=0)).then_inc(got[r], 16)

            with pool.Fori(0, quads) as quad:
                for r in range(4):
                    pool.wait_ge(idx_ready, quad * 4 + (r + 1)).then_inc(pool_go, 1)
                    gather(r)
            pool.wait_ge(idx_ready, quads * 4 + 1).then_inc(pool_go, 1)
            gather(0)

        @block.tensor
        def _(pe):
            quads = load_steps(pe, m)

            def transpose_sel(v, r):
                pe.wait_ge(sel_ready, v + 1)
                for k in range(G):
                    ins = nc.tensor.transpose(ps_selT[:, k * P:(k + 1) * P], sel[r][:, k * P:(k + 1) * P], m.ident[:])
                ins.then_inc(selT_ps, 1)

            def spread_er(v, u, er_loads):
                pe.wait_ge(er_in[u], er_loads)
                W = PARTS * HEADS
                for k in range(G):
                    if k % (G // 2) == 0:
                        pe.wait_ge(selT_ready, v * 2 + (k // (G // 2) + 1))
                    ins = nc.tensor.matmul(ps_er[:, k * W:(k + 1) * W], selT[:, k * P:(k + 1) * P], erw[:, u, :],
                                           start=(k == 0), stop=(k == G - 1), skip_group_check=True)
                ins.then_inc(er_ready, 1)

            def transpose_scores(v, u):
                pe.wait_ge(score_ready, v + 1)
                for k in range(G):
                    ins = nc.tensor.transpose(ps_eT[:, k * P:(k + 1) * P], per_head(score[u][:, :])[:, k, :], m.ident[:])
                ins.then_inc(eT_ready, 1)

            transpose_sel(0, 0)
            spread_er(0, 0, 16)
            transpose_sel(1, 1)
            transpose_scores(0, 0)
            with pe.Fori(0, quads) as quad:
                for r in range(4):
                    v = quad * 4 + r
                    u = r % 2
                    pe.wait_ge(max_ready, v + 1).then_inc(pe_go, 1)
                    for k in range(G):
                        ins = nc.tensor.transpose(ps_max[:, k * HEADS:(k + 1) * HEADS], top[:, k * P:(k + 1) * P],
                                                  m.ident[0:HEADS, 0:HEADS])
                    ins.then_inc(maxT_ready, 1)
                    spread_er(v + 1, 1 - u, quad * 32 + ((r + 1) // 2 + 1) * 16)
                    transpose_sel(v + 2, (r + 2) % 4)
                    transpose_scores(v + 1, 1 - u)
                    pe.wait_ge(ex_ready, v * 2 + 2)
                    pe.wait_ge(added, v + 1)
                    for c in range(2):
                        nc.tensor.matmul(ps_sum[u][:, FAC + c:FAC + c + 1], m.headsel[:, c, :], fac[u][:, :],
                                         start=(c == 0), stop=True, skip_group_check=True)
                    for k in range(G):
                        if k == 0:
                            pe.wait_ge(zs_ready, v * 2 + 1)
                        if k == SPLIT:
                            pe.wait_ge(zs_ready, v * 2 + 2)
                        if k == G - ACT_TILES:
                            pe.wait_ge(zs_act_ready, v + 1)
                        s = sel[r][:, k * NW:(k + 1) * NW]
                        for c in range(2):
                            nc.tensor.matmul(ps_sum[u][:, c * NW:(c + 1) * NW],
                                             zs[u][:, k * D + c * P:k * D + (c + 1) * P], s,
                                             start=False, stop=(k == G - 1), skip_group_check=True)
                        ins = nc.tensor.matmul(ps_sum[u][0:HEADS, 2 * NW:3 * NW], per_head(ex[u][:, :])[:, k, :], s,
                                               start=False, stop=(k == G - 1), skip_group_check=True)
                    ins.then_inc(summed, 1)

        @block.vector
        def _(dve):
            quads = load_steps(dve, m)
            cols = m.nodes[:, 0:2 * NC].rearrange("p (c n) -> p c n", c=2)
            den = m.nodes[0:HEADS, 2 * NC:3 * NC]

            def relative(v, u):
                g = load_group(dve, m, v)
                V.tensor_scalar(rel[:, u, :], m.dst[:, bass.ds(g * G, G)], m.base_col[:, bass.ds(v, 1)], None,
                                ALU.subtract).then_inc(rel_ready, 1)

            def one_hots(v, r):
                dve.wait_ge(rel_ready, v + 1)
                V.tensor_tensor(sel[r].rearrange("p (k n) -> p k n", k=G),
                                m.cols[:, :].rearrange("p (o n) -> p o n", o=1).broadcast_to([P, G, NW]),
                                rel[:, r % 2, :].rearrange("p (k o) -> p k o", o=1).broadcast_to([P, G, NW]),
                                ALU.is_equal).then_inc(sel_ready, 1)

            def scores(v, r, gathered):
                dve.wait_ge(er_ready, v + 1)
                part_of = ps_er[:, :].rearrange("p (k a h) -> p k h a", k=G, a=PARTS)
                V.tensor_reduce(per_head(part_sum[:, :]), part_of, AX.X, ALU.add).then_inc(er_summed, 1)
                dve.wait_ge(er_summed, v + 1)
                dve.wait_ge(got[r], gathered)
                rows = zg[r].rearrange("p (k w) -> p k w", k=G)
                V.tensor_tensor(per_head(raw[:, :]), rows[:, :, D:D + HEADS], per_head(part_sum[:, :]), ALU.add
                                ).then_inc(raw_ready, 1)
                dve.wait_ge(raw_ready, v + 1)
                V.scalar_tensor_tensor(score[r % 2][:, :], raw[:, :], NEG_SLOPE, raw[:, :], ALU.mult, ALU.max
                                       ).then_inc(score_ready, 1)

            def scale_first(v, u, base):
                dve.wait_ge(summed, v + 2)
                dve.wait_ge(added, v + 2)
                first = cols[:, :, bass.ds(base, 1)]
                V.tensor_tensor(first, first, ps_sum[u][:, FAC:FAC + 2].rearrange("p (c o) -> p c o", o=1), ALU.mult)
                V.tensor_scalar(den[:, bass.ds(base, 1)], den[:, bass.ds(base, 1)], fac[u][:, :], None,
                                ALU.mult).then_inc(scaled, 1)

            def add_window(v, u, base):
                dve.wait_ge(scaled, v + 2)
                window = cols[:, :, bass.ds(base, NW)]
                V.tensor_tensor(window, window, ps_sum[u][:, 0:2 * NW].rearrange("p (c n) -> p c n", c=2), ALU.add)
                dwin = den[:, bass.ds(base, NW)]
                V.tensor_tensor(dwin, dwin, ps_sum[u][0:HEADS, 2 * NW:3 * NW], ALU.add).then_inc(added, 1)

            V.memset(fac[1][:, :], 1.0)
            V.memset(ps_sum[1][:], 0.0).then_inc(added, 1)
            V.memset(m.carry[:], LOW).then_inc(carry_ready, 1)
            dve.sem_inc(summed, 1)
            for u in range(2):
                relative(u, u)
                one_hots(u, u)
            scores(0, 0, 16 * G)
            with dve.Fori(0, quads) as quad:
                for r in range(4):
                    v = quad * 4 + r
                    u = r % 2
                    dve.wait_ge(eT_ready, v + 1)
                    dve.wait_ge(seg_in[u], quad * 32 + (r // 2 + 1) * 16)
                    dve.wait_ge(carry_ready, v + 1)
                    V.tensor_tensor_scan(top, seg[u][:, 0:GE], ps_eT[:, :], m.carry[:, u:u + 1], ALU.add, ALU.max
                                         ).then_inc(fwd_ready, 1)
                    relative(v + 2, u)
                    dve.wait_ge(fwd_ready, v + 1)
                    V.tensor_tensor_scan(top[:, ::-1], seg[u][:, GE:0:-1], top[:, ::-1], LOW, ALU.add, ALU.max
                                         ).then_inc(max_ready, 1)
                    dve.wait_ge(max_ready, v + 1)
                    V.scalar_tensor_tensor(fd[u][:, :], m.carry[:, u:u + 1], seg[u][:, 0:1], top[:, 0:1],
                                           ALU.add, ALU.subtract)
                    V.tensor_copy(m.carry[:, 1 - u:2 - u], top[:, GE - 1:GE]).then_inc(carry_ready, 1)
                    one_hots(v + 2, (r + 2) % 4)
                    base = load_base(dve, m, v - 1)
                    dve.wait_ge(maxT_ready, v + 1)
                    V.tensor_tensor(diff[u][:, :], score[u][:, :], ps_max[:, :], ALU.subtract).then_inc(diff_ready, 1)
                    scores(v + 1, (r + 1) % 4, quad * 128 + (128 if r < 3 else 256))
                    scale_first(v - 1, 1 - u, base)
                    dve.wait_ge(ex_ready, v * 2 + 1)
                    out = zs[u].rearrange("p (k h f) -> p k h f", k=G, h=HEADS)
                    z = zg[r].rearrange("p (k w) -> p k w", k=G)[:, :, 0:D].rearrange("p k (h f) -> p k h f", h=HEADS)
                    weight = ex[u][:, :].rearrange("p (k h o) -> p k h o", k=G, o=1).broadcast_to([P, G, HEADS, HF])
                    for k in (slice(0, SPLIT), slice(SPLIT, G - ACT_TILES)):
                        V.tensor_tensor(out[:, k], z[:, k], weight[:, k], ALU.mult).then_inc(zs_ready, 1)
                    add_window(v - 1, 1 - u, base)
            last = quads * 4 - 1
            base = load_base(dve, m, last)
            scale_first(last, 1, base)
            add_window(last, 1, base)


def gat_node_stage(nc, m, layer):
    V = nc.vector
    with ExitStack() as ctx:
        def sem(name):
            return m.sems.enter_context(nc.semaphore(f"gn{layer}_" + name))

        def ps(name, cols):
            return ctx.enter_context(nc.psum_tensor(f"gn{layer}_" + name, [P, cols], F32))

        b = node_buffers(m, "gat")
        pR = [ps(f"pR{u}", 512) for u in range(2)]
        pT = [ps(f"pT{u}", 512) for u in range(2)]
        pZ = [[ps(f"pZ{u}{t}", ZW) for t in range(2)] for u in range(2)]
        x_in, den_in, skip_in = [[sem(f"{n}_in{r}") for r in range(4)] for n in ("x", "den", "skip")]
        den_moved, s_max, s_den, s_pR, s_t, s_v, s_neg, s_ex, s_em, s_hT, s_pT, s_pZ, s_rows, s_parts, s_zero, pool_go = [
            sem(n) for n in ("den_moved", "max", "den", "pR", "t", "v", "neg", "ex", "em", "hT", "pT", "pZ", "rows", "parts", "zeroed", "pool_go")]
        st_hT, st_rows, st_parts = [[sem(f"st_{n}{u}") for u in range(2)] for n in ("hT", "rows", "parts")]
        stores = (st_hT, st_rows, st_parts) if layer == 0 else (st_rows,)
        block = ctx.enter_context(nc.Block())

        @block.sync
        def _(sp):
            def load_den(n, r):
                wait_slot(sp, s_pR, n)
                sp.dma_start(b.den[r], m.den_rows[:, bass.ds(n * PB, PB)]).then_inc(den_in[r], 16)

            def load_x(n, r):
                wait_slot(sp, s_hT, n)
                sp.dma_start(b.x[r], m.hT[layer][bass.ds(n, 1), :, :].rearrange("o p n -> (o p) n")).then_inc(x_in[r], 16)

            def load_skip(n, r):
                if layer == 1:
                    wait_slot(sp, s_rows, n)
                    sp.dma_start(tile(b.skip[r]), rows_of(m.x1_rows, n)).then_inc(skip_in[r], 16)

            def store_hT(n, r):
                u = r % 2
                if layer == 0:
                    sp.wait_ge(s_hT, n + 1)
                    sp.dma_start(m.hT[1][bass.ds(n, 1), :, :].rearrange("o p n -> (o p) n"), b.hT[u]).then_inc(st_hT[u], 16)

            def store_rows(n, r):
                u = r % 2
                if layer == 0:
                    store_table(sp, m, b, 1, n, u, s_rows, s_parts, st_rows, st_parts)
                else:
                    sp.wait_ge(s_rows, n + 1)
                    sp.dma_start(rows_of(m.io["out"], n), tile(b.rows[u])).then_inc(st_rows[u], 16)

            for st in stores:
                for u in range(2):
                    sp.sem_inc(st[u], 16)
            by_step = m.den_rows.rearrange("h (s n) -> (h s) n", n=PB)
            sp.dma_start(m.den_rows, m.nodes[0:HEADS, 2 * NC:3 * NC]).then_inc(den_moved, 16)
            sp.wait_ge(den_moved, 16)
            sp.dma_start(b.all_den, by_step).then_inc(den_moved, 16)
            sp.wait_ge(s_den, 1)
            sp.dma_start(by_step, b.all_den).then_inc(den_moved, 16)
            sp.wait_ge(den_moved, 48)
            in_order(sp, (-3, load_den), (-2, load_x), (0, load_skip), (1, store_hT), (2, store_rows))
            for st in stores:
                for u in range(2):
                    sp.wait_ge(st[u], NPB * 8 + 16)

        @block.gpsimd
        def _(pool):
            def parts(n, r):
                er_in_parts(nc, pool, b, n, r % 2, s_rows, s_parts, st_parts, pool_go)

            if layer == 0:
                nc.gpsimd.memset(b.zero, 0.0).then_inc(s_zero, 1)
                in_order(pool, (2, parts))

        @block.tensor
        def _(pe):
            def spread(n, r):
                u = r % 2
                pe.wait_ge(den_in[r], slot_loaded(n, r))
                wait_slot(pe, s_t, n, 2)
                for c in range(2):
                    ins = nc.tensor.matmul(pR[u][:, c * PB:(c + 1) * PB], m.headsel[:, c, :], b.den[r],
                                           start=(c == 0), stop=True, skip_group_check=True)
                ins.then_inc(s_pR, 1)

            def table(n, r):
                table_products(nc, pe, m, b, 1, n, r % 2, pZ, s_hT, s_rows, s_pZ)

            def to_rows(n, r):
                u = r % 2
                pe.wait_ge(s_hT, n + 1)
                wait_slot(pe, s_rows, n, 2)
                for t in range(2):
                    for c in range(2):
                        ins = nc.tensor.transpose(pT[u][:, t * D + c * P:t * D + (c + 1) * P],
                                                  b.hT[u][:, c * PB + t * P:c * PB + (t + 1) * P], m.ident[:])
                ins.then_inc(s_pT, 1)

            in_order(pe, (-1, spread), (1, to_rows if layer else table))

        @block.vector
        def _(dve):
            cols = chunks(m.nodes[:, 0:2 * NC])

            every = chunks(m.nodes[:, 0:3 * NC], 3)
            if layer == 0:
                dve.wait_ge(s_zero, 1)
            dve.wait_ge(den_moved, 32)
            V.tensor_scalar(b.all_den, b.all_den, 1e-30, None, ALU.max).then_inc(s_max, 1)
            dve.wait_ge(s_max, 1)
            V.reciprocal(b.all_den, b.all_den).then_inc(s_den, 1)

            def state(n, r):
                u = r % 2
                x, t = chunks(b.x[r]), chunks(b.h[u])
                dve.wait_ge(x_in[r], slot_loaded(n, r))
                dve.wait_ge(s_pR, n + 1)
                wait_slot(dve, s_hT, n, 2)
                V.tensor_tensor(t, cols[:, :, bass.ds(n * PB, PB)], chunks(pR[u][:, :]), ALU.mult).then_inc(s_t, 1)
                dve.wait_ge(s_t, n + 1)
                for c in range(2):
                    ins = V.scalar_tensor_tensor(x[:, c, :], x[:, c, :], m.bias[layer][:, c:c + 1], t[:, c, :],
                                                 ALU.add, ALU.add)
                ins.then_inc(s_v, 1)
                if layer == 0:
                    V.tensor_copy(every[:, :, bass.ds(n * PB, PB)], zeros_of(b))

            def elu(n, r):
                u = r % 2
                dve.wait_ge(s_em, n + 1)
                if layer == 0:
                    dve.wait_ge(st_hT[u], slot_stored(n, u))
                    wait_slot(dve, s_pZ, n, 2)
                else:
                    wait_slot(dve, s_pT, n, 2)
                V.scalar_tensor_tensor(b.hT[u], b.x[r], 0.0, b.h[u], ALU.max, ALU.add).then_inc(s_hT, 1)

            def output(n, r):
                u = r % 2
                dve.wait_ge(s_pT, n + 1)
                dve.wait_ge(skip_in[r], slot_loaded(n, r))
                dve.wait_ge(st_rows[u], slot_stored(n, u))
                V.tensor_tensor(b.rows[u][:, 0:2 * D], pT[u][:, :], b.skip[r], ALU.add).then_inc(s_rows, 1)

            if layer == 0:
                in_order(dve, (0, state), (1, elu))
            else:
                in_order(dve, (0, state), (1, elu), (2, output))

        @block.scalar
        def _(act):
            def exponential(n, r):
                h = b.h[r % 2]
                act.wait_ge(s_v, n + 1)
                nc.scalar.activation(h, b.x[r], ACT.Relu, scale=-1.0).then_inc(s_neg, 1)
                act.wait_ge(s_neg, n + 1)
                nc.scalar.activation(h, h, ACT.Exp, scale=-1.0).then_inc(s_ex, 1)
                act.wait_ge(s_ex, n + 1)
                nc.scalar.activation(h, h, ACT.Copy, bias=-1.0).then_inc(s_em, 1)

            def rows(n, r):
                table_rows(nc, act, b, n, r % 2, pZ, s_pZ, s_parts, st_rows, s_rows)

            if layer == 0:
                in_order(act, (0, exponential), (2, rows))
            else:
                in_order(act, (0, exponential))


def build(nc, io):
    with ExitStack() as ctx:
        m = allocate(nc, ctx, io)
        setup_stage(nc, m)
        input_stage(nc, m)
        conv_edge_stage(nc, m)
        conv_node_stage(nc, m)
        for layer in range(2):
            with nc.cleanup_on_exit():
                m.sems = ExitStack()
                gat_edge_stage(nc, m, layer)
                gat_node_stage(nc, m, layer)


def kernel(**inputs):
    import numpy as np
    import concourse.bacc as bacc
    from concourse.bass_utils import run_bass_kernel_spmd as run

    a = {k: np.ascontiguousarray(v) for k, v in inputs.items()}

    def padded(rows, n, fill=0):
        out = np.full((n,) + rows.shape[1:], fill, rows.dtype)
        out[:rows.shape[0]] = rows
        return out

    dst = padded(a["dst"], EP, N)
    line = np.full((NG + 1) * GE + 1, N, dst.dtype)
    line[0] = -1
    line[1:1 + EP] = dst
    arrays = {
        "x": padded(a["x"], NC),
        "nvec_t": np.ascontiguousarray(padded(a["node_vec1"], NC).reshape(NT, P).T),
        "src_t": np.ascontiguousarray(padded(a["src"], EP).reshape(NTILES, P).T),
        "dst_t": np.ascontiguousarray(dst.reshape(NTILES, P).T),
        "dst_line": line,
        "dst_ends": np.concatenate([dst[0::GE], dst[GE - 1::GE]]).reshape(1, 2 * NG),
        "sh_t": np.ascontiguousarray(padded(a["edge_attr_4"], EP).reshape(NTILES, P, 4).transpose(1, 0, 2)).reshape(P, 4 * NTILES),
        "ea8_t": np.ascontiguousarray(padded(a["edge_attr_8"], EP).reshape(NG, 2, GE // 2, NBAS).transpose(0, 1, 3, 2)).reshape(NG * 2 * NBAS, GE // 2),
    }
    for name in ("W_sc0", "W_sc1", "W_lin1_0", "W_lin1_1", "fc_w0", "fc_w1", "W_lin2_0", "W_lin2_1"):
        arrays[name] = a["L0_gnn_" + name]
    for l in range(2):
        arrays[f"W{l}"] = a[f"L1_gnn_W{l}"]
        arrays[f"al{l}"] = a[f"L1_gnn_al{l}"].reshape(D)
        arrays[f"ar{l}"] = a[f"L1_gnn_ar{l}"].reshape(D)
        arrays[f"b{l}_t"] = np.ascontiguousarray(a[f"L1_gnn_b{l}"].reshape(2, P).T)

    nc = bacc.Bacc("TRN2", target_bir_lowering=False, num_devices=1)
    io = {k: nc.dram_tensor(k, v.shape, mybir.dt.from_np(v.dtype), kind="ExternalInput").ap() for k, v in arrays.items()}
    io["out"] = nc.dram_tensor("out", (NC, D), F32, kind="ExternalOutput").ap()
    build(nc, io)
    r = run(nc, [arrays], core_ids=[0])
    return r.results[0]["out"][:N]
```
